# Optimizing a Trainium2 kernel written in Bass

```python
import numpy as np
import jax
import jax.numpy as jnp

def _softmax(x, axis=-1):
    return jax.nn.softmax(x, axis=axis)

def _gelu(x):
    return jax.nn.gelu(x, approximate=True)

def _silu(x):
    return jax.nn.silu(x)

def _sigmoid(x):
    return jax.nn.sigmoid(x)

def _layernorm(x, axis=-1, eps=1e-05):
    m = jnp.mean(x, axis=axis, keepdims=True)
    v = jnp.var(x, axis=axis, keepdims=True)
    return (x - m) / jnp.sqrt(v + eps)

def _scatter_add(tgt, idx, src, axis=0):
    return tgt.at[idx].add(src)

def _segment_sum(src, seg, n):
    return jax.ops.segment_sum(src, seg, n)
kernel_name = 'mk_seq_preln_d2_jaxref_r4_488afe'

def setup_inputs(seed: int=0):
    np.random.seed(seed)
    _w = jnp.asarray

    def _L0_attn_setup():
        import jax, jax.numpy as jnp
        import numpy as np
        import math
        B, T, DIM, NH = (2, 512, 256, 16)
        HD = DIM // NH

        def rope_embed(seq_len, hd):
            inv_freq = 1.0 / 10000.0 ** (jnp.arange(0, hd, 2, dtype=jnp.float32) / hd)
            t = jnp.arange(seq_len, dtype=jnp.float32)
            freqs = t[:, None] * inv_freq[None, :]
            return jnp.concatenate([jnp.sin(freqs), jnp.cos(freqs)], axis=-1)

        def apply_rotary(x, emb):
            x1, x2 = (x[..., ::2], x[..., 1::2])
            sin, cos = (emb[..., ::2], emb[..., 1::2])
            return jnp.concatenate([x1 * cos - x2 * sin, x1 * sin + x2 * cos], axis=-1)
        key = jax.random.key(seed)
        ks = jax.random.split(key, 5)
        s = 0.02
        return {'x': jax.random.normal(ks[0], (B, T, DIM), dtype=jnp.float32), 'qkv_w': jax.random.normal(ks[1], (3 * DIM, DIM), dtype=jnp.float32) * s, 'qkv_b': jax.random.normal(ks[2], (3 * DIM,), dtype=jnp.float32) * s, 'out_w': jax.random.normal(ks[3], (DIM, DIM), dtype=jnp.float32) * s, 'out_b': jax.random.normal(ks[4], (DIM,), dtype=jnp.float32) * s}
    _L0_attn_in = _L0_attn_setup()

    def _L0_ffn_setup():
        import jax, jax.numpy as jnp
        from jax import lax
        import numpy as np
        D_MODEL = 256
        HIDDEN = 128
        N_EXPERTS = 32
        TOP_K = 2
        B, S = (1, 1024)

        def _moe_group(x2, router_w, wg, wu, wd, top_k):
            T = x2.shape[0]
            n_experts = router_w.shape[1]
            logits = x2 @ router_w
            scores = jax.nn.softmax(logits, axis=-1)
            expert_weights, expert_indices = lax.top_k(scores, top_k)
            flat_e = expert_indices.reshape(-1)
            flat_w = expert_weights.reshape(-1)
            flat_t = jnp.repeat(jnp.arange(T), top_k)
            order = jnp.argsort(flat_e)
            tok = flat_t[order]
            xs = x2[tok]
            group_sizes = jnp.bincount(flat_e, length=n_experts).astype(jnp.int32)
            gate = lax.ragged_dot(xs, wg, group_sizes)
            up = lax.ragged_dot(xs, wu, group_sizes)
            ys = lax.ragged_dot(jax.nn.silu(gate) * up, wd, group_sizes)
            ys = ys * flat_w[order][:, None]
            return jnp.zeros_like(x2).at[tok].add(ys)
        key = jax.random.key(seed)
        ks = jax.random.split(key, 9)
        w = lambda k, shape: jax.random.normal(k, shape, dtype=jnp.float32) * 0.02
        return {'x': jax.random.normal(ks[0], (B, S, D_MODEL), dtype=jnp.float32), 'router_w0': w(ks[1], (D_MODEL, N_EXPERTS)), 'wg0': w(ks[2], (N_EXPERTS, D_MODEL, HIDDEN)), 'wu0': w(ks[3], (N_EXPERTS, D_MODEL, HIDDEN)), 'wd0': w(ks[4], (N_EXPERTS, HIDDEN, D_MODEL)), 'router_w1': w(ks[5], (D_MODEL, N_EXPERTS)), 'wg1': w(ks[6], (N_EXPERTS, D_MODEL, HIDDEN)), 'wu1': w(ks[7], (N_EXPERTS, D_MODEL, HIDDEN)), 'wd1': w(ks[8], (N_EXPERTS, HIDDEN, D_MODEL))}
    _L0_ffn_in = _L0_ffn_setup()

    def _L1_attn_setup():
        import jax, jax.numpy as jnp
        import numpy as np
        D_MODEL = 256
        N_HEADS = 16
        HEAD_DIM = D_MODEL // N_HEADS
        EPS = 1e-05

        def _layernorm(x, g, b):
            mu = jnp.mean(x, axis=-1, keepdims=True)
            var = jnp.mean(jnp.square(x - mu), axis=-1, keepdims=True)
            return (x - mu) * jax.lax.rsqrt(var + EPS) * g + b

        def _gdn(x, Wq, Wk, Wv, Wb, Wg, Wo, bo):
            B, S, D = x.shape
            H, Dh = (N_HEADS, HEAD_DIM)
            q = (x @ Wq).reshape(B, S, H, Dh) * Dh ** (-0.5)
            k = (x @ Wk).reshape(B, S, H, Dh)
            k = k / (jnp.linalg.norm(k, axis=-1, keepdims=True) + 1e-06)
            v = (x @ Wv).reshape(B, S, H, Dh)
            beta = jax.nn.sigmoid(x @ Wb)
            g = jax.nn.sigmoid(x @ Wg)
            qt = jnp.moveaxis(q, 1, 0)
            kt = jnp.moveaxis(k, 1, 0)
            vt = jnp.moveaxis(v, 1, 0)
            bt = jnp.moveaxis(beta, 1, 0)
            gt = jnp.moveaxis(g, 1, 0)
            S0 = jnp.zeros((B, H, Dh, Dh), x.dtype)

            def step(Sst, inp):
                q_t, k_t, v_t, b_t, g_t = inp
                Sst = Sst * g_t[..., None, None]
                kS = jnp.einsum('bhk,bhkv->bhv', k_t, Sst)
                Sst = Sst + b_t[..., None, None] * jnp.einsum('bhk,bhv->bhkv', k_t, v_t - kS)
                o_t = jnp.einsum('bhk,bhkv->bhv', q_t, Sst)
                return (Sst, o_t)
            _, out = jax.lax.scan(step, S0, (qt, kt, vt, bt, gt))
            out = jnp.moveaxis(out, 0, 1).reshape(B, S, D)
            return out @ Wo + bo
        key = jax.random.key(seed)
        ks = jax.random.split(key, 16)
        B, S, D = (4, 512, D_MODEL)
        s = 0.02
        inp = {'x': jax.random.normal(ks[0], (B, S, D), dtype=jnp.float32), 'Wq': jax.random.normal(ks[1], (D, D), jnp.float32) * s, 'Wk': jax.random.normal(ks[2], (D, D), jnp.float32) * s, 'Wv': jax.random.normal(ks[3], (D, D), jnp.float32) * s, 'Wb': jax.random.normal(ks[4], (D, N_HEADS), jnp.float32) * s, 'Wg': jax.random.normal(ks[5], (D, N_HEADS), jnp.float32) * s, 'Wo': jax.random.normal(ks[6], (D, D), jnp.float32) * s, 'bo': jnp.zeros((D,), jnp.float32), 'ln1_g': jnp.ones((D,), jnp.float32), 'ln1_b': jnp.zeros((D,), jnp.float32), 'ln2_g': jnp.ones((D,), jnp.float32), 'ln2_b': jnp.zeros((D,), jnp.float32), 'w1': jax.random.normal(ks[7], (D, 4 * D), jnp.float32) * s, 'b1': jnp.zeros((4 * D,), jnp.float32), 'w2': jax.random.normal(ks[8], (4 * D, D), jnp.float32) * s, 'b2': jnp.zeros((D,), jnp.float32)}
        return inp
    _L1_attn_in = _L1_attn_setup()

    def _L1_ffn_setup():
        import jax, jax.numpy as jnp
        import numpy as np
        B, N, D = (4, 1024, 256)
        E, S, F = (16, 64, 512)
        DO = 256
        EPS = 1e-05

        def _layernorm(x, g, b):
            mu = jnp.mean(x, axis=-1, keepdims=True)
            var = jnp.mean(jnp.square(x - mu), axis=-1, keepdims=True)
            return (x - mu) * jax.lax.rsqrt(var + EPS) * g + b
        key = jax.random.key(seed)
        ks = jax.random.split(key, 8)
        d = {'x': jax.random.normal(ks[0], (B, N, D), dtype=jnp.float32), 'norm_g': jnp.ones((D,), jnp.float32), 'norm_b': jnp.zeros((D,), jnp.float32), 'slot_g': jnp.ones((D,), jnp.float32), 'slot_b': jnp.zeros((D,), jnp.float32), 'scale': jnp.ones((1,), jnp.float32), 'slot_embeds': jax.random.normal(ks[1], (E, S, D), jnp.float32) / np.sqrt(D), 'Wg': jax.random.normal(ks[2], (E, D, F), jnp.float32) * np.sqrt(2.0 / (D + F)), 'bg': jnp.zeros((E, F), jnp.float32), 'Wu': jax.random.normal(ks[3], (E, D, F), jnp.float32) * np.sqrt(2.0 / (D + F)), 'bu': jnp.zeros((E, F), jnp.float32), 'Wd': jax.random.normal(ks[4], (E, F, DO), jnp.float32) * np.sqrt(2.0 / (F + DO)), 'bd': jnp.zeros((E, DO), jnp.float32)}
        return d
    _L1_ffn_in = _L1_ffn_setup()
    _d = {'L0_attn_x': _L0_attn_in['x'], 'L0_attn_qkv_w': _L0_attn_in['qkv_w'], 'L0_attn_qkv_b': _L0_attn_in['qkv_b'], 'L0_attn_out_w': _L0_attn_in['out_w'], 'L0_attn_out_b': _L0_attn_in['out_b'], 'L0_ffn_router_w0': _L0_ffn_in['router_w0'], 'L0_ffn_wg0': _L0_ffn_in['wg0'], 'L0_ffn_wu0': _L0_ffn_in['wu0'], 'L0_ffn_wd0': _L0_ffn_in['wd0'], 'L0_ffn_router_w1': _L0_ffn_in['router_w1'], 'L0_ffn_wg1': _L0_ffn_in['wg1'], 'L0_ffn_wu1': _L0_ffn_in['wu1'], 'L0_ffn_wd1': _L0_ffn_in['wd1'], 'L1_attn_Wq': _L1_attn_in['Wq'], 'L1_attn_Wk': _L1_attn_in['Wk'], 'L1_attn_Wv': _L1_attn_in['Wv'], 'L1_attn_Wb': _L1_attn_in['Wb'], 'L1_attn_Wg': _L1_attn_in['Wg'], 'L1_attn_Wo': _L1_attn_in['Wo'], 'L1_attn_bo': _L1_attn_in['bo'], 'L1_attn_ln1_g': _L1_attn_in['ln1_g'], 'L1_attn_ln1_b': _L1_attn_in['ln1_b'], 'L1_attn_ln2_g': _L1_attn_in['ln2_g'], 'L1_attn_ln2_b': _L1_attn_in['ln2_b'], 'L1_attn_w1': _L1_attn_in['w1'], 'L1_attn_b1': _L1_attn_in['b1'], 'L1_attn_w2': _L1_attn_in['w2'], 'L1_attn_b2': _L1_attn_in['b2'], 'L1_ffn_norm_g': _L1_ffn_in['norm_g'], 'L1_ffn_norm_b': _L1_ffn_in['norm_b'], 'L1_ffn_slot_g': _L1_ffn_in['slot_g'], 'L1_ffn_slot_b': _L1_ffn_in['slot_b'], 'L1_ffn_scale': _L1_ffn_in['scale'], 'L1_ffn_slot_embeds': _L1_ffn_in['slot_embeds'], 'L1_ffn_Wg': _L1_ffn_in['Wg'], 'L1_ffn_bg': _L1_ffn_in['bg'], 'L1_ffn_Wu': _L1_ffn_in['Wu'], 'L1_ffn_bu': _L1_ffn_in['bu'], 'L1_ffn_Wd': _L1_ffn_in['Wd'], 'L1_ffn_bd': _L1_ffn_in['bd']}
    _x0 = _d['L0_attn_x']
    _d['L0_attn_x'] = jax.random.normal(jax.random.fold_in(jax.random.key(seed), 1), (2, 2048, 256), dtype=_x0.dtype)
    del _x0
    return _d

def reference(L0_attn_x, L0_attn_qkv_w, L0_attn_qkv_b, L0_attn_out_w, L0_attn_out_b, L0_ffn_router_w0, L0_ffn_wg0, L0_ffn_wu0, L0_ffn_wd0, L0_ffn_router_w1, L0_ffn_wg1, L0_ffn_wu1, L0_ffn_wd1, L1_attn_Wq, L1_attn_Wk, L1_attn_Wv, L1_attn_Wb, L1_attn_Wg, L1_attn_Wo, L1_attn_bo, L1_attn_ln1_g, L1_attn_ln1_b, L1_attn_ln2_g, L1_attn_ln2_b, L1_attn_w1, L1_attn_b1, L1_attn_w2, L1_attn_b2, L1_ffn_norm_g, L1_ffn_norm_b, L1_ffn_slot_g, L1_ffn_slot_b, L1_ffn_scale, L1_ffn_slot_embeds, L1_ffn_Wg, L1_ffn_bg, L1_ffn_Wu, L1_ffn_bu, L1_ffn_Wd, L1_ffn_bd):

    def _L0_attn_ref(x, qkv_w, qkv_b, out_w, out_b):
        import jax, jax.numpy as jnp
        import numpy as np
        import math
        B, T, DIM, NH = (2, 512, 256, 16)
        HD = DIM // NH

        def rope_embed(seq_len, hd):
            inv_freq = 1.0 / 10000.0 ** (jnp.arange(0, hd, 2, dtype=jnp.float32) / hd)
            t = jnp.arange(seq_len, dtype=jnp.float32)
            freqs = t[:, None] * inv_freq[None, :]
            return jnp.concatenate([jnp.sin(freqs), jnp.cos(freqs)], axis=-1)

        def apply_rotary(x, emb):
            x1, x2 = (x[..., ::2], x[..., 1::2])
            sin, cos = (emb[..., ::2], emb[..., 1::2])
            return jnp.concatenate([x1 * cos - x2 * sin, x1 * sin + x2 * cos], axis=-1)
        b, t, c = x.shape
        nh, hd = (NH, c // NH)
        qkv = x @ qkv_w.T + qkv_b
        q, k, v = jnp.split(qkv, 3, axis=-1)
        q = q.reshape(b, t, nh, hd).transpose(0, 2, 1, 3)
        k = k.reshape(b, t, nh, hd).transpose(0, 2, 1, 3)
        v = v.reshape(b, t, nh, hd).transpose(0, 2, 1, 3)
        emb = rope_embed(t, hd)
        q = apply_rotary(q, emb)
        k = apply_rotary(k, emb)
        scores = jnp.einsum('bhtd,bhsd->bhts', q, k) / math.sqrt(hd)
        attn = jax.nn.softmax(scores, axis=-1)
        out = jnp.einsum('bhts,bhsd->bhtd', attn, v)
        out = out.transpose(0, 2, 1, 3).reshape(b, t, c)
        return out @ out_w.T + out_b

    def _L0_ffn_ref(x, router_w0, wg0, wu0, wd0, router_w1, wg1, wu1, wd1):
        import jax, jax.numpy as jnp
        from jax import lax
        import numpy as np
        D_MODEL = 256
        HIDDEN = 128
        N_EXPERTS = 32
        TOP_K = 2
        B, S = (1, 1024)

        def _moe_group(x2, router_w, wg, wu, wd, top_k):
            T = x2.shape[0]
            n_experts = router_w.shape[1]
            logits = x2 @ router_w
            scores = jax.nn.softmax(logits, axis=-1)
            expert_weights, expert_indices = lax.top_k(scores, top_k)
            flat_e = expert_indices.reshape(-1)
            flat_w = expert_weights.reshape(-1)
            flat_t = jnp.repeat(jnp.arange(T), top_k)
            order = jnp.argsort(flat_e)
            tok = flat_t[order]
            xs = x2[tok]
            group_sizes = jnp.bincount(flat_e, length=n_experts).astype(jnp.int32)
            gate = lax.ragged_dot(xs, wg, group_sizes)
            up = lax.ragged_dot(xs, wu, group_sizes)
            ys = lax.ragged_dot(jax.nn.silu(gate) * up, wd, group_sizes)
            ys = ys * flat_w[order][:, None]
            return jnp.zeros_like(x2).at[tok].add(ys)
        b, s, d = x.shape
        x2 = x.reshape(-1, d)
        out0 = _moe_group(x2, router_w0, wg0, wu0, wd0, TOP_K)
        out1 = _moe_group(x2, router_w1, wg1, wu1, wd1, TOP_K)
        out = (out0 * TOP_K + out1 * TOP_K) / (TOP_K + TOP_K)
        return out.reshape(b, s, d)

    def _L1_attn_ref(x, Wq, Wk, Wv, Wb, Wg, Wo, bo, ln1_g, ln1_b, ln2_g, ln2_b, w1, b1, w2, b2):
        import jax, jax.numpy as jnp
        import numpy as np
        D_MODEL = 256
        N_HEADS = 16
        HEAD_DIM = D_MODEL // N_HEADS
        EPS = 1e-05

        def _layernorm(x, g, b):
            mu = jnp.mean(x, axis=-1, keepdims=True)
            var = jnp.mean(jnp.square(x - mu), axis=-1, keepdims=True)
            return (x - mu) * jax.lax.rsqrt(var + EPS) * g + b

        def _gdn(x, Wq, Wk, Wv, Wb, Wg, Wo, bo):
            B, S, D = x.shape
            H, Dh = (N_HEADS, HEAD_DIM)
            q = (x @ Wq).reshape(B, S, H, Dh) * Dh ** (-0.5)
            k = (x @ Wk).reshape(B, S, H, Dh)
            k = k / (jnp.linalg.norm(k, axis=-1, keepdims=True) + 1e-06)
            v = (x @ Wv).reshape(B, S, H, Dh)
            beta = jax.nn.sigmoid(x @ Wb)
            g = jax.nn.sigmoid(x @ Wg)
            qt = jnp.moveaxis(q, 1, 0)
            kt = jnp.moveaxis(k, 1, 0)
            vt = jnp.moveaxis(v, 1, 0)
            bt = jnp.moveaxis(beta, 1, 0)
            gt = jnp.moveaxis(g, 1, 0)
            S0 = jnp.zeros((B, H, Dh, Dh), x.dtype)

            def step(Sst, inp):
                q_t, k_t, v_t, b_t, g_t = inp
                Sst = Sst * g_t[..., None, None]
                kS = jnp.einsum('bhk,bhkv->bhv', k_t, Sst)
                Sst = Sst + b_t[..., None, None] * jnp.einsum('bhk,bhv->bhkv', k_t, v_t - kS)
                o_t = jnp.einsum('bhk,bhkv->bhv', q_t, Sst)
                return (Sst, o_t)
            _, out = jax.lax.scan(step, S0, (qt, kt, vt, bt, gt))
            out = jnp.moveaxis(out, 0, 1).reshape(B, S, D)
            return out @ Wo + bo
        x = x + _gdn(_layernorm(x, ln1_g, ln1_b), Wq, Wk, Wv, Wb, Wg, Wo, bo)
        h = _layernorm(x, ln2_g, ln2_b)
        h = jax.nn.gelu(h @ w1 + b1, approximate=False) @ w2 + b2
        return x + h

    def _L1_ffn_ref(x, norm_g, norm_b, slot_g, slot_b, scale, slot_embeds, Wg, bg, Wu, bu, Wd, bd):
        import jax, jax.numpy as jnp
        import numpy as np
        B, N, D = (4, 1024, 256)
        E, S, F = (16, 64, 512)
        DO = 256
        EPS = 1e-05

        def _layernorm(x, g, b):
            mu = jnp.mean(x, axis=-1, keepdims=True)
            var = jnp.mean(jnp.square(x - mu), axis=-1, keepdims=True)
            return (x - mu) * jax.lax.rsqrt(var + EPS) * g + b
        x = _layernorm(x, norm_g, norm_b)
        se = _layernorm(slot_embeds, slot_g, slot_b) * scale
        logits = jnp.einsum('bnd,esd->bnes', x, se)
        dispatch = jax.nn.softmax(logits, axis=1)
        combine = jax.nn.softmax(logits.reshape(x.shape[0], x.shape[1], -1), axis=-1)
        slots = jnp.einsum('bnd,bnes->besd', x, dispatch)
        gate = jax.nn.gelu(jnp.einsum('besd,edf->besf', slots, Wg) + bg[None, :, None, :], approximate=False)
        up = jnp.einsum('besd,edf->besf', slots, Wu) + bu[None, :, None, :]
        eout = jnp.einsum('besf,efo->beso', gate * up, Wd) + bd[None, :, None, :]
        eout = eout.reshape(eout.shape[0], -1, eout.shape[-1])
        return jnp.einsum('bns,bso->bno', combine, eout)
    x = L0_attn_x
    x = x + _L0_attn_ref(_layernorm(x, axis=-1), L0_attn_qkv_w, L0_attn_qkv_b, L0_attn_out_w, L0_attn_out_b)
    x = x + _L0_ffn_ref(_layernorm(x, axis=-1), L0_ffn_router_w0, L0_ffn_wg0, L0_ffn_wu0, L0_ffn_wd0, L0_ffn_router_w1, L0_ffn_wg1, L0_ffn_wu1, L0_ffn_wd1)
    x = x + _L1_attn_ref(_layernorm(x, axis=-1), L1_attn_Wq, L1_attn_Wk, L1_attn_Wv, L1_attn_Wb, L1_attn_Wg, L1_attn_Wo, L1_attn_bo, L1_attn_ln1_g, L1_attn_ln1_b, L1_attn_ln2_g, L1_attn_ln2_b, L1_attn_w1, L1_attn_b1, L1_attn_w2, L1_attn_b2)
    x = x + _L1_ffn_ref(_layernorm(x, axis=-1), L1_ffn_norm_g, L1_ffn_norm_b, L1_ffn_slot_g, L1_ffn_slot_b, L1_ffn_scale, L1_ffn_slot_embeds, L1_ffn_Wg, L1_ffn_bg, L1_ffn_Wu, L1_ffn_bu, L1_ffn_Wd, L1_ffn_bd)
    return x

_drawn_inputs = setup_inputs


def setup_inputs(seed=0):
    import zlib

    import numpy as np

    out = dict(_drawn_inputs(seed))
    spreads = {'L1_attn_bo': (0.0, 0.8),
     'L1_attn_ln1_g': (1.0, 0.6),
     'L1_attn_ln1_b': (0.0, 0.8),
     'L1_attn_ln2_g': (1.0, 0.6),
     'L1_attn_ln2_b': (0.0, 2.0),
     'L1_attn_b1': (0.0, 2.0),
     'L1_attn_b2': (0.0, 0.8),
     'L1_ffn_norm_g': (1.0, 0.2),
     'L1_ffn_norm_b': (0.0, 0.511),
     'L1_ffn_slot_g': (1.0, 0.2),
     'L1_ffn_slot_b': (0.0, 0.592),
     'L1_ffn_bg': (0.0, 1.817),
     'L1_ffn_bu': (0.0, 1.878),
     'L1_ffn_bd': (0.0, 0.8)}
    factors = {'L0_attn_qkv_w': 8.0,
     'L0_attn_qkv_b': 5.583,
     'L0_attn_out_w': 5.587,
     'L0_ffn_router_w0': 8.0,
     'L0_ffn_wg0': 8.0,
     'L0_ffn_wu0': 8.0,
     'L0_ffn_wd0': 8.0,
     'L0_ffn_router_w1': 8.0,
     'L0_ffn_wg1': 8.0,
     'L0_ffn_wu1': 8.0,
     'L0_ffn_wd1': 8.0,
     'L1_attn_Wq': 8.0,
     'L1_attn_Wk': 8.0,
     'L1_attn_Wv': 8.0,
     'L1_attn_Wb': 8.0,
     'L1_attn_Wg': 8.0,
     'L1_attn_Wo': 8.0,
     'L1_attn_w1': 3.799,
     'L1_attn_w2': 3.03}
    for name, (base, spread) in spreads.items():
        noise = np.random.default_rng([zlib.crc32(name.encode()), seed]).standard_normal(out[name].shape)
        drawn = base * np.exp(spread * noise) if base else spread * noise
        out[name] = jnp.asarray(drawn.astype(out[name].dtype))
    for name, factor in factors.items():
        out[name] = (out[name] * factor).astype(out[name].dtype)
    return out
```

```python
from contextlib import ExitStack

import numpy as np

import concourse.bass as bass
from concourse import mybir

F32 = mybir.dt.float32
BF16 = mybir.dt.bfloat16
I32 = mybir.dt.int32
U32 = mybir.dt.uint32
ALU = mybir.AluOpType
ACT = mybir.ActivationFunctionType
X = mybir.AxisListType.X

P = 128
D = 256
KD = D // P
B = 2
S = 2048
T = B * S
NT = T // P
ST = S // P
H = 16
HD = D // H
EPS = 1e-5


class Steps:

    def __init__(self, sem, per=1, ahead=2):
        self.sem, self.per, self.ahead = sem, per, ahead

    def prime(self, eng):
        eng.sem_inc(self.sem, self.per * self.ahead)

    def at(self, t, j=None):
        return t * self.per + (self.ahead * self.per + (self.per if j is None else j))

    def before(self, t, back=None):
        back = self.ahead if back is None else back
        return t * self.per + (self.ahead - back + 1) * self.per


class Transfers:

    def __init__(self, sems, per=1, soft=False):
        self.sems, self.per, self.primed = sems, per, 0 if soft else 32

    def prime(self, eng):
        for s in self.sems:
            eng.sem_inc(s, 32 * self.per)

    def at(self, t, p):
        return t * (16 * self.per) + (self.primed + 32 - 16 * p) * self.per

    def before(self, t, p):
        return t * (16 * self.per) + (32 - 16 * p) * self.per


def hold(eng, gate):
    eng.sem_inc(gate, 1)


def staged(eng, n, *stages, first=0):
    lag = len(stages) - 1

    def peeled(r):
        for s, stage in enumerate(stages):
            if 0 <= r - s < n:
                stage(first + r - s, (r - s) % 2)

    pairs = (n - lag) // 2
    for r in range(lag):
        peeled(r)
    with eng.Fori(0, pairs) as i:
        for r in (lag, lag + 1):
            for s, stage in enumerate(stages):
                stage(i * 2 + (first + r - s), (r - s) % 2)
    for r in range(lag + 2 * pairs, n + lag):
        peeled(r)


class Semaphores:

    def __init__(self, nc, lasting):
        self.nc, self.lasting, self.ctx, self.taken = nc, lasting, ExitStack(), []

    def __enter__(self):
        return self

    def __exit__(self, *a):
        return self.ctx.__exit__(*a)

    def take(self, name, soft=False):
        if soft:
            return self.lasting.enter_context(self.nc.semaphore(name))
        self.taken.append(self.ctx.enter_context(self.nc.semaphore(name)))
        return self.taken[-1]

    def clear(self):
        with self.nc.Block() as block:
            @block.sync
            def _(sp):
                for sem in self.taken:
                    sp.sem_clear(sem)
        self.ctx.close()
        self.taken = []


class Phase:

    def __init__(self, nc, name, sems):
        self.nc, self.name, self.sems, self.ctx = nc, name, sems, ExitStack()

    def __enter__(self):
        self.ctx.__enter__()
        return self

    def __exit__(self, *a):
        return self.ctx.__exit__(*a)

    def sb(self, name, shape, dt=F32):
        return self.ctx.enter_context(self.nc.sbuf_tensor(f"{self.name}_{name}", shape, dt))

    def ps(self, name, shape, dt=F32):
        return self.ctx.enter_context(self.nc.psum_tensor(f"{self.name}_{name}", shape, dt))

    def sem(self, name, soft=False):
        return self.sems.take(f"{self.name}_{name}", soft)

    def steps(self, name, per=1, ahead=2):
        return Steps(self.sem(name), per, ahead)

    def transfers(self, name, per=1, soft=False):
        return Transfers([self.sem(f"{name}{p}", soft) for p in range(2)], per, soft)

    def block(self):
        return self.ctx.enter_context(self.nc.Block())


def row_broadcast(vec, parts=P):
    return vec.rearrange("(a n) -> a n", a=1).to_broadcast([parts, vec.shape[0]])


def identity(nc, ph, ident):
    zeroed, made = ph.sem("ident_zeroed"), ph.sem("ident_made")
    with nc.Block() as block:
        @block.gpsimd
        def _(pool):
            pool.memset(ident[:, :], 0.0).then_inc(zeroed, 1)
            pool.wait_ge(zeroed, 1)
            pool.affine_select(out=ident[:, :], in_=ident[:, :], compare_op=ALU.not_equal, fill=1.0,
                               base=0, pattern=[[-1, P]], channel_multiplier=1).then_inc(made, 1)
            pool.wait_ge(made, 1)


def rope_tables():
    inv = (1.0 / np.float32(10000.0) ** (np.arange(0, HD, 2, dtype=np.float32) / np.float32(HD))).astype(np.float32)
    freqs = np.arange(S, dtype=np.float32)[:, None] * inv[None, :]
    emb = np.concatenate([np.sin(freqs), np.cos(freqs)], axis=-1).astype(np.float32)
    sin, cos = emb[:, ::2], emb[:, 1::2]
    lay = lambda a: a.reshape(ST, P, HD // 2).transpose(1, 0, 2)
    both = np.stack([lay(cos), lay(sin)], axis=1)
    return np.ascontiguousarray(np.concatenate([both, both], axis=2))


def phase_qkv(nc, sems, x, qkv_w, qkv_b, rope, qk_sb, v_sb, ident):
    C3 = 3 * D
    WC = C3 // P
    HH = 2 * H
    HE = HD // 2
    with Phase(nc, "qkv", sems) as ph:
        w_in = ph.sb("w_in", [P, WC, D])
        w_t = ph.sb("w_t", [P, KD, C3])
        bias = ph.sb("bias", [P, C3])
        rope_sb = ph.sb("rope", [P, 2, NT, HE])
        x_in = ph.sb("x_in", [P, 2, D])
        stats = ph.sb("stats", [P, 2, 6])
        mv = ph.sb("mv", [P, 2, 2])
        veps = ph.sb("veps", [P, 2, 1])
        rstd = ph.sb("rstd", [P, 2, 1])
        neg_half = ph.sb("neg_half", [P, 1])
        xn = ph.sb("xn", [P, 2, D])
        xn_t = ph.sb("xn_t", [P, 2, KD, P])
        qk_raw = ph.sb("qk_raw", [P, 2, HH, HE, 2])
        prod = ph.sb("prod", [P, 2, 4, HH, HE])
        ps_t = [ph.ps(f"ps_t{i}", [P, 512]) for i in range(2)]
        ps_q = [ph.ps(f"ps_q{i}", [P, 1024]) for i in range(2)]

        consts_in = ph.sem("consts_in")
        ones_set = ph.sem("ones_set")
        w_turned = ph.steps("w_turned")
        w_kept = ph.steps("w_kept")
        x_landed = ph.transfers("x_landed")
        gate = ph.sem("gate")
        norm = ph.steps("norm", 4)
        rstd_ready = ph.steps("rstd_ready")
        turned = ph.steps("turned")
        xn_t_ready = ph.steps("xn_t_ready")
        projected = ph.steps("projected")
        biased = ph.steps("biased", 2)
        first_half = ph.steps("first_half", 3)
        second_half = ph.steps("second_half", 3)
        block = ph.block()

        @block.sync
        def _(sp):
            sp.dma_start(w_in[:, :, :], qkv_w.rearrange("(c p) d -> p c d", p=P)).then_inc(consts_in, 16)
            sp.dma_start(bias[:, :], row_broadcast(qkv_b)).then_inc(consts_in, 16)
            sp.dma_start(rope_sb[:, :, :, :], rope).then_inc(consts_in, 16)
            x_landed.prime(sp)

            def load(t, p):
                sp.wait_ge(norm.sem, norm.before(t))
                sp.dma_start(x_in[:, p, :], x[bass.ds(t * P, P), :]).then_inc(x_landed.sems[p], 32)
            staged(sp, NT, load)

        @block.vector
        def _(v):
            norm.prime(v)
            biased.prime(v)
            first_half.prime(v)
            v.memset(neg_half[:, :], -0.5).then_inc(ones_set, 1)
            v.wait_ge(consts_in, 48)

            def normalise(t, p):
                v.wait_ge(x_landed.sems[p], x_landed.at(t, p))
                v.bn_stats(stats[:, p, :], x_in[:, p, :]).then_inc(norm.sem, 1)
                v.wait_ge(norm.sem, norm.at(t, 1))
                hold(v, gate)
                v.bn_aggr(mv[:, p, :], stats[:, p, :]).then_inc(norm.sem, 1)
                v.wait_ge(norm.sem, norm.at(t, 2))
                v.tensor_scalar(veps[:, p, :], mv[:, p, 1:2], EPS, None, ALU.add).then_inc(norm.sem, 1)
                v.wait_ge(rstd_ready.sem, rstd_ready.at(t))
                v.tensor_scalar(xn[:, p, :], x_in[:, p, :], mv[:, p, 0:1], rstd[:, p, :],
                                ALU.subtract, ALU.mult).then_inc(norm.sem, 1)

            def rotate(t, p):
                v.wait_ge(projected.sem, projected.at(t))
                v.wait_ge(second_half.sem, second_half.before(t))
                v.wait_ge(first_half.sem, first_half.before(t, 1))
                v.tensor_tensor(qk_raw[:, p, :, :, :].rearrange("q h d e -> q (h d e)"),
                                ps_q[p][:, 0:2 * D], bias[:, 0:2 * D], ALU.add).then_inc(biased.sem, 1)
                v.tensor_tensor(v_sb[:, bass.ds(t, 1), :].rearrange("q a c -> q (a c)"), ps_q[p][:, 2 * D:C3],
                                bias[:, 2 * D:C3], ALU.add).then_inc(biased.sem, 1)
                v.wait_ge(biased.sem, biased.at(t, 1))
                cos = rope_sb[:, 0, bass.ds(t, 1), :].to_broadcast([P, HH, HE])
                sin = rope_sb[:, 1, bass.ds(t, 1), :].to_broadcast([P, HH, HE])
                v.tensor_tensor(prod[:, p, 0, :, :], qk_raw[:, p, :, :, 0], cos, ALU.mult).then_inc(first_half.sem, 1)
                v.tensor_tensor(prod[:, p, 1, :, :], qk_raw[:, p, :, :, 1], sin, ALU.mult).then_inc(first_half.sem, 1)
                v.wait_ge(first_half.sem, first_half.at(t, 2))
                out = qk_sb[:, bass.ds(t, 1), :].rearrange("q a (h e) -> q (a h) e", h=HH)
                v.tensor_tensor(out[:, :, 0:HE], prod[:, p, 0, :, :], prod[:, p, 1, :, :],
                                ALU.subtract).then_inc(first_half.sem, 1)
            staged(v, NT, normalise, rotate)

        @block.gpsimd
        def _(pool):
            rstd_ready.prime(pool)
            second_half.prime(pool)
            pool.wait_ge(consts_in, 48)
            pool.wait_ge(ones_set, 1)

            def root(t, p):
                pool.wait_ge(norm.sem, norm.at(t, 3))
                pool.tensor_tensor(rstd[:, p, :], veps[:, p, :], neg_half[:, :], ALU.pow).then_inc(rstd_ready.sem, 1)

            def rotate(t, p):
                pool.wait_ge(biased.sem, biased.at(t, 1))
                pool.wait_ge(second_half.sem, second_half.before(t, 1))
                cos = rope_sb[:, 0, bass.ds(t, 1), :].to_broadcast([P, HH, HE])
                sin = rope_sb[:, 1, bass.ds(t, 1), :].to_broadcast([P, HH, HE])
                pool.tensor_tensor(prod[:, p, 2, :, :], qk_raw[:, p, :, :, 0], sin, ALU.mult).then_inc(second_half.sem, 1)
                pool.tensor_tensor(prod[:, p, 3, :, :], qk_raw[:, p, :, :, 1], cos, ALU.mult).then_inc(second_half.sem, 1)
                pool.wait_ge(second_half.sem, second_half.at(t, 2))
                out = qk_sb[:, bass.ds(t, 1), :].rearrange("q a (h e) -> q (a h) e", h=HH)
                pool.tensor_tensor(out[:, :, HE:HD], prod[:, p, 2, :, :], prod[:, p, 3, :, :],
                                   ALU.add).then_inc(second_half.sem, 1)
            staged(pool, NT, root, rotate)

        @block.tensor
        def _(pe):
            w_turned.prime(pe)
            turned.prime(pe)
            projected.prime(pe)
            pe.wait_ge(consts_in, 48)
            for c in range(WC):
                pe.wait_ge(w_kept.sem, w_kept.before(c))
                for k in range(KD):
                    mm = pe.transpose(ps_t[c % 2][:, k * P:(k + 1) * P], w_in[:, c, k * P:(k + 1) * P], ident[:, :])
                mm.then_inc(w_turned.sem, 1)
            pe.wait_ge(w_kept.sem, w_kept.at(WC - 1))

            def turn(t, p):
                pe.wait_ge(norm.sem, norm.at(t))
                for k in range(KD):
                    mm = pe.transpose(ps_t[p][:, k * P:(k + 1) * P], xn[:, p, k * P:(k + 1) * P], ident[:, :])
                mm.then_inc(turned.sem, 1)

            def project(t, p):
                pe.wait_ge(xn_t_ready.sem, xn_t_ready.at(t))
                pe.wait_ge(biased.sem, biased.before(t))
                for a, b in ((0, 512), (512, C3)):
                    for k in range(KD):
                        mm = pe.matmul(ps_q[p][:, a:b], xn_t[:, p, k, :], w_t[:, k, a:b],
                                       start=(k == 0), stop=(k == KD - 1))
                mm.then_inc(projected.sem, 1)
            staged(pe, NT, turn, project)

        @block.scalar
        def _(act):
            w_kept.prime(act)
            xn_t_ready.prime(act)
            for c in range(WC):
                act.wait_ge(w_turned.sem, w_turned.at(c))
                nc.scalar.copy(w_t[:, :, c * P:(c + 1) * P],
                               ps_t[c % 2][:, 0:D].rearrange("q (k n) -> q k n", k=KD)).then_inc(w_kept.sem, 1)

            def keep(t, p):
                act.wait_ge(turned.sem, turned.at(t))
                nc.scalar.copy(xn_t[:, p, :, :].rearrange("q k n -> q (k n)"), ps_t[p][:, 0:D]).then_inc(xn_t_ready.sem, 1)
            staged(act, NT, keep)


def phase_attention(nc, sems, qk_sb, v_sb, o_sb, ident, ident_bf):
    PARTS = 3
    PAIRS = 6 * HD
    ROWS = PAIRS + PARTS
    W = 512
    CH = S // W
    NH = 2
    GK = 4
    VW = 32
    STEPS = S // W * (ST // GK)
    GS = ST // GK
    WT = W // P
    TG = 1024 // P
    GR = ST // TG
    RING = 4
    SCALE = float(HD) ** -0.5
    plan = [[], []] + [[0, 1], [2, 3]] + [[j] for j in range(4, ST)]
    assert len(plan) == STEPS

    with Phase(nc, "att", sems) as ph:
        k_stack = ph.sb("k_stack", [P, 2, ST, ROWS], BF16)
        q_stack = ph.sb("q_stack", [P, 2, ST, PAIRS], BF16)
        rest = ph.sb("rest", [P, 2, ST, HD])
        k_t = ph.sb("k_t", [P, 2, S], BF16)
        q_t = ph.sb("q_t", [P, 2, S], BF16)
        prob = ph.sb("prob", [P, RING, 2, W])
        v_h = ph.sb("v_h", [P, 2, ST, VW])
        o_t = ph.sb("o_t", [P, W])
        o_sum = ph.sb("o_sum", [P, WT, HD + 1])
        maxes = ph.sb("maxes", [P, 2, ST, CH])
        neg_max = ph.sb("neg_max", [P, ST])
        max_rest = ph.sb("max_rest", [P, ST])
        max_parts = ph.sb("max_parts", [P, ST, 4], BF16)
        sums_inv = ph.sb("sums_inv", [P, WT, 1])
        ps_m = [ph.ps(f"ps_m{i}", [P, W]) for i in range(2)]
        ps_s = [ph.ps(f"ps_s{i}", [P, 2 * W]) for i in range(NH)]
        ps_o = ph.ps("ps_o", [P, W])
        ps_tro = ph.ps("ps_tr", [P, W])
        ps_tr = ps_tro[:, :].bitcast(BF16)

        set_up = ph.sem("set_up")
        split_k = ph.steps("split_k", 6)
        split_q = ph.steps("split_q", 6)
        v_copied = ph.steps("v_copied")
        gate = ph.sem("gate")
        turned = ph.steps("turned", 3 * GR)
        kept = ph.steps("kept", 3 * GR)
        max_scores = ph.steps("max_scores", ST * CH)
        reduced = ph.steps("reduced", ST * CH)
        max_split = ph.steps("max_split", 5)
        scores = ph.steps("scores", STEPS * NH)
        expd = ph.steps("expd", STEPS * NH)
        pv = ph.steps("pv", STEPS)
        o_kept = ph.steps("o_kept", CH)
        o_turned = ph.steps("o_turned", CH)
        o_out = ph.steps("o_out", 3 * CH)
        block = ph.block()

        def heads(eng, turn):
            with eng.Fori(0, H - 1) as h:
                turn(h * 2, h, 0, False)
                turn(h * 2 + 1, h, 1, False)
            turn(2 * H - 2, H - 1, 0, False)
            turn(2 * H - 1, H - 1, 1, True)

        @block.gpsimd
        def _(pool):
            split_k.prime(pool)
            split_q.prime(pool)
            v_copied.prime(pool)
            pool.wait_ge(set_up, 4)

            def split(n, h, p, last=False):
                tiles = slice(p * ST, (p + 1) * ST)
                k = qk_sb[:, tiles, bass.ds(h * HD + D, HD)]
                q = qk_sb[:, tiles, bass.ds(h * HD, HD)]
                ks = k_stack[:, p, :, 0:PAIRS].rearrange("q n (s e) -> q n s e", e=HD)
                qs = q_stack[:, p, :, :].rearrange("q n (s e) -> q n s e", e=HD)
                pool.wait_ge(pv.sem, pv.before(n))
                hold(pool, gate)
                pool.tensor_copy(v_h[:, p, :, 0:HD], v_sb[:, tiles, bass.ds(h * HD, HD)]).then_inc(v_copied.sem, 1)
                pool.wait_ge(turned.sem, turned.before(n))
                hold(pool, gate)
                pool.tensor_copy(ks[:, :, 0, :], k).then_inc(split_k.sem, 1)
                pool.tensor_copy(qs[:, :, 0, :], q).then_inc(split_q.sem, 1)
                pool.wait_ge(split_k.sem, split_k.at(n, 1))
                hold(pool, gate)
                pool.tensor_tensor(rest[:, 0, :, :], k, ks[:, :, 0, :], ALU.subtract).then_inc(split_k.sem, 1)
                pool.wait_ge(split_q.sem, split_q.at(n, 1))
                hold(pool, gate)
                pool.tensor_tensor(rest[:, 1, :, :], q, qs[:, :, 0, :], ALU.subtract).then_inc(split_q.sem, 1)
                pool.wait_ge(split_k.sem, split_k.at(n, 2))
                hold(pool, gate)
                pool.tensor_copy(ks[:, :, 2, :], rest[:, 0, :, :]).then_inc(split_k.sem, 1)
                pool.wait_ge(split_q.sem, split_q.at(n, 2))
                hold(pool, gate)
                pool.tensor_copy(qs[:, :, 1, :], rest[:, 1, :, :]).then_inc(split_q.sem, 1)
                pool.wait_ge(split_k.sem, split_k.at(n, 3))
                hold(pool, gate)
                pool.tensor_tensor(ks[:, :, 4, :], rest[:, 0, :, :], ks[:, :, 2, :], ALU.subtract).then_inc(split_k.sem, 1)
                pool.tensor_copy(ks[:, :, 1:6:4, :], ks[:, :, 0:1, :].to_broadcast([P, ST, 2, HD])).then_inc(split_k.sem, 1)
                pool.tensor_copy(ks[:, :, 3, :], ks[:, :, 2, :]).then_inc(split_k.sem, 1)
                pool.wait_ge(split_q.sem, split_q.at(n, 3))
                hold(pool, gate)
                pool.tensor_tensor(qs[:, :, 5, :], rest[:, 1, :, :], qs[:, :, 1, :], ALU.subtract).then_inc(split_q.sem, 1)
                pool.tensor_copy(qs[:, :, 2:4, :], qs[:, :, 0:2, :]).then_inc(split_q.sem, 1)
                pool.tensor_copy(qs[:, :, 4, :], qs[:, :, 0, :]).then_inc(split_q.sem, 1)
            heads(pool, split)

        @block.tensor
        def _(pe):
            turned.prime(pe)
            max_scores.prime(pe)
            scores.prime(pe)
            pv.prime(pe)
            o_turned.prime(pe)
            pe.wait_ge(set_up, 4)

            def turn_group(n, p, g, outs):
                kind, g0 = divmod(g, GR)
                if g == 0:
                    pe.wait_ge(split_k.sem, split_k.at(n))
                if g == GR:
                    pe.wait_ge(split_q.sem, split_q.at(n))
                if g == 2 * GR:
                    pe.wait_ge(max_split.sem, max_split.at(n))
                pe.wait_ge(kept.sem, kept.at(n, g))
                pe.wait_ge(o_out.sem, o_out.at(n - 1, 3 * outs))
                for j in range(TG):
                    tile = g0 * TG + j
                    if kind == 0:
                        mm = pe.transpose(ps_tr[0:ROWS, j * P:(j + 1) * P], k_stack[:, p, tile, :], ident_bf[:, :])
                    elif kind == 1:
                        mm = pe.transpose(ps_tr[0:PAIRS, j * P:(j + 1) * P], q_stack[:, p, tile, :], ident_bf[:, :])
                    else:
                        mm = pe.transpose(ps_tr[PAIRS:ROWS, j * P:(j + 1) * P], max_parts[:, tile, 0:PARTS], ident_bf[:, :])
                mm.then_inc(turned.sem, 1)

            def first_pass(n, p, tile):
                if tile == 0:
                    pe.wait_ge(kept.sem, kept.at(n, 2 * GR))
                for c in range(CH):
                    i = tile * CH + c
                    pe.wait_ge(reduced.sem, reduced.at(n, i - 1))
                    pe.matmul(ps_m[i % 2][:, :], q_t[0:PAIRS, p, tile * P:(tile + 1) * P],
                              k_t[0:PAIRS, p, c * W:(c + 1) * W], start=True, stop=True).then_inc(max_scores.sem, 1)

            def score(n, p, j, half):
                if j == 0 and half == 0:
                    pe.wait_ge(kept.sem, kept.at(n))
                chunk, group = divmod(j, GS)
                pe.wait_ge(expd.sem, expd.at(n, j * NH + half - NH + 1))
                for i in range(2):
                    tile = group * GK + half * 2 + i
                    mm = pe.matmul(ps_s[half][:, i * W:(i + 1) * W], k_t[0:ROWS, p, tile * P:(tile + 1) * P],
                                   q_t[0:ROWS, p, chunk * W:(chunk + 1) * W], start=True, stop=True)
                mm.then_inc(scores.sem, 1)

            def against_v(n, p, j):
                chunk, group = divmod(j, GS)
                if j == 0:
                    pe.wait_ge(v_copied.sem, v_copied.at(n))
                if group == 0:
                    pe.wait_ge(o_kept.sem, o_kept.at(n, chunk))
                pe.wait_ge(expd.sem, expd.at(n, (j + 1) * NH))
                for i in range(GK):
                    mm = pe.matmul(ps_o[i * VW:(i + 1) * VW, :], v_h[:, p, group * GK + i, :],
                                   prob[:, (j * NH + i // 2) % RING, i % 2, :],
                                   start=(group == 0), stop=(group == GS - 1), skip_group_check=True)
                mm.then_inc(pv.sem, 1)

            def turn_output(n, chunk, groups):
                pe.wait_ge(o_kept.sem, o_kept.at(n, chunk + 1))
                pe.wait_ge(o_out.sem, o_out.at(n, 3 * chunk))
                pe.wait_ge(kept.sem, kept.at(n + 1, groups))
                for i in range(WT):
                    mm = pe.transpose(ps_tro[:, i * P:(i + 1) * P], o_t[:, i * P:(i + 1) * P], ident[:, :])
                mm.then_inc(o_turned.sem, 1)

            def turn(n, h, p, last):
                for j in range(STEPS):
                    if not last:
                        for tile in plan[j]:
                            first_pass(n + 1, 1 - p, tile)
                    for half in range(NH):
                        if not last and j < GR:
                            turn_group(n + 1, 1 - p, j * 2 + half, 0)
                        score(n, p, j, half)
                    if j % GS == 1 and j > GS:
                        turn_output(n, j // GS - 1, 0 if last else 2 * GR)
                    if j:
                        against_v(n, p, j - 1)
                against_v(n, p, STEPS - 1)
                if not last:
                    for g in range(2 * GR, 3 * GR):
                        turn_group(n + 1, 1 - p, g, CH - 1)
                turn_output(n, CH - 1, 0 if last else 3 * GR)

            for g in range(2 * GR):
                turn_group(0, 0, g, 0)
            for tile in range(ST):
                first_pass(0, 0, tile)
            for g in range(2 * GR, 3 * GR):
                turn_group(0, 0, g, 0)
            heads(pe, turn)

        @block.scalar
        def _(act):
            kept.prime(act)
            expd.prime(act)
            o_kept.prime(act)

            def keep(n, p, g):
                kind, g0 = divmod(g, GR)
                act.wait_ge(turned.sem, turned.at(n, g + 1))
                cols = slice(g0 * TG * P, (g0 + 1) * TG * P)
                if kind == 0:
                    nc.scalar.copy(k_t[0:ROWS, p, cols], ps_tr[0:ROWS, :]).then_inc(kept.sem, 1)
                elif kind == 1:
                    nc.scalar.copy(q_t[0:PAIRS, p, cols], ps_tr[0:PAIRS, :]).then_inc(kept.sem, 1)
                else:
                    nc.scalar.copy(q_t[PAIRS:ROWS, p, cols], ps_tr[PAIRS:ROWS, :]).then_inc(kept.sem, 1)

            def keep_output(n, chunk):
                act.wait_ge(pv.sem, pv.at(n, (chunk + 1) * GS))
                act.wait_ge(o_turned.sem, o_turned.at(n, chunk))
                nc.scalar.copy(o_t[:, :], ps_o[:, :]).then_inc(o_kept.sem, 1)

            def turn(n, h, p, last):
                for j in range(STEPS):
                    for half in range(NH):
                        if not last and j < GR:
                            keep(n + 1, 1 - p, j * 2 + half)
                        i = j * NH + half
                        act.wait_ge(scores.sem, scores.at(n, i + 1))
                        act.wait_ge(pv.sem, pv.at(n, j - RING // NH + 1))
                        nc.scalar.activation(prob[:, i % RING, :, :].rearrange("q a w -> q (a w)"), ps_s[half][:, :],
                                             ACT.Exp, scale=SCALE).then_inc(expd.sem, 1)
                    if j % GS == 0 and j:
                        keep_output(n, j // GS - 1)
                keep_output(n, CH - 1)
                if not last:
                    for g in range(2 * GR, 3 * GR):
                        keep(n + 1, 1 - p, g)

            for g in range(3 * GR):
                keep(0, 0, g)
            heads(act, turn)

        @block.vector
        def _(v):
            reduced.prime(v)
            max_split.prime(v)
            o_out.prime(v)
            v.memset(k_stack[:, 0, :, PAIRS:ROWS], 1.0).then_inc(set_up, 1)
            v.memset(k_stack[:, 1, :, PAIRS:ROWS], 1.0).then_inc(set_up, 1)
            v.memset(v_h[:, :, :, HD:VW], 0.0).then_inc(set_up, 1)
            v.wait_ge(set_up, 3)
            v.memset(v_h[:, :, :, HD:HD + 1], 1.0).then_inc(set_up, 1)

            def reduce(n, p, tile):
                for c in range(CH):
                    i = tile * CH + c
                    v.wait_ge(max_scores.sem, max_scores.at(n, i + 1))
                    v.tensor_reduce(maxes[:, p, tile, c:c + 1], ps_m[i % 2][:, :], X, ALU.max).then_inc(reduced.sem, 1)

            def split_max(n, p):
                v.wait_ge(reduced.sem, reduced.at(n))
                v.tensor_reduce(neg_max[:, :], maxes[:, p, :, :], X, ALU.max, negate=True).then_inc(max_split.sem, 1)
                v.wait_ge(max_split.sem, max_split.at(n, 1))
                v.wait_ge(turned.sem, turned.at(n, 0))
                v.tensor_copy(max_parts[:, :, 0], neg_max[:, :]).then_inc(max_split.sem, 1)
                v.wait_ge(max_split.sem, max_split.at(n, 2))
                v.tensor_tensor(max_rest[:, :], neg_max[:, :], max_parts[:, :, 0], ALU.subtract).then_inc(max_split.sem, 1)
                v.wait_ge(max_split.sem, max_split.at(n, 3))
                v.tensor_copy(max_parts[:, :, 1], max_rest[:, :]).then_inc(max_split.sem, 1)
                v.wait_ge(max_split.sem, max_split.at(n, 4))
                v.tensor_tensor(max_parts[:, :, 2], max_rest[:, :], max_parts[:, :, 1], ALU.subtract).then_inc(max_split.sem, 1)

            def output(n, h, p, chunk):
                v.wait_ge(o_turned.sem, o_turned.at(n, chunk + 1))
                v.tensor_reduce(o_sum[:, :, :],
                                ps_tro[:, :].rearrange("q (t g e) -> q t e g", t=WT, g=GK)[:, :, 0:HD + 1, :],
                                X, ALU.add).then_inc(o_out.sem, 1)
                v.wait_ge(o_out.sem, o_out.at(n, 3 * chunk + 1))
                v.reciprocal(sums_inv[:, :, :], o_sum[:, :, HD:HD + 1]).then_inc(o_out.sem, 1)
                v.wait_ge(o_out.sem, o_out.at(n, 3 * chunk + 2))
                tiles = slice(p * ST + chunk * WT, p * ST + (chunk + 1) * WT)
                v.tensor_tensor(o_sb[:, tiles, bass.ds(h * HD, HD)], o_sum[:, :, 0:HD],
                                sums_inv[:, :, :].to_broadcast([P, WT, HD]), ALU.mult).then_inc(o_out.sem, 1)

            def turn(n, h, p, last):
                for j in range(STEPS):
                    if not last:
                        for tile in plan[j]:
                            reduce(n + 1, 1 - p, tile)
                    if j % GS == 1 and j > GS:
                        output(n, h, p, j // GS - 1)
                if not last:
                    split_max(n + 1, 1 - p)
                output(n, h, p, CH - 1)

            for tile in range(ST):
                reduce(0, 0, tile)
            split_max(0, 0)
            heads(v, turn)


E = 32
G = 2
GE = G * E
TOPK = 2
HID = 128
SLOT_TILES = T * TOPK // P + E
SLOTS = SLOT_TILES * P


def phase_route(nc, sems, x, o_sb, out_w, out_b, routers, x1_sb, xn_sb, lg_sb, top_val, top_idx, ident):
    with Phase(nc, "route", sems) as ph:
        w_in = ph.sb("w_in", [P, KD, D])
        w_t = ph.sb("w_t", [P, KD, D])
        r_w = ph.sb("r_w", [P, KD, GE])
        bias = ph.sb("bias", [P, D])
        x_in = ph.sb("x_in", [P, 2, D])
        x_b = ph.sb("x_b", [P, 2, D])
        o_c = ph.sb("o_c", [P, 2, D])
        o_t = ph.sb("o_t", [P, 2, KD, P])
        x1 = ph.sb("x1", [P, 2, D])
        stats = ph.sb("stats", [P, 2, 6])
        mv = ph.sb("mv", [P, 2, 2])
        veps = ph.sb("veps", [P, 2, 1])
        rstd = ph.sb("rstd", [P, 2, 1])
        neg_half = ph.sb("neg_half", [P, 1])
        xn = ph.sb("xn", [P, 2, D])
        xn_t = ph.sb("xn_t", [P, 2, KD, P])
        val8 = ph.sb("val8", [P, 2, G, 8])
        idx8 = ph.sb("idx8", [P, 2, G, 8], U32)
        ps_t = [ph.ps(f"ps_t{i}", [P, 512]) for i in range(2)]
        ps_o = [ph.ps(f"ps_o{i}", [P, 512]) for i in range(2)]
        ps_x = [ph.ps(f"ps_x{i}", [P, 512]) for i in range(2)]
        ps_l = [ph.ps(f"ps_l{i}", [P, 512]) for i in range(2)]

        gate = ph.sem("gate")
        consts_in = ph.sem("consts_in")
        half_set = ph.sem("half_set")
        w_turned = ph.steps("w_turned")
        w_kept = ph.steps("w_kept")
        x_landed = ph.transfers("x_landed")
        copied = ph.steps("copied")
        x_b_ready = ph.steps("x_b_ready")
        rstd_ready = ph.steps("rstd_ready")
        kept_xn = ph.steps("kept_xn", 2)
        o_turned = ph.steps("o_turned")
        o_t_ready = ph.steps("o_t_ready")
        projected = ph.steps("projected")
        norm = ph.steps("norm", 5)
        xn_turned = ph.steps("xn_turned")
        xn_t_ready = ph.steps("xn_t_ready")
        routed = ph.steps("routed")
        topped = ph.steps("topped", 3 + 2 * G)
        block = ph.block()

        @block.sync
        def _(sp):
            x_landed.prime(sp)
            sp.dma_start(w_in[:, :, :], out_w.rearrange("(c p) d -> p c d", p=P)).then_inc(consts_in, 16)
            sp.dma_start(bias[:, :], row_broadcast(out_b)).then_inc(consts_in, 16)
            for g, r in enumerate(routers):
                sp.dma_start(r_w[:, :, g * E:(g + 1) * E], r.rearrange("(k p) e -> p k e", p=P)).then_inc(consts_in, 16)

            def load(t, p):
                sp.wait_ge(x_b_ready.sem, x_b_ready.before(t))
                sp.dma_start(x_in[:, p, :], x[bass.ds(t * P, P), :]).then_inc(x_landed.sems[p], 32)
            staged(sp, NT, load)

        @block.gpsimd
        def _(pool):
            for s in (copied, x_b_ready, rstd_ready, kept_xn):
                s.prime(pool)
            pool.memset(neg_half[:, :], -0.5).then_inc(half_set, 1)
            pool.wait_ge(half_set, 1)
            pool.wait_ge(consts_in, 16 * (2 + G))

            def prepare(t, p):
                pool.wait_ge(o_turned.sem, o_turned.before(t))
                hold(pool, gate)
                pool.tensor_copy(o_c[:, p, :], o_sb[:, bass.ds(t, 1), :].rearrange("q a c -> q (a c)")).then_inc(copied.sem, 1)
                pool.wait_ge(x_landed.sems[p], x_landed.at(t, p))
                pool.wait_ge(norm.sem, norm.before(t))
                pool.tensor_tensor(x_b[:, p, :], x_in[:, p, :], bias[:, :], ALU.add).then_inc(x_b_ready.sem, 1)

            def root(t, p):
                pool.wait_ge(norm.sem, norm.at(t, 4))
                pool.tensor_tensor(rstd[:, p, :], veps[:, p, :], neg_half[:, :], ALU.pow).then_inc(rstd_ready.sem, 1)

            def keep(t, p):
                pool.wait_ge(norm.sem, norm.at(t))
                hold(pool, gate)
                pool.tensor_copy(x1_sb[:, bass.ds(t, 1), :].rearrange("q a c -> q (a c)"), x1[:, p, :]).then_inc(kept_xn.sem, 1)
                pool.tensor_copy(xn_sb[:, bass.ds(t, 1), :].rearrange("q a c -> q (a c)"), xn[:, p, :]).then_inc(kept_xn.sem, 1)
            staged(pool, NT, prepare, root, keep)

        @block.tensor
        def _(pe):
            for s in (w_turned, o_turned, projected, xn_turned, routed):
                s.prime(pe)
            pe.wait_ge(consts_in, 16 * (2 + G))
            for c in range(KD):
                for k in range(KD):
                    mm = pe.transpose(ps_t[c % 2][:, k * P:(k + 1) * P], w_in[:, c, k * P:(k + 1) * P], ident[:, :])
                mm.then_inc(w_turned.sem, 1)
            pe.wait_ge(w_kept.sem, w_kept.at(KD - 1))

            def turn_o(t, p):
                pe.wait_ge(copied.sem, copied.at(t))
                for k in range(KD):
                    mm = pe.transpose(ps_t[p][:, k * P:(k + 1) * P], o_c[:, p, k * P:(k + 1) * P], ident[:, :])
                mm.then_inc(o_turned.sem, 1)

            def project(t, p):
                pe.wait_ge(o_t_ready.sem, o_t_ready.at(t))
                pe.wait_ge(norm.sem, norm.before(t))
                for k in range(KD):
                    mm = pe.matmul(ps_o[p][:, 0:D], o_t[:, p, k, :], w_t[:, k, :], start=(k == 0), stop=(k == KD - 1))
                mm.then_inc(projected.sem, 1)

            def turn_x(t, p):
                pe.wait_ge(norm.sem, norm.at(t))
                for k in range(KD):
                    mm = pe.transpose(ps_x[p][:, k * P:(k + 1) * P], xn[:, p, k * P:(k + 1) * P], ident[:, :])
                mm.then_inc(xn_turned.sem, 1)

            def route(t, p):
                pe.wait_ge(xn_t_ready.sem, xn_t_ready.at(t))
                pe.wait_ge(topped.sem, topped.before(t))
                for k in range(KD):
                    mm = pe.matmul(ps_l[p][:, 0:GE], xn_t[:, p, k, :], r_w[:, k, :], start=(k == 0), stop=(k == KD - 1))
                mm.then_inc(routed.sem, 1)
            staged(pe, NT, turn_o, project, turn_x, route)

        @block.scalar
        def _(act):
            for s in (w_kept, o_t_ready, xn_t_ready):
                s.prime(act)
            for c in range(KD):
                act.wait_ge(w_turned.sem, w_turned.at(c))
                nc.scalar.copy(w_t[:, :, c * P:(c + 1) * P],
                               ps_t[c % 2][:, 0:D].rearrange("q (k n) -> q k n", k=KD)).then_inc(w_kept.sem, 1)

            def keep_o(t, p):
                act.wait_ge(o_turned.sem, o_turned.at(t))
                nc.scalar.copy(o_t[:, p, :, :].rearrange("q k n -> q (k n)"), ps_t[p][:, 0:D]).then_inc(o_t_ready.sem, 1)

            def idle(t, p):
                pass

            def keep_x(t, p):
                act.wait_ge(xn_turned.sem, xn_turned.at(t))
                nc.scalar.copy(xn_t[:, p, :, :].rearrange("q k n -> q (k n)"), ps_x[p][:, 0:D]).then_inc(xn_t_ready.sem, 1)
            staged(act, NT, keep_o, idle, keep_x)

        @block.vector
        def _(v):
            norm.prime(v)
            topped.prime(v)

            def normalise(t, p):
                v.wait_ge(projected.sem, projected.at(t))
                v.wait_ge(x_b_ready.sem, x_b_ready.at(t))
                v.wait_ge(kept_xn.sem, kept_xn.before(t))
                v.tensor_tensor(x1[:, p, :], ps_o[p][:, 0:D], x_b[:, p, :], ALU.add).then_inc(norm.sem, 1)
                v.wait_ge(norm.sem, norm.at(t, 1))
                v.bn_stats(stats[:, p, :], x1[:, p, :]).then_inc(norm.sem, 1)
                v.wait_ge(norm.sem, norm.at(t, 2))
                hold(v, gate)
                v.bn_aggr(mv[:, p, :], stats[:, p, :]).then_inc(norm.sem, 1)
                v.wait_ge(norm.sem, norm.at(t, 3))
                v.tensor_scalar(veps[:, p, :], mv[:, p, 1:2], EPS, None, ALU.add).then_inc(norm.sem, 1)
                v.wait_ge(rstd_ready.sem, rstd_ready.at(t))
                v.wait_ge(xn_turned.sem, xn_turned.before(t))
                v.tensor_scalar(xn[:, p, :], x1[:, p, :], mv[:, p, 0:1], rstd[:, p, :],
                                ALU.subtract, ALU.mult).then_inc(norm.sem, 1)

            def top(t, p):
                v.wait_ge(routed.sem, routed.at(t))
                v.tensor_copy(lg_sb[:, bass.ds(t, 1), :].rearrange("q a e -> q (a e)"), ps_l[p][:, 0:GE]).then_inc(topped.sem, 1)
                for g in range(G):
                    v.max(val8[:, p, g, :], ps_l[p][:, g * E:(g + 1) * E]).then_inc(topped.sem, 1)
                v.wait_ge(topped.sem, topped.at(t, 1 + G))
                hold(v, gate)
                for g in range(G):
                    v.max_index(idx8[:, p, g, :], val8[:, p, g, :], ps_l[p][:, g * E:(g + 1) * E]).then_inc(topped.sem, 1)
                v.wait_ge(topped.sem, topped.at(t, 1 + 2 * G))
                v.tensor_copy(top_val[:, bass.ds(t, 1), :, :].rearrange("q a g k -> q (a g) k"), val8[:, p, :, 0:TOPK]).then_inc(topped.sem, 1)
                v.tensor_copy(top_idx[:, bass.ds(t, 1), :, :].rearrange("q a g k -> q (a g) k"), idx8[:, p, :, 0:TOPK]).then_inc(topped.sem, 1)
            staged(v, NT, normalise, top)


def phase_slots(nc, sems, xn_sb, lg_sb, top_val, top_idx, weight, pos, tile_expert, slots_x):
    TE = SLOT_TILES + 1
    with Phase(nc, "slots", sems) as ph:
        iota_e = ph.sb("iota_e", [P, E])
        iota_t = ph.sb("iota_t", [1, TE])
        idx_f = ph.sb("idx_f", [P, NT, G, TOPK])
        hot = [ph.sb(f"hot{r}", [P, NT, G, E]) for r in range(TOPK)]
        both = ph.sb("both", [P, NT, GE], BF16)
        before = ph.sb("before", [P, NT + 1, GE], BF16)
        tri = ph.sb("tri", [P, P], BF16)
        ones = ph.sb("ones", [P, P], BF16)
        work = ph.sb("work", [P, NT, G, E])
        gap = ph.sb("gap", [P, NT, G, TOPK])
        total = ph.sb("total", [P, NT, G, 1])
        inverse = ph.sb("inverse", [P, NT, G, 1])
        tiles_i = ph.sb("tiles_i", [P, GE], I32)
        tiles_f = ph.sb("tiles_f", [P, GE])
        ones_f = ph.sb("ones_f", [P, E])
        ends = ph.sb("ends", [P, GE])
        starts = ph.sb("starts", [P, G, E])
        pos_f = ph.sb("pos_f", [P, NT, G, TOPK])
        past = ph.sb("past", [1, TE, E])
        count_f = ph.sb("count_f", [1, G, TE])
        ps_w = [ph.ps(f"ps_w{i}", [P, 512]) for i in range(NT * GE // 512)]
        ps_n = ph.ps("ps_n", [P, 512])

        made = ph.sem("made")
        step = ph.sem("step")
        exped = ph.sem("exped")
        counted = ph.sem("counted")
        scattered = ph.sem("scattered", soft=True)
        n = {}
        block = ph.block()

        @block.vector
        def _(v):
            done = [0]

            def did(ins, name=None):
                ins.then_inc(step, 1)
                done[0] += 1
                if name:
                    n[name] = done[0]

            def settle():
                v.wait_ge(step, done[0])

            did(v.memset(before[:, 0, :], 0.0))
            did(v.memset(ones_f[:, :], 1.0))
            did(v.tensor_tensor(work[:, :, :, :].rearrange("q t g e -> q (t g) e"),
                                lg_sb[:, :, :].rearrange("q t (g e) -> q (t g) e", g=G),
                                top_val[:, :, :, 0:1].rearrange("q t g k -> q (t g) k").to_broadcast([P, NT * G, E]),
                                ALU.subtract))
            did(v.tensor_tensor(gap[:, :, :, :].rearrange("q t g k -> q (t g) k"),
                                top_val[:, :, :, :].rearrange("q t g k -> q (t g) k"),
                                top_val[:, :, :, 0:1].rearrange("q t g k -> q (t g) k").to_broadcast([P, NT * G, TOPK]),
                                ALU.subtract), "shifted")
            v.wait_ge(made, 6)
            for r in range(TOPK):
                did(v.tensor_tensor(hot[r][:, :, :, :].rearrange("q t g e -> q (t g) e"),
                                    top_idx[:, :, :, r:r + 1].rearrange("q t g k -> q (t g) k").to_broadcast([P, NT * G, E]),
                                    iota_e[:, :].unsqueeze(1).to_broadcast([P, NT * G, E]), ALU.is_equal))
            settle()
            did(v.tensor_tensor(both[:, :, :], hot[0][:, :, :, :].rearrange("q t g e -> q t (g e)"),
                                hot[1][:, :, :, :].rearrange("q t g e -> q t (g e)"), ALU.add))
            for t in range(NT):
                settle()
                did(v.tensor_tensor(before[:, t + 1, :], before[:, t, :], both[:, t, :], ALU.add))
            n["before"] = done[0]
            v.wait_ge(exped, 2)
            did(v.tensor_reduce(total[:, :, :, :].rearrange("q t g a -> q (t g) a"),
                                work[:, :, :, :].rearrange("q t g e -> q (t g) e"), X, ALU.add))
            settle()
            did(v.reciprocal(inverse[:, :, :, :].rearrange("q t g a -> q (t g) a"),
                             total[:, :, :, :].rearrange("q t g a -> q (t g) a")))
            settle()
            did(v.tensor_scalar(inverse[:, :, :, :].rearrange("q t g a -> q (t g a)"),
                                inverse[:, :, :, :].rearrange("q t g a -> q (t g a)"), 1.0 / G, None, ALU.mult))
            settle()
            did(v.tensor_tensor(weight[:, :, :, :].rearrange("q t g k -> q (t g) k"),
                                gap[:, :, :, :].rearrange("q t g k -> q (t g) k"),
                                inverse[:, :, :, :].rearrange("q t g a -> q (t g) a").to_broadcast([P, NT * G, TOPK]),
                                ALU.mult))
            v.wait_ge(counted, 1)
            did(v.tensor_scalar(tiles_f[:, :], ps_n[:, 0:GE], float(P - 1), None, ALU.add))
            settle()
            did(v.tensor_copy(tiles_i[:, :], tiles_f[:, :]))
            settle()
            did(v.tensor_scalar(tiles_i[:, :], tiles_i[:, :], P.bit_length() - 1, None, ALU.logical_shift_right))
            settle()
            did(v.tensor_copy(tiles_f[:, :], tiles_i[:, :]))
            settle()
            for g in range(G):
                did(v.tensor_tensor_scan(ends[:, g * E:(g + 1) * E], ones_f[:, :], tiles_f[:, g * E:(g + 1) * E],
                                         0.0, ALU.mult, ALU.add))
            settle()
            did(v.tensor_tensor(starts[:, :, :].rearrange("q g e -> q (g e)"), ends[:, :], tiles_f[:, :], ALU.subtract))
            settle()
            for g in range(G):
                did(v.tensor_scalar(starts[:, g, :], starts[:, g, :], float(P), float(g * (SLOTS + P)), ALU.mult, ALU.add))
            for g in range(G):
                settle()
                did(v.tensor_tensor(past[:, :, :], ends[0:1, g * E:(g + 1) * E].unsqueeze(1).to_broadcast([1, TE, E]),
                                    iota_t[:, :].unsqueeze(2).to_broadcast([1, TE, E]), ALU.is_le))
                settle()
                did(v.tensor_reduce(count_f[:, g, :], past[:, :, :], X, ALU.add))
            settle()
            did(v.tensor_scalar(tile_expert[:, :, :], count_f[:, :, :], float(E - 1), None, ALU.min))
            NB = 512 // GE
            v.wait_ge(counted, 2)
            for i, ps in enumerate(ps_w):
                did(v.tensor_tensor(work[:, i * NB:(i + 1) * NB, :, :].rearrange("q t g e -> q t (g e)"),
                                    ps[:, :].rearrange("q (t e) -> q t e", t=NB),
                                    starts[:, :, :].rearrange("q g e -> q (g e)").unsqueeze(1).to_broadcast([P, NB, GE]),
                                    ALU.add))
            settle()
            for r in range(TOPK):
                did(v.tensor_tensor(hot[r][:, :, :, :].rearrange("q t g e -> q (t g e)"),
                                    hot[r][:, :, :, :].rearrange("q t g e -> q (t g e)"),
                                    work[:, :, :, :].rearrange("q t g e -> q (t g e)"), ALU.mult))
            settle()
            for r in range(TOPK):
                did(v.tensor_reduce(pos_f[:, :, :, r:r + 1].rearrange("q t g a -> q (t g) a"),
                                    hot[r][:, :, :, :].rearrange("q t g e -> q (t g) e"), X, ALU.add))
            settle()
            did(v.tensor_copy(pos[:, :, :, :], pos_f[:, :, :, :]), "pos")
            settle()

        @block.scalar
        def _(act):
            act.wait_ge(step, n["shifted"])
            nc.scalar.activation(work[:, :, :, :], work[:, :, :, :], ACT.Exp).then_inc(exped, 1)
            nc.scalar.activation(gap[:, :, :, :], gap[:, :, :, :], ACT.Exp).then_inc(exped, 1)

        @block.tensor
        def _(pe):
            pe.wait_ge(made, 6)
            pe.wait_ge(step, n["before"])
            pe.matmul(ps_n[:, 0:GE], ones[:, :], before[:, NT, :], start=True, stop=True).then_inc(counted, 1)
            NB = 512 // GE
            for i, ps in enumerate(ps_w):
                pe.matmul(ps[:, :], tri[:, :], both[:, i * NB:(i + 1) * NB, :].rearrange("q t e -> q (t e)"),
                          start=True, stop=False)
                mm = pe.matmul(ps[:, :], ones[:, :], before[:, i * NB:(i + 1) * NB, :].rearrange("q t e -> q (t e)"),
                               start=False, stop=True)
            mm.then_inc(counted, 1)

        @block.gpsimd
        def _(pool):
            pool.iota(iota_e[:, :], pattern=[[1, E]], base=0, channel_multiplier=0,
                      allow_small_or_imprecise_dtypes=True).then_inc(made, 1)
            pool.iota(iota_t[:, :], pattern=[[1, TE]], base=0, channel_multiplier=0,
                      allow_small_or_imprecise_dtypes=True).then_inc(made, 1)
            pool.memset(ones[:, :], 1.0).then_inc(made, 1)
            pool.memset(tri[:, :], 1.0).then_inc(made, 1)
            pool.wait_ge(made, 4)
            pool.affine_select(out=tri[:, :], in_=tri[:, :], compare_op=ALU.is_gt, fill=0.0, base=0,
                               pattern=[[1, P]], channel_multiplier=-1).then_inc(made, 1)
            pool.nop().then_inc(made, 1)
            pool.wait_ge(step, n["pos"])
            for t in range(NT):
                for g in range(G):
                    for r in range(TOPK):
                        pool.indirect_dma_start(out=slots_x, out_offset=bass.IndirectOffsetOnAxis(ap=pos[:, t, g, r:r + 1], axis=0),
                                                in_=xn_sb[:, t, :], in_offset=None).then_inc(scattered, 16)
            pool.wait_ge(scattered, 16 * NT * G * TOPK)


def zero_slots(nc, sp, zeros, slots_x, slots_y, zeroed):
    rows = slots_x.shape[0]
    view = slots_x.rearrange("(n p r) c -> n p (r c)", p=P, r=2)
    for n in range(rows // (2 * P)):
        sp.dma_start(view[n], zeros[:, 0:2 * D]).then_inc(zeroed, 16)
    for g in range(G):
        end = (g + 1) * (SLOTS + P)
        sp.dma_start(slots_y[end - P:end, :], zeros[:, 0:D]).then_inc(zeroed, 16)


ZEROINGS = G * (SLOTS + P) // (2 * P) + G


def load_gate_up(sp, w_gu, wg, wu, landed):
    for k in range(KD):
        for i, w in enumerate((wg, wu)):
            sp.dma_start(w_gu[:, k, :, i, :], w[:, k * P:(k + 1) * P, :].rearrange("e p h -> p e h")).then_inc(landed, 16)


def phase_experts(nc, sems, g, w_gu, w_d, weights, w_landed, slots_x, slots_y, tile_expert, ident):
    N = SLOT_TILES
    base = g * (SLOTS + P)
    with Phase(nc, f"experts{g}", sems) as ph:
        xs = ph.sb("xs", [P, 2, D])
        x_t = ph.sb("x_t", [P, 2, KD, P])
        gs = ph.sb("gs", [P, 2, HID])
        h = ph.sb("h", [P, 2, HID])
        h_t = ph.sb("h_t", [P, 2, P])
        y = ph.sb("y", [P, 2, D])
        ps_t = [ph.ps(f"ps_t{i}", [P, 512]) for i in range(2)]
        ps_g = [ph.ps(f"ps_g{i}", [P, 512]) for i in range(2)]
        ps_h = [ph.ps(f"ps_h{i}", [P, 512]) for i in range(2)]
        ps_y = [ph.ps(f"ps_y{i}", [P, 512]) for i in range(2)]

        gate = ph.sem("gate")
        down_landed = ph.sem("down_landed")
        x_landed = ph.transfers("x_landed")
        turned = ph.steps("turned")
        x_ready = ph.steps("x_ready")
        gated = ph.steps("gated")
        silu = ph.steps("silu")
        h_ready = ph.steps("h_ready")
        h_turned = ph.steps("h_turned")
        h_t_ready = ph.steps("h_t_ready")
        down = ph.steps("down")
        y_ready = ph.steps("y_ready")
        stored = ph.transfers("stored")
        block = ph.block()

        @block.sync
        def _(sp):
            x_landed.prime(sp)
            stored.prime(sp)
            wg, wu, wd = weights
            if g:
                load_gate_up(sp, w_gu, wg, wu, w_landed)
            sp.dma_start(w_d[:, :, :], wd.rearrange("e h d -> h e d")).then_inc(down_landed, 16)

            def load(t, p):
                sp.wait_ge(turned.sem, turned.before(t))
                hold(sp, gate)
                sp.dma_start(xs[:, p, :], slots_x[bass.ds(t * P + base, P), :]).then_inc(x_landed.sems[p], 32)

            def idle(t, p):
                pass

            def store(t, p):
                sp.wait_ge(y_ready.sem, y_ready.at(t))
                hold(sp, gate)
                sp.dma_start(slots_y[bass.ds(t * P + base, P), :], y[:, p, :]).then_inc(stored.sems[p], 32)
            staged(sp, N, load, idle, idle, idle, store)
            for t in (N - 2, N - 1):
                sp.wait_ge(stored.sems[t % 2], stored.at(t, t % 2))

        @block.tensor
        def _(pe):
            for s in (turned, gated, h_turned, down):
                s.prime(pe)
            pe.wait_ge(w_landed, 16 * 2 * KD)
            pe.wait_ge(down_landed, 16)

            def expert(t):
                return pe.value_load(tile_expert[0:1, g, bass.ds(t, 1)], min_val=0, max_val=E - 1)

            def turn_x(t, p):
                pe.wait_ge(x_landed.sems[p], x_landed.at(t, p))
                for k in range(KD):
                    mm = pe.transpose(ps_t[p][:, k * P:(k + 1) * P], xs[:, p, k * P:(k + 1) * P], ident[:, :])
                mm.then_inc(turned.sem, 1)

            def gate_up(t, p):
                e = expert(t)
                pe.wait_ge(x_ready.sem, x_ready.at(t))
                for k in range(KD):
                    mm = pe.matmul(ps_g[p][:, 0:2 * HID], x_t[:, p, k, :],
                                   w_gu[:, k, bass.ds(e, 1), :, :].rearrange("q a i h -> q (a i h)"),
                                   start=(k == 0), stop=(k == KD - 1))
                mm.then_inc(gated.sem, 1)

            def turn_h(t, p):
                pe.wait_ge(h_ready.sem, h_ready.at(t))
                pe.transpose(ps_h[p][:, 0:P], h[:, p, :], ident[:, :]).then_inc(h_turned.sem, 1)

            def go_down(t, p):
                e = expert(t)
                pe.wait_ge(h_t_ready.sem, h_t_ready.at(t))
                pe.wait_ge(y_ready.sem, y_ready.before(t))
                pe.matmul(ps_y[p][:, 0:D], h_t[:, p, :], w_d[:, bass.ds(e, 1), :].rearrange("q a c -> q (a c)"),
                          start=True, stop=True).then_inc(down.sem, 1)
            staged(pe, N, turn_x, gate_up, turn_h, go_down)

        @block.scalar
        def _(act):
            for s in (x_ready, silu, y_ready):
                s.prime(act)

            def keep_x(t, p):
                act.wait_ge(turned.sem, turned.at(t))
                nc.scalar.copy(x_t[:, p, :, :].rearrange("q k n -> q (k n)"), ps_t[p][:, 0:D]).then_inc(x_ready.sem, 1)

            def activate(t, p):
                act.wait_ge(gated.sem, gated.at(t))
                nc.scalar.activation(gs[:, p, :], ps_g[p][:, 0:HID], ACT.Silu).then_inc(silu.sem, 1)

            def idle(t, p):
                pass

            def keep_y(t, p):
                act.wait_ge(down.sem, down.at(t))
                act.wait_ge(stored.sems[p], stored.before(t, p))
                nc.scalar.copy(y[:, p, :], ps_y[p][:, 0:D]).then_inc(y_ready.sem, 1)
            staged(act, N, keep_x, activate, idle, keep_y)

        @block.vector
        def _(v):
            for s in (h_ready, h_t_ready):
                s.prime(v)

            def multiply(t, p):
                v.wait_ge(silu.sem, silu.at(t))
                v.tensor_tensor(h[:, p, :], gs[:, p, :], ps_g[p][:, HID:2 * HID], ALU.mult).then_inc(h_ready.sem, 1)

            def keep_h(t, p):
                v.wait_ge(h_turned.sem, h_turned.at(t))
                v.tensor_copy(h_t[:, p, :], ps_h[p][:, 0:P]).then_inc(h_t_ready.sem, 1)
            staged(v, N, multiply, keep_h)


GN = 8
NBK = S // GN
PW = 3 * D + 2 * H


def phase_combine(nc, sems, x1_sb, z_sb, weight, pos, slots_y, w_qkv, w_bg, ln_g, ln_b, proj, ident):
    HALVES = ((0, 512), (512, PW))
    with Phase(nc, "comb", sems) as ph:
        w_in = ph.sb("w_in", [P, KD, PW])
        w_s = ph.sb("w_s", [P, KD, PW])
        g_col = ph.sb("g_col", [P, KD])
        b_col = ph.sb("b_col", [P, KD])
        b_wide = ph.sb("b_wide", [P, KD, P])
        bias = ph.sb("bias", [P, PW])
        y_in = ph.sb("y_in", [P, 2, G * TOPK, D])
        w_c = ph.sb("w_c", [P, 2, G * TOPK])
        part = ph.sb("part", [P, 2, D])
        x2 = ph.sb("x2", [P, 2, D])
        z = ph.sb("z", [P, 2, D])
        hn = ph.sb("hn", [P, 2, D])
        stats = ph.sb("stats", [P, 2, 2, 6])
        mv = ph.sb("mv", [P, 2, 2, 2])
        veps = ph.sb("veps", [P, 2, 2])
        rstd = ph.sb("rstd", [P, 2, 2])
        neg_half = ph.sb("neg_half", [P, 1])
        half = ph.sb("half", [P, H])
        h_t = ph.sb("h_t", [P, 2, KD, P])
        pr = ph.sb("pr", [P, 2, PW])
        sq = ph.sb("sq", [P, 2, D])
        norm2 = ph.sb("norm2", [P, 2, H])
        length = ph.sb("length", [P, 2, H])
        inv_len = ph.sb("inv_len", [P, 2, H])
        ps_t = [ph.ps(f"ps_t{i}", [P, 512]) for i in range(2)]
        ps_p = [ph.ps(f"ps_p{i}", [P, 1024]) for i in range(2)]

        gate = ph.sem("gate")
        consts_in = ph.sem("consts_in")
        set_up = ph.sem("set_up")
        scaled = ph.sem("scaled")
        biased = ph.sem("biased")
        bias_kept = ph.sem("bias_kept")
        y_landed = ph.transfers("y_landed", G * TOPK, soft=True)
        weights_at = ph.steps("weights_at")
        x1_at = ph.steps("x1_at")
        added = ph.steps("added", G * TOPK)
        norm = ph.steps("norm", 8)
        roots = ph.steps("roots", 2)
        kept = ph.steps("kept", 2)
        turned = ph.steps("turned")
        h_ready = ph.steps("h_ready")
        projected = ph.steps("projected")
        proj_kept = ph.steps("proj_kept")
        squared = ph.steps("squared", 2)
        k_done = ph.steps("k_done", 4)
        sigmoid = ph.steps("sigmoid")
        stored = ph.transfers("stored")
        block = ph.block()

        @block.sync
        def _(sp):
            stored.prime(sp)
            for i, w in enumerate(w_qkv):
                sp.dma_start(w_in[:, :, i * D:(i + 1) * D], w.rearrange("(k p) c -> p k c", p=P)).then_inc(consts_in, 16)
            for i, w in enumerate(w_bg):
                sp.dma_start(w_in[:, :, 3 * D + i * H:3 * D + (i + 1) * H], w.rearrange("(k p) c -> p k c", p=P)).then_inc(consts_in, 16)
            with nc.allow_non_contiguous_dma("two short columns"):
                sp.dma_start(g_col[:, :], ln_g.rearrange("(k p) -> p k", p=P)).then_inc(consts_in, 16)
                sp.dma_start(b_col[:, :], ln_b.rearrange("(k p) -> p k", p=P)).then_inc(consts_in, 16)

            def store(t, p):
                sp.wait_ge(k_done.sem, k_done.at(t))
                hold(sp, gate)
                sp.wait_ge(sigmoid.sem, sigmoid.at(t))
                sp.dma_start(proj[bass.ds(t * P, P), :], pr[:, p, :]).then_inc(stored.sems[p], 32)
            staged(sp, NT, store)
            for t in (NT - 2, NT - 1):
                sp.wait_ge(stored.sems[t % 2], stored.at(t, t % 2))

        @block.gpsimd
        def _(pool):
            for s in (roots, squared):
                s.prime(pool)
            pool.memset(neg_half[:, :], -0.5).then_inc(set_up, 1)
            pool.memset(half[:, :], 0.5).then_inc(set_up, 1)
            pool.wait_ge(set_up, 2)

            def fetch(t):
                p = t % 2
                pool.wait_ge(added.sem, added.before(t))
                hold(pool, gate)
                for i in range(G * TOPK):
                    pool.indirect_dma_start(
                        out=y_in[:, p, i, :], out_offset=None, in_=slots_y,
                        in_offset=bass.IndirectOffsetOnAxis(ap=pos[:, t, i // TOPK, i % TOPK:i % TOPK + 1], axis=0)).then_inc(y_landed.sems[p], 32)

            def root(t, i):
                pool.wait_ge(norm.sem, norm.at(t, 3 + 4 * i))
                pool.tensor_tensor(rstd[:, t % 2, i:i + 1], veps[:, t % 2, i:i + 1], neg_half[:, :], ALU.pow).then_inc(roots.sem, 1)

            def lengths(t):
                p = t % 2
                pool.wait_ge(proj_kept.sem, proj_kept.at(t))
                pool.wait_ge(k_done.sem, k_done.before(t))
                pool.tensor_tensor(sq[:, p, :], pr[:, p, D:2 * D], pr[:, p, D:2 * D], ALU.mult).then_inc(squared.sem, 1)
                pool.wait_ge(k_done.sem, k_done.at(t, 1))
                pool.tensor_tensor(length[:, p, :], norm2[:, p, :], half[:, :], ALU.pow).then_inc(squared.sem, 1)

            fetch(0)
            for r in range(NT + 1):
                if r + 1 < NT:
                    fetch(r + 1)
                if r < NT:
                    root(r, 0)
                    root(r, 1)
                if r:
                    lengths(r - 1)

        @block.vector
        def _(v):
            for s in (added, norm, proj_kept, k_done):
                s.prime(v)
            v.wait_ge(consts_in, 16 * 7)
            for k in range(KD):
                v.tensor_scalar(w_s[:, k, :], w_in[:, k, :], g_col[:, k:k + 1], None, ALU.mult).then_inc(scaled, 1)
                v.tensor_copy(b_wide[:, k, :], b_col[:, k:k + 1].to_broadcast([P, P])).then_inc(scaled, 1)
            v.wait_ge(scaled, 2 * KD)
            v.tensor_scalar(w_s[:, :, 0:D], w_s[:, :, 0:D], float(HD) ** -0.5, None, ALU.mult).then_inc(scaled, 1)
            v.tensor_scalar(w_in[:, :, 0:D], w_in[:, :, 0:D], float(HD) ** -0.5, None, ALU.mult).then_inc(scaled, 1)
            v.wait_ge(biased, 1)
            for a, b in HALVES:
                v.tensor_copy(bias[:, a:b], ps_p[0][:, a:b]).then_inc(bias_kept, 1)
            v.wait_ge(bias_kept, 2)

            def combine(t, p):
                v.wait_ge(y_landed.sems[p], y_landed.at(t, p))
                v.wait_ge(weights_at.sem, weights_at.at(t))
                v.wait_ge(x1_at.sem, x1_at.at(t))
                v.wait_ge(kept.sem, kept.before(t))
                n = G * TOPK
                for i in range(n):
                    if i:
                        v.wait_ge(added.sem, added.at(t, i))
                    src = x2[:, p, :] if i % 2 == 0 else part[:, p, :]
                    dst = part[:, p, :] if i % 2 == 0 else x2[:, p, :]
                    v.scalar_tensor_tensor(dst, y_in[:, p, i, :], w_c[:, p, i:i + 1], src, ALU.mult, ALU.add).then_inc(added.sem, 1)
                v.wait_ge(added.sem, added.at(t))
                for i, (a, b) in enumerate(((x2, z), (z, hn))):
                    v.bn_stats(stats[:, p, i, :], a[:, p, :]).then_inc(norm.sem, 1)
                    v.wait_ge(norm.sem, norm.at(t, 4 * i + 1))
                    hold(v, gate)
                    v.bn_aggr(mv[:, p, i, :], stats[:, p, i, :]).then_inc(norm.sem, 1)
                    v.wait_ge(norm.sem, norm.at(t, 4 * i + 2))
                    v.tensor_scalar(veps[:, p, i:i + 1], mv[:, p, i, 1:2], EPS, None, ALU.add).then_inc(norm.sem, 1)
                    v.wait_ge(roots.sem, roots.at(t, i + 1))
                    v.tensor_scalar(b[:, p, :], a[:, p, :], mv[:, p, i, 0:1], rstd[:, p, i:i + 1],
                                    ALU.subtract, ALU.mult).then_inc(norm.sem, 1)
                    v.wait_ge(norm.sem, norm.at(t, 4 * i + 4))

            def finish(t, p):
                v.wait_ge(projected.sem, projected.at(t))
                v.wait_ge(stored.sems[p], stored.before(t, p))
                v.tensor_tensor(pr[:, p, :], ps_p[p][:, 0:PW], bias[:, :], ALU.add).then_inc(proj_kept.sem, 1)
                v.wait_ge(squared.sem, squared.at(t, 1))
                v.tensor_reduce(norm2[:, p, :], sq[:, p, :].rearrange("q (h d) -> q h d", h=H), X, ALU.add).then_inc(k_done.sem, 1)
                v.wait_ge(squared.sem, squared.at(t, 2))
                v.tensor_scalar(inv_len[:, p, :], length[:, p, :], 1e-6, None, ALU.add).then_inc(k_done.sem, 1)
                v.wait_ge(k_done.sem, k_done.at(t, 2))
                v.reciprocal(inv_len[:, p, :], inv_len[:, p, :]).then_inc(k_done.sem, 1)
                v.wait_ge(k_done.sem, k_done.at(t, 3))
                k = pr[:, p, D:2 * D].rearrange("q (h d) -> q h d", h=H)
                v.tensor_tensor(k, k, inv_len[:, p, :].unsqueeze(2).to_broadcast([P, H, HD]), ALU.mult).then_inc(k_done.sem, 1)
            staged(v, NT, combine, finish)

        @block.tensor
        def _(pe):
            for s in (turned, projected):
                s.prime(pe)
            pe.wait_ge(scaled, 2 * KD + 2)
            for a, b in HALVES:
                for k in range(KD):
                    mm = pe.matmul(ps_p[0][:, a:b], b_wide[:, k, :], w_in[:, k, a:b], start=(k == 0), stop=(k == KD - 1))
            mm.then_inc(biased, 1)
            pe.wait_ge(bias_kept, 2)

            def turn(t, p):
                pe.wait_ge(norm.sem, norm.at(t))
                for k in range(KD):
                    mm = pe.transpose(ps_t[p][:, k * P:(k + 1) * P], hn[:, p, k * P:(k + 1) * P], ident[:, :])
                mm.then_inc(turned.sem, 1)

            def project(t, p):
                pe.wait_ge(h_ready.sem, h_ready.at(t))
                pe.wait_ge(proj_kept.sem, proj_kept.before(t))
                for a, b in HALVES:
                    for k in range(KD):
                        mm = pe.matmul(ps_p[p][:, a:b], h_t[:, p, k, :], w_s[:, k, a:b], start=(k == 0), stop=(k == KD - 1))
                mm.then_inc(projected.sem, 1)
            staged(pe, NT, turn, project)

        @block.scalar
        def _(act):
            for s in (weights_at, x1_at, kept, h_ready, sigmoid):
                s.prime(act)

            def fetch(t, p):
                act.wait_ge(added.sem, added.before(t))
                act.wait_ge(kept.sem, kept.before(t))
                hold(act, gate)
                nc.scalar.copy(w_c[:, p, :], weight[:, bass.ds(t, 1), :, :].rearrange("q a g k -> q (a g k)")).then_inc(weights_at.sem, 1)
                act.wait_ge(norm.sem, norm.before(t))
                hold(act, gate)
                nc.scalar.copy(x2[:, p, :], x1_sb[:, bass.ds(t, 1), :].rearrange("q a c -> q (a c)")).then_inc(x1_at.sem, 1)

            def keep(t, p):
                act.wait_ge(norm.sem, norm.at(t))
                hold(act, gate)
                nc.scalar.copy(x1_sb[:, bass.ds(t, 1), :].rearrange("q a c -> q (a c)"), x2[:, p, :]).then_inc(kept.sem, 1)
                nc.scalar.copy(z_sb[:, bass.ds(t, 1), :].rearrange("q a c -> q (a c)"), z[:, p, :]).then_inc(kept.sem, 1)
                act.wait_ge(turned.sem, turned.at(t))
                nc.scalar.copy(h_t[:, p, :, :].rearrange("q k n -> q (k n)"), ps_t[p][:, 0:D]).then_inc(h_ready.sem, 1)

            def squash(t, p):
                act.wait_ge(proj_kept.sem, proj_kept.at(t))
                nc.scalar.activation(pr[:, p, 3 * D:PW], pr[:, p, 3 * D:PW], ACT.Sigmoid).then_inc(sigmoid.sem, 1)
            staged(act, NT, fetch, keep, squash)


VQ = 4
V4 = HD // VQ
HH = H // 2
HW = HH * HD
REC1 = 3 * GN * HD
REC2 = 2 * GN * V4 + 1
UW = GN * V4


def phase_blocks(nc, sems, proj, rec1, rec2):
    ROUNDS = 2 * T // (GN * P)
    with Phase(nc, "blocks", sems) as ph:
        raw = ph.sb("raw", [P, 2, GN, 3, HW])
        bg = ph.sb("bg", [P, 2, GN, 2, HH])
        decay = ph.sb("decay", [P, GN, GN, HH])
        neg_b = ph.sb("neg_b", [P, GN, HH])
        neg_bd = ph.sb("neg_bd", [P, GN, GN, HH])
        gam = ph.sb("gam", [P, GN, HH])
        b_gam = ph.sb("b_gam", [P, GN, HH])
        kk = ph.sb("kk", [P, GN, GN, HH])
        a_neg = ph.sb("a_neg", [P, GN, GN, HH])
        qk = ph.sb("qk", [P, GN, GN, HH])
        qd = ph.sb("qd", [P, GN, GN, HH])
        z = ph.sb("z", [P, GN, HH, 2, HD])
        total = ph.sb("total", [P, HH * 2 * HD])
        oq = ph.sb("oq", [P, GN, HH, 2, HD])
        dprod = ph.sb("dprod", [P, GN * 2 * HW])
        pprod = ph.sb("pprod", [P, 2, GN * 2 * HW])
        out1 = ph.sb("out1", [P, 2, HH, 3, GN, HD])
        out2 = ph.sb("out2", [P, 2, VQ, HH, REC2])

        gate = ph.sem("gate")
        cleared = ph.sem("cleared")
        landed = ph.transfers("landed", 5)
        decays = ph.steps("decays", GN + 3)
        kks = ph.steps("kks", 2 * (GN - 1) + 1)
        qks = ph.steps("qks", GN + 1)
        zs = ph.steps("zs", 3 * (GN - 1))
        oqs = ph.steps("oqs", GN)
        qk_prods = ph.steps("qk_prods", GN)
        rhs = ph.steps("rhs", 2)
        o_prods = ph.steps("o_prods", GN)
        kqs = ph.steps("kqs", 3)
        packed = ph.steps("packed", 2 + 2 * VQ)
        stored = ph.transfers("stored", 2)
        block = ph.block()

        @block.sync
        def _(sp):
            for s in (landed, stored):
                s.prime(sp)

            def load(r):
                p = r % 2
                sp.wait_ge(kqs.sem, kqs.before(r))
                rows = proj[r // 2 * GN * P:(r // 2 + 1) * GN * P, :].rearrange("(n t) c -> n t c", t=GN)
                for i in range(3):
                    sp.dma_start(raw[:, p, :, i, :], rows[:, :, i * D + p * HW:i * D + (p + 1) * HW]).then_inc(landed.sems[p], 32)
                for i in range(2):
                    c = 3 * D + i * H + p * HH
                    sp.dma_start(bg[:, p, :, i, :], rows[:, :, c:c + HH]).then_inc(landed.sems[p], 32)

            def store(r):
                p = r % 2
                sp.wait_ge(kqs.sem, kqs.at(r))
                sp.wait_ge(packed.sem, packed.at(r))
                b, first = r // 2 // (NBK // P), r // 2 % (NBK // P) * P
                sp.dma_start(rec1[first:first + P, b, p * HH:(p + 1) * HH, :],
                                            out1[:, p, :, :, :, :].rearrange("q h a t k -> q h (a t k)")).then_inc(stored.sems[p], 32)
                sp.dma_start(rec2[first:first + P, :, b, p * HH:(p + 1) * HH, :], out2[:, p, :, :, :]).then_inc(stored.sems[p], 32)
            load(0)
            for r in range(ROUNDS):
                if r + 1 < ROUNDS:
                    load(r + 1)
                store(r)
            for r in (ROUNDS - 2, ROUNDS - 1):
                sp.wait_ge(stored.sems[r % 2], stored.at(r, r % 2))

        @block.vector
        def _(v):
            for s in (decays, kks, qks, zs, oqs):
                s.prime(v)
            v.memset(decay[:, :, :, :], 0.0).then_inc(cleared, 1)
            v.memset(kk[:, :, :, :], 0.0).then_inc(cleared, 1)
            v.memset(qk[:, :, :, :], 0.0).then_inc(cleared, 1)
            v.wait_ge(cleared, 3)
            for t in range(GN):
                v.memset(decay[:, t, t, :], 1.0).then_inc(cleared, 1)
            v.wait_ge(cleared, 3 + GN)

            def one_round(r, p):
                k = raw[:, p, :, 1, :]
                beta, g = bg[:, p, :, 0, :], bg[:, p, :, 1, :]
                v.wait_ge(landed.sems[p], landed.at(r, p))
                v.wait_ge(kqs.sem, kqs.before(r, 1))
                v.wait_ge(packed.sem, packed.before(r, 1))
                for t in range(1, GN):
                    if t > 1:
                        v.wait_ge(decays.sem, decays.at(r, t - 1))
                    v.tensor_tensor(decay[:, t, 0:t, :], decay[:, t - 1, 0:t, :],
                                    g[:, t:t + 1, :].to_broadcast([P, t, HH]), ALU.mult).then_inc(decays.sem, 1)
                v.wait_ge(decays.sem, decays.at(r, GN - 1))
                v.tensor_tensor(gam[:, :, :], decay[:, :, 0, :], g[:, 0:1, :].to_broadcast([P, GN, HH]),
                                ALU.mult).then_inc(decays.sem, 1)
                v.wait_ge(decays.sem, decays.at(r, GN))
                v.tensor_tensor(b_gam[:, :, :], gam[:, :, :], beta, ALU.mult).then_inc(decays.sem, 1)
                v.tensor_scalar(neg_b[:, :, :], beta, -1.0, None, ALU.mult).then_inc(decays.sem, 1)
                v.wait_ge(decays.sem, decays.at(r, GN + 2))
                v.tensor_tensor(neg_bd[:, :, :, :], decay[:, :, :, :],
                                neg_b[:, :, :].unsqueeze(2).to_broadcast([P, GN, GN, HH]), ALU.mult).then_inc(decays.sem, 1)
                for t in range(1, GN):
                    if t > 1:
                        v.wait_ge(kks.sem, kks.at(r, 2 * (t - 1)))
                    prod = dprod[:, 0:t * HW].rearrange("q (i c) -> q i c", i=t)
                    v.tensor_tensor(prod, k[:, 0:t, :], k[:, t:t + 1, :].to_broadcast([P, t, HW]), ALU.mult).then_inc(kks.sem, 1)
                    v.wait_ge(kks.sem, kks.at(r, 2 * t - 1))
                    v.tensor_reduce(kk[:, t, 0:t, :], dprod[:, 0:t * HW].rearrange("q (i h d) -> q i h d", i=t, h=HH),
                                    X, ALU.add).then_inc(kks.sem, 1)
                v.wait_ge(decays.sem, decays.at(r))
                v.wait_ge(kks.sem, kks.at(r, 2 * (GN - 1)))
                v.tensor_tensor(a_neg[:, :, :, :], kk[:, :, :, :], neg_bd[:, :, :, :], ALU.mult).then_inc(kks.sem, 1)
                for t in range(GN):
                    v.wait_ge(qk_prods.sem, qk_prods.at(r, t + 1))
                    v.tensor_reduce(qk[:, t, 0:t + 1, :],
                                    pprod[:, t % 2, 0:(t + 1) * HW].rearrange("q (i h d) -> q i h d", i=t + 1, h=HH),
                                    X, ALU.add).then_inc(qks.sem, 1)
                v.wait_ge(qks.sem, qks.at(r, GN))
                v.tensor_tensor(qd[:, :, :, :], qk[:, :, :, :], decay[:, :, :, :], ALU.mult).then_inc(qks.sem, 1)

                def sum_outputs(t):
                    v.wait_ge(o_prods.sem, o_prods.at(r, t + 1))
                    v.tensor_reduce(oq[:, t, :, :, :].rearrange("q h a d -> q (h a d)"),
                                    pprod[:, t % 2, 0:(t + 1) * 2 * HW].rearrange("q (i c) -> q c i", i=t + 1),
                                    X, ALU.add).then_inc(oqs.sem, 1)
                v.wait_ge(rhs.sem, rhs.at(r))
                v.wait_ge(kks.sem, kks.at(r))
                for t in range(1, GN):
                    if t > 1:
                        v.wait_ge(zs.sem, zs.at(r, 3 * (t - 1)))
                    v.tensor_tensor(dprod[:, 0:t * 2 * HW].rearrange("q (i h c) -> q i h c", i=t, h=HH),
                                    z[:, 0:t, :, :, :].rearrange("q i h a d -> q i h (a d)"),
                                    a_neg[:, t, 0:t, :].unsqueeze(3).to_broadcast([P, t, HH, 2 * HD]),
                                    ALU.mult).then_inc(zs.sem, 1)
                    v.wait_ge(zs.sem, zs.at(r, 3 * t - 2))
                    v.tensor_reduce(total[:, :], dprod[:, 0:t * 2 * HW].rearrange("q (i c) -> q c i", i=t),
                                    X, ALU.add).then_inc(zs.sem, 1)
                    v.wait_ge(zs.sem, zs.at(r, 3 * t - 1))
                    row = z[:, t, :, :, :].rearrange("q h a d -> q (h a d)")
                    v.tensor_tensor(row, row, total[:, :], ALU.add).then_inc(zs.sem, 1)
                    if t > 1:
                        sum_outputs(t - 2)
                sum_outputs(GN - 2)
                sum_outputs(GN - 1)
            staged(v, ROUNDS, one_round)

        @block.gpsimd
        def _(pool):
            for s in (qk_prods, rhs, o_prods, kqs):
                s.prime(pool)

            def one_round(r, p):
                q, k, v_in = raw[:, p, :, 0, :], raw[:, p, :, 1, :], raw[:, p, :, 2, :]
                beta = bg[:, p, :, 0, :]
                pool.wait_ge(landed.sems[p], landed.at(r, p))

                def multiply_qk(t):
                    if t < 2:
                        pool.wait_ge(oqs.sem, oqs.before(r, 1))
                    else:
                        pool.wait_ge(qks.sem, qks.at(r, t - 1))
                    pool.tensor_tensor(pprod[:, t % 2, 0:(t + 1) * HW].rearrange("q (i c) -> q i c", i=t + 1),
                                       k[:, 0:t + 1, :], q[:, t:t + 1, :].to_broadcast([P, t + 1, HW]),
                                       ALU.mult).then_inc(qk_prods.sem, 1)

                def by_head(x):
                    return x.rearrange("q t (h d) -> q t h d", h=HH)

                def wide(x):
                    return x.unsqueeze(3).to_broadcast([P, GN, HH, HD])
                multiply_qk(0)
                multiply_qk(1)
                pool.wait_ge(packed.sem, packed.before(r, 1))
                pool.tensor_tensor(z[:, :, :, 0, :], by_head(v_in), wide(beta), ALU.mult).then_inc(rhs.sem, 1)
                pool.wait_ge(decays.sem, decays.at(r))
                pool.tensor_tensor(z[:, :, :, 1, :], by_head(k), wide(b_gam[:, :, :]), ALU.mult).then_inc(rhs.sem, 1)
                for t in range(2, GN):
                    multiply_qk(t)
                pool.wait_ge(stored.sems[p], stored.before(r, p))
                pool.tensor_tensor(out1[:, p, :, 1, :, :].rearrange("q h t d -> q t h d"), by_head(k),
                                   wide(decay[:, GN - 1, :, :]), ALU.mult).then_inc(kqs.sem, 1)
                q_out = out1[:, p, :, 2, :, :].rearrange("q h t d -> q t h d")
                pool.tensor_tensor(q_out, by_head(q), wide(gam[:, :, :]), ALU.mult).then_inc(kqs.sem, 1)
                pool.wait_ge(qks.sem, qks.at(r))
                pool.wait_ge(rhs.sem, rhs.at(r))
                for t in range(GN):
                    if t:
                        pool.wait_ge(zs.sem, zs.at(r, 3 * t))
                    if t > 1:
                        pool.wait_ge(oqs.sem, oqs.at(r, t - 1))
                    pool.tensor_tensor(pprod[:, t % 2, 0:(t + 1) * 2 * HW].rearrange("q (i h c) -> q i h c", i=t + 1, h=HH),
                                       z[:, 0:t + 1, :, :, :].rearrange("q i h a d -> q i h (a d)"),
                                       qd[:, t, 0:t + 1, :].unsqueeze(3).to_broadcast([P, t + 1, HH, 2 * HD]),
                                       ALU.mult).then_inc(o_prods.sem, 1)
                pool.wait_ge(oqs.sem, oqs.at(r))
                pool.wait_ge(kqs.sem, kqs.at(r, 2))
                pool.tensor_tensor(q_out, q_out, oq[:, :, :, 1, :], ALU.subtract).then_inc(kqs.sem, 1)
            staged(pool, ROUNDS, one_round)

        @block.scalar
        def _(act):
            packed.prime(act)

            def pack(r, p):
                act.wait_ge(stored.sems[p], stored.before(r, p))
                act.wait_ge(decays.sem, decays.at(r))
                nc.scalar.copy(out2[:, p, :, :, UW], gam[:, GN - 1:GN, :].to_broadcast([P, VQ, HH])).then_inc(packed.sem, 1)
                act.wait_ge(zs.sem, zs.at(r))
                act.wait_ge(rhs.sem, rhs.at(r))
                nc.scalar.mul(out1[:, p, :, 0, :, :], z[:, :, :, 1, :].rearrange("q t h d -> q h t d"), -1.0).then_inc(packed.sem, 1)
                for a, src in ((0, z), (1, oq)):
                    if a:
                        act.wait_ge(oqs.sem, oqs.at(r))
                    for w in range(VQ):
                        nc.scalar.copy(
                            out2[:, p, w, :, a * (UW + 1):a * (UW + 1) + UW].rearrange("q h (t v) -> q h t v", t=GN),
                            src[:, :, :, 0, w * V4:(w + 1) * V4].rearrange("q t h v -> q h t v")).then_inc(packed.sem, 1)
            staged(act, ROUNDS, pack)


CB = P // GN


def phase_chain(nc, sems, rec1, rec2, o_dram, ident):
    N = NBK // CB
    with Phase(nc, "chain", sems) as ph:
        r1 = ph.sb("r1", [P, 2, CB, 3, GN, HD])
        r2 = ph.sb("r2", [P, 2, CB, UW + 1])
        own = ph.sb("own", [P, 2, CB * GN, V4])
        state = ph.sb("state", [P, 2, V4, HD])
        terms1 = ph.sb("terms1", [P, 2, GN * V4, HD + 1])
        terms2 = ph.sb("terms2", [P, 2, GN + 1, V4 * HD])
        u = ph.sb("u", [P, GN, V4])
        terms3 = ph.sb("terms3", [P, 2, CB * GN, V4, HD])
        o_out = ph.sb("o_out", [P, 2, B, D])
        ps = [ph.ps(f"ps{i}", [P, 512]) for i in range(2)]

        gate = ph.sem("gate")
        cleared = ph.sem("cleared")
        landed = ph.transfers("landed", VQ + 2)
        chain = ph.steps("chain", 4 * CB)
        u_put = ph.steps("u_put", CB)
        decayed = ph.steps("decayed", CB)
        q_prods = ph.steps("q_prods", CB)
        summed = ph.steps("summed")
        o_ready = ph.steps("o_ready", B)
        stored = ph.transfers("stored", B)
        block = ph.block()

        @block.sync
        def _(sp):
            for s in (landed, stored):
                s.prime(sp)

            def load(t, p):
                sp.wait_ge(chain.sem, chain.before(t))
                hold(sp, gate)
                sp.wait_ge(summed.sem, summed.before(t))
                hold(sp, gate)
                rows = bass.ds(t * CB, CB)
                for w in range(VQ):
                    sp.dma_start(r1[w * B * H:(w + 1) * B * H, p, :, :, :, :].rearrange("q n a t k -> q n (a t k)"),
                                                rec1[rows, :, :, :].rearrange("n b h c -> (b h) n c")).then_inc(landed.sems[p], 32)
                sp.dma_start(r2[:, p, :, :], rec2[rows, :, :, :, 0:UW + 1].rearrange("n w b h c -> (w b h) n c")).then_inc(landed.sems[p], 32)
                sp.dma_start(own[:, p, :, :].rearrange("q (n t) v -> q n (t v)", n=CB),
                                            rec2[rows, :, :, :, UW + 1:REC2].rearrange("n w b h c -> (w b h) n c")).then_inc(landed.sems[p], 32)

            def idle(t, p):
                pass

            def store(t, p):
                sp.wait_ge(o_ready.sem, o_ready.at(t))
                hold(sp, gate)
                for b in range(B):
                    sp.dma_start(o_dram[bass.ds(t * P + b * S, P), :], o_out[:, p, b, :]).then_inc(stored.sems[p], 32)
            staged(sp, N, load, idle, store)
            for t in (N - 2, N - 1):
                sp.wait_ge(stored.sems[t % 2], stored.at(t, t % 2))

        @block.vector
        def _(v):
            chain.prime(v)
            v.memset(state[:, 0, :, :], 0.0).then_inc(cleared, 1)
            v.wait_ge(cleared, 1)

            def chunk(t, p):
                v.wait_ge(landed.sems[p], landed.at(t, p))
                for c in range(CB):
                    i = c % 2
                    if c:
                        v.wait_ge(chain.sem, chain.at(t, 4 * c))
                    else:
                        v.wait_ge(chain.sem, chain.before(t, 1))
                    before = state[:, i, :, :].unsqueeze(1).to_broadcast([P, GN, V4, HD])
                    v.tensor_tensor(terms1[:, i, :, 0:HD].rearrange("q (t v) k -> q t v k", t=GN), before,
                                    r1[:, p, c, 0, :, :].unsqueeze(2).to_broadcast([P, GN, V4, HD]),
                                    ALU.mult).then_inc(chain.sem, 1)
                    v.wait_ge(chain.sem, chain.at(t, 4 * c + 1))
                    v.wait_ge(u_put.sem, u_put.at(t, c + 1))
                    v.tensor_reduce(u[:, :, :].rearrange("q t v -> q (t v)"), terms1[:, i, :, :], X, ALU.add).then_inc(chain.sem, 1)
                    v.wait_ge(chain.sem, chain.at(t, 4 * c + 2))
                    v.tensor_tensor(terms2[:, i, 0:GN, :].rearrange("q t (v k) -> q t v k", v=V4),
                                    u[:, :, :].unsqueeze(3).to_broadcast([P, GN, V4, HD]),
                                    r1[:, p, c, 1, :, :].unsqueeze(2).to_broadcast([P, GN, V4, HD]),
                                    ALU.mult).then_inc(chain.sem, 1)
                    v.wait_ge(chain.sem, chain.at(t, 4 * c + 3))
                    v.wait_ge(decayed.sem, decayed.at(t, c + 1))
                    if c:
                        v.wait_ge(q_prods.sem, q_prods.at(t, c))
                    else:
                        v.wait_ge(q_prods.sem, q_prods.before(t, 1))
                    v.tensor_reduce(state[:, 1 - i, :, :].rearrange("q v k -> q (v k)"),
                                    terms2[:, i, :, :].rearrange("q t c -> q c t"), X, ALU.add).then_inc(chain.sem, 1)
            staged(v, N, chunk)

        @block.gpsimd
        def _(pool):
            q_prods.prime(pool)
            pool.wait_ge(cleared, 1)

            def chunk(t, p):
                pool.wait_ge(landed.sems[p], landed.at(t, p))
                pool.wait_ge(summed.sem, summed.before(t))
                for c in range(CB):
                    if c:
                        pool.wait_ge(chain.sem, chain.at(t, 4 * c))
                    else:
                        pool.wait_ge(chain.sem, chain.before(t, 1))
                    pool.tensor_tensor(terms3[:, p, c * GN:(c + 1) * GN, :, :],
                                       state[:, c % 2, :, :].unsqueeze(1).to_broadcast([P, GN, V4, HD]),
                                       r1[:, p, c, 2, :, :].unsqueeze(2).to_broadcast([P, GN, V4, HD]),
                                       ALU.mult).then_inc(q_prods.sem, 1)
            staged(pool, N, chunk)

        @block.tensor
        def _(pe):
            summed.prime(pe)

            def chunk(t, p):
                pe.wait_ge(q_prods.sem, q_prods.at(t))
                pe.wait_ge(o_ready.sem, o_ready.before(t))
                for j in range(V4):
                    out = ps[p][:, j * P:(j + 1) * P]
                    for k in range(HD):
                        pe.matmul(out, terms3[:, p, :, j, k], ident[:, :], start=(k == 0), stop=False)
                    mm = pe.matmul(out, own[:, p, :, j], ident[:, :], start=False, stop=True)
                mm.then_inc(summed.sem, 1)
            staged(pe, N, chunk)

        @block.scalar
        def _(act):
            for s in (u_put, decayed, o_ready):
                s.prime(act)
            act.wait_ge(cleared, 1)

            def chunk(t, p):
                act.wait_ge(landed.sems[p], landed.at(t, p))
                for c in range(CB):
                    i = c % 2
                    if c > 1:
                        act.wait_ge(chain.sem, chain.at(t, 4 * (c - 1) - 2))
                    elif c:
                        act.wait_ge(chain.sem, chain.at(t, 0))
                    else:
                        act.wait_ge(chain.sem, chain.before(t, 1))
                    nc.scalar.copy(terms1[:, i, :, HD], r2[:, p, c, 0:UW]).then_inc(u_put.sem, 1)
                    if c:
                        act.wait_ge(chain.sem, chain.at(t, 4 * c))
                    nc.scalar.activation(terms2[:, i, GN, :], state[:, i, :, :].rearrange("q v k -> q (v k)"), ACT.Copy,
                                         scale=r2[:, p, c, UW:UW + 1]).then_inc(decayed.sem, 1)

            def keep(t, p):
                act.wait_ge(summed.sem, summed.at(t))
                act.wait_ge(stored.sems[p], stored.before(t, p))
                for b in range(B):
                    nc.scalar.copy(o_out[:, p, b, :].rearrange("q (h w v) -> q h w v", h=H, w=VQ),
                                   ps[p][:, :].rearrange("q (v w b h) -> q b h w v", v=V4, w=VQ, b=B)[:, b]).then_inc(o_ready.sem, 1)
            staged(act, N, chunk, keep)


GT = 4
GP = GT * P
FB = 4 * D // P
LN = 3 * GT + 1


def flat(x):
    return x.rearrange("q a c -> q (a c)")


def layer_norm(v, t, steps, roots, src, dst, stats, mv, veps, rstd, gate):
    for i in range(GT):
        v.bn_stats(stats[:, i, :], src[:, i, :]).then_inc(steps.sem, 1)
    for i in range(GT):
        v.wait_ge(steps.sem, steps.at(t, i + 1))
        hold(v, gate)
        v.bn_aggr(mv[:, i, :], stats[:, i, :]).then_inc(steps.sem, 1)
    v.wait_ge(steps.sem, steps.at(t, 2 * GT))
    v.tensor_scalar(veps, mv[:, :, 1], EPS, None, ALU.add).then_inc(steps.sem, 1)
    v.wait_ge(roots.sem, roots.at(t))
    for i in range(GT):
        v.tensor_scalar(dst[:, i, :], src[:, i, :], mv[:, i, 0:1], rstd[:, i:i + 1],
                        ALU.subtract, ALU.mult).then_inc(steps.sem, 1)


def phase_mlp(nc, sems, o_dram, x_sb, z_sb, wo, bo, ln_g, ln_b, w1, b1, w2, b2, norm_g, norm_b, ident):
    N = NT // GT
    with Phase(nc, "mlp", sems) as ph:
        wo_sb = ph.sb("wo_sb", [P, KD, D])
        w1_sb = ph.sb("w1_sb", [P, KD, FB, P])
        w2_sb = ph.sb("w2_sb", [P, FB, D])
        g_col = ph.sb("g_col", [P, KD])
        b_col = ph.sb("b_col", [P, KD])
        b1_col = ph.sb("b1_col", [P, FB])
        rows = ph.sb("rows", [P, 4, D])
        neg_half = ph.sb("neg_half", [P, GT])
        o_in = ph.sb("o_in", [P, 2, GT, D])
        o_t = ph.sb("o_t", [P, 2, KD, GP])
        y = ph.sb("y", [P, 2, GT, D])
        base = ph.sb("base", [P, 2, GT, D])
        hn = ph.sb("hn", [P, 2, GT, D])
        h_t = ph.sb("h_t", [P, 2, KD, GP])
        hidden = ph.sb("hidden", [P, FB, GP])
        x3 = ph.sb("x3", [P, 2, GT, D])
        w = ph.sb("w", [P, 2, GT, D])
        xn = ph.sb("xn", [P, 2, GT, D])
        stats = ph.sb("stats", [P, 3, GT, 6])
        mv = ph.sb("mv", [P, 3, GT, 2])
        veps = ph.sb("veps", [P, 3, GT])
        rstd = ph.sb("rstd", [P, 3, GT])
        ps_ot = ph.ps("ps_ot", [P, GP])
        ps_ht = ph.ps("ps_ht", [P, GP])
        ps_y = ph.ps("ps_y", [P, GT, D])
        ps_1 = [ph.ps(f"ps_1{i}", [P, GP]) for i in range(2)]
        ps_2 = ph.ps("ps_2", [P, GT, D])

        gate = ph.sem("gate")
        consts_in = ph.sem("consts_in")
        set_up = ph.sem("set_up")
        shifted = ph.sem("shifted")
        b1_ready = ph.sem("b1_ready")
        scaled = ph.sem("scaled")
        o_landed = ph.transfers("o_landed")
        o_turned = ph.steps("o_turned", KD)
        o_kept = ph.steps("o_kept", KD)
        wo_done = ph.steps("wo_done")
        ys = ph.steps("ys", 2)
        bases = ph.steps("bases", 2)
        norm_h = ph.steps("norm_h", LN)
        norm_w = ph.steps("norm_w", LN)
        norm_x = ph.steps("norm_x", LN)
        root_h = ph.steps("root_h")
        root_w = ph.steps("root_w")
        root_x = ph.steps("root_x")
        h_turned = ph.steps("h_turned", KD)
        h_kept = ph.steps("h_kept", KD)
        up = ph.steps("up", FB)
        gelu = ph.steps("gelu", FB)
        down = ph.steps("down")
        x3s = ph.steps("x3s")
        x3_kept = ph.steps("x3_kept")
        affine = ph.steps("affine", 2)
        block = ph.block()

        @block.sync
        def _(sp):
            o_landed.prime(sp)
            sp.dma_start(w1_sb[:, :, :, :].rearrange("q k f c -> q k (f c)"), w1.rearrange("(k p) c -> p k c", p=P)).then_inc(consts_in, 16)
            sp.dma_start(wo_sb[:, :, :], wo.rearrange("(k p) c -> p k c", p=P)).then_inc(consts_in, 16)
            sp.dma_start(w2_sb[:, :, :], w2.rearrange("(f p) c -> p f c", p=P)).then_inc(consts_in, 16)
            for i, vec in enumerate((bo, b2, norm_g, norm_b)):
                sp.dma_start(rows[:, i, :], row_broadcast(vec)).then_inc(consts_in, 16)
            with nc.allow_non_contiguous_dma("short columns"):
                sp.dma_start(g_col[:, :], ln_g.rearrange("(k p) -> p k", p=P)).then_inc(consts_in, 16)
                sp.dma_start(b_col[:, :], ln_b.rearrange("(k p) -> p k", p=P)).then_inc(consts_in, 16)
                sp.dma_start(b1_col[:, :], b1.rearrange("(f p) -> p f", p=P)).then_inc(consts_in, 16)

            def load(t, p):
                sp.wait_ge(o_turned.sem, o_turned.before(t))
                hold(sp, gate)
                sp.dma_start(o_in[:, p, :, :], o_dram[bass.ds(t * GP, GP), :].rearrange("(n q) c -> q n c", q=P)).then_inc(o_landed.sems[p], 32)
            staged(sp, N, load)

        @block.tensor
        def _(pe):
            for s in (o_turned, wo_done, h_turned, up, down):
                s.prime(pe)
            pe.wait_ge(consts_in, 16 * 10)
            for f in range(FB):
                for k in range(KD):
                    mm = pe.matmul(ps_1[0][:, f:f + 1], w1_sb[:, k, f, :], b_col[:, k:k + 1], start=(k == 0), stop=(k == KD - 1))
            mm.then_inc(shifted, 1)
            pe.wait_ge(scaled, KD)

            def turn_o(t, p):
                pe.wait_ge(o_landed.sems[p], o_landed.at(t, p))
                for k in range(KD):
                    if k:
                        pe.wait_ge(o_kept.sem, o_kept.at(t, k))
                    else:
                        pe.wait_ge(o_kept.sem, o_kept.before(t, 1))
                    for i in range(GT):
                        mm = pe.transpose(ps_ot[:, i * P:(i + 1) * P], o_in[:, p, i, k * P:(k + 1) * P], ident[:, :])
                    mm.then_inc(o_turned.sem, 1)

            def project(t, p):
                pe.wait_ge(o_kept.sem, o_kept.at(t))
                pe.wait_ge(ys.sem, ys.before(t, 1))
                for i in range(GT):
                    for k in range(KD):
                        mm = pe.matmul(ps_y[:, i, :], o_t[:, p, k, i * P:(i + 1) * P], wo_sb[:, k, :], start=(k == 0), stop=(k == KD - 1))
                mm.then_inc(wo_done.sem, 1)

            def turn_h(t, p):
                pe.wait_ge(norm_h.sem, norm_h.at(t))
                for k in range(KD):
                    if k:
                        pe.wait_ge(h_kept.sem, h_kept.at(t, k))
                    else:
                        pe.wait_ge(h_kept.sem, h_kept.before(t, 1))
                    for i in range(GT):
                        mm = pe.transpose(ps_ht[:, i * P:(i + 1) * P], hn[:, p, i, k * P:(k + 1) * P], ident[:, :])
                    mm.then_inc(h_turned.sem, 1)

            def mlp(t, p):
                pe.wait_ge(h_kept.sem, h_kept.at(t))
                for f in range(FB):
                    if f > 1:
                        pe.wait_ge(gelu.sem, gelu.at(t, f - 1))
                    else:
                        pe.wait_ge(gelu.sem, gelu.before(t, 1))
                    for k in range(KD):
                        mm = pe.matmul(ps_1[f % 2][:, :], w1_sb[:, k, f, :], h_t[:, p, k, :], start=(k == 0), stop=(k == KD - 1))
                    mm.then_inc(up.sem, 1)
                pe.wait_ge(gelu.sem, gelu.at(t))
                pe.wait_ge(x3s.sem, x3s.before(t, 1))
                for i in range(GT):
                    for f in range(FB):
                        mm = pe.matmul(ps_2[:, i, :], hidden[:, f, i * P:(i + 1) * P], w2_sb[:, f, :], start=(f == 0), stop=(f == FB - 1))
                mm.then_inc(down.sem, 1)
            staged(pe, N, turn_o, project, turn_h, mlp)

        @block.scalar
        def _(act):
            for s in (o_kept, h_kept, gelu, x3_kept):
                s.prime(act)
            act.wait_ge(b1_ready, 1)

            def keep_o(t, p):
                act.wait_ge(wo_done.sem, wo_done.before(t))
                for k in range(KD):
                    act.wait_ge(o_turned.sem, o_turned.at(t, k + 1))
                    nc.scalar.copy(o_t[:, p, k, :], ps_ot[:, :]).then_inc(o_kept.sem, 1)

            def idle(t, p):
                pass

            def keep_h(t, p):
                act.wait_ge(up.sem, up.before(t))
                for k in range(KD):
                    act.wait_ge(h_turned.sem, h_turned.at(t, k + 1))
                    nc.scalar.copy(h_t[:, p, k, :], ps_ht[:, :]).then_inc(h_kept.sem, 1)

            def activate(t, p):
                act.wait_ge(down.sem, down.before(t, 1))
                for f in range(FB):
                    act.wait_ge(up.sem, up.at(t, f + 1))
                    nc.scalar.activation(hidden[:, f, :], ps_1[f % 2][:, :], ACT.Gelu, bias=b1_col[:, f:f + 1]).then_inc(gelu.sem, 1)

            def keep_x(t, p):
                act.wait_ge(x3s.sem, x3s.at(t))
                hold(act, gate)
                nc.scalar.copy(flat(x_sb[:, bass.ds(t * GT, GT), :]), flat(x3[:, p, :, :])).then_inc(x3_kept.sem, 1)
            staged(act, N, keep_o, idle, keep_h, activate, keep_x)

        @block.vector
        def _(v):
            for s in (ys, norm_h, norm_w, norm_x, x3s):
                s.prime(v)
            v.wait_ge(shifted, 1)
            v.tensor_tensor(b1_col[:, :], ps_1[0][:, 0:FB], b1_col[:, :], ALU.add).then_inc(b1_ready, 1)
            for k in range(KD):
                part = w1_sb[:, k, :, :].rearrange("q f c -> q (f c)")
                v.tensor_scalar(part, part, g_col[:, k:k + 1], None, ALU.mult).then_inc(scaled, 1)

            def idle(t, p):
                pass

            def first(t, p):
                v.wait_ge(wo_done.sem, wo_done.at(t))
                v.wait_ge(bases.sem, bases.before(t))
                hold(v, gate)
                v.tensor_tensor(flat(y[:, p, :, :]), flat(ps_y[:, :, :]), flat(z_sb[:, bass.ds(t * GT, GT), :]), ALU.add).then_inc(ys.sem, 1)
                v.wait_ge(ys.sem, ys.at(t, 1))
                v.tensor_tensor(y[:, p, :, :], y[:, p, :, :], rows[:, 0:1, :].to_broadcast([P, GT, D]), ALU.add).then_inc(ys.sem, 1)
                v.wait_ge(ys.sem, ys.at(t))
                v.wait_ge(h_turned.sem, h_turned.before(t))
                layer_norm(v, t, norm_h, root_h, y[:, p], hn[:, p], stats[:, 0], mv[:, 0], veps[:, 0, :], rstd[:, 0, :], gate)

            def last(t, p):
                v.wait_ge(down.sem, down.at(t))
                v.wait_ge(bases.sem, bases.at(t))
                v.wait_ge(x3_kept.sem, x3_kept.before(t))
                v.tensor_tensor(flat(x3[:, p, :, :]), flat(ps_2[:, :, :]), flat(base[:, p, :, :]), ALU.add).then_inc(x3s.sem, 1)
                v.wait_ge(x3s.sem, x3s.at(t))
                layer_norm(v, t, norm_w, root_w, x3[:, p], w[:, p], stats[:, 1], mv[:, 1], veps[:, 1, :], rstd[:, 1, :], gate)
                v.wait_ge(norm_w.sem, norm_w.at(t))
                v.wait_ge(affine.sem, affine.before(t))
                layer_norm(v, t, norm_x, root_x, w[:, p], xn[:, p], stats[:, 2], mv[:, 2], veps[:, 2, :], rstd[:, 2, :], gate)
            staged(v, N, idle, first, idle, last)

        @block.gpsimd
        def _(pool):
            for s in (bases, root_h, root_w, root_x, affine):
                s.prime(pool)
            pool.memset(neg_half[:, :], -0.5).then_inc(set_up, 1)
            pool.wait_ge(set_up, 1)
            pool.wait_ge(consts_in, 16 * 10)

            def root(t, i, norm, roots):
                pool.wait_ge(norm.sem, norm.at(t, 2 * GT + 1))
                pool.tensor_tensor(rstd[:, i, :], veps[:, i, :], neg_half[:, :], ALU.pow).then_inc(roots.sem, 1)

            def idle(t, p):
                pass

            def first(t, p):
                root(t, 0, norm_h, root_h)
                pool.wait_ge(ys.sem, ys.at(t))
                pool.wait_ge(x3s.sem, x3s.before(t))
                hold(pool, gate)
                pool.tensor_tensor(flat(base[:, p, :, :]), flat(y[:, p, :, :]), flat(x_sb[:, bass.ds(t * GT, GT), :]), ALU.add).then_inc(bases.sem, 1)
                pool.wait_ge(bases.sem, bases.at(t, 1))
                pool.tensor_tensor(base[:, p, :, :], base[:, p, :, :], rows[:, 1:2, :].to_broadcast([P, GT, D]), ALU.add).then_inc(bases.sem, 1)

            def last(t, p):
                root(t, 1, norm_w, root_w)
                root(t, 2, norm_x, root_x)
                pool.wait_ge(norm_x.sem, norm_x.at(t))
                pool.tensor_tensor(xn[:, p, :, :], xn[:, p, :, :], rows[:, 2:3, :].to_broadcast([P, GT, D]), ALU.mult).then_inc(affine.sem, 1)
                pool.wait_ge(affine.sem, affine.at(t, 1))
                hold(pool, gate)
                pool.tensor_tensor(z_sb[:, bass.ds(t * GT, GT), :], xn[:, p, :, :], rows[:, 3:4, :].to_broadcast([P, GT, D]), ALU.add).then_inc(affine.sem, 1)
            staged(pool, N, idle, first, idle, last)


SE = 16
SPE = 64
NS = SE * SPE
JT = NS // P
F = 512
FT = F // P


def phase_soft_turn(nc, sems, xf_sb, xf_t, slot_embeds, slot_g, slot_b, scale, bg, bu, se_t, bias_cols, ident):
    N = NT // GT
    with Phase(nc, "sturn", sems) as ph:
        xs = ph.sb("xs", [P, 2, GT, D])
        se = ph.sb("se", [P, 2, GT, D])
        sn = ph.sb("sn", [P, 2, GT, D])
        rows = ph.sb("rows", [P, 2, D])
        scale_col = ph.sb("scale_col", [P, 1])
        neg_half = ph.sb("neg_half", [P, GT])
        bias_rows = ph.sb("bias_rows", [P, P])
        stats = ph.sb("stats", [P, GT, 6])
        mv = ph.sb("mv", [P, GT, 2])
        veps = ph.sb("veps", [P, GT])
        rstd = ph.sb("rstd", [P, GT])
        ps = [ph.ps(f"ps{i}", [P, KD, GP]) for i in range(2)]
        ps_b = ph.ps("ps_b", [P, P])

        gate = ph.sem("gate")
        consts_in = ph.sem("consts_in")
        set_up = ph.sem("set_up")
        fetched = ph.steps("fetched")
        turned = ph.steps("turned")
        kept = ph.steps("kept", KD)
        norm = ph.steps("norm", LN)
        roots = ph.steps("roots")
        affine = ph.steps("affine", 2)
        scaled = ph.steps("scaled")
        biases = ph.sem("biases")
        block = ph.block()
        HALVES = JT // GT

        @block.sync
        def _(sp):
            sp.dma_start(se[:, :, :, :].rearrange("q a n c -> q (a n) c"),
                         slot_embeds.rearrange("e s d -> (e s) d").rearrange("(n p) c -> p n c", p=P)).then_inc(consts_in, 16)
            sp.dma_start(rows[:, 0, :], row_broadcast(slot_g)).then_inc(consts_in, 16)
            sp.dma_start(rows[:, 1, :], row_broadcast(slot_b)).then_inc(consts_in, 16)
            sp.dma_start(scale_col[:, :], row_broadcast(scale)).then_inc(consts_in, 16)
            for i, vec in enumerate((bg, bu)):
                sp.dma_start(bias_rows[i * SE * FT:(i + 1) * SE * FT, :], vec.rearrange("e (f p) -> (e f) p", p=P)).then_inc(consts_in, 16)

        @block.scalar
        def _(act):
            fetched.prime(act)

            def fetch(t, p):
                act.wait_ge(turned.sem, turned.before(t))
                hold(act, gate)
                nc.scalar.copy(flat(xs[:, p]), flat(xf_sb[:, bass.ds(t * GT, GT), :])).then_inc(fetched.sem, 1)
            staged(act, N, fetch)

        @block.tensor
        def _(pe):
            turned.prime(pe)

            def turn_from(src, t, p):
                pe.wait_ge(kept.sem, kept.before(t))
                for k in range(KD):
                    for i in range(GT):
                        mm = pe.transpose(ps[p][:, k, i * P:(i + 1) * P], src[:, i, k * P:(k + 1) * P], ident[:, :])
                mm.then_inc(turned.sem, 1)

            def turn(t, p):
                pe.wait_ge(fetched.sem, fetched.at(t))
                turn_from(xs[:, p], t, p)
            staged(pe, N, turn)
            for a in range(HALVES):
                pe.wait_ge(scaled.sem, scaled.at(a))
                turn_from(sn[:, a], N + a, a)
            pe.wait_ge(consts_in, 16 * 6)
            pe.transpose(ps_b[:, :], bias_rows[:, :], ident[:, :]).then_inc(biases, 1)

        @block.vector
        def _(v):
            for s in (kept, norm, scaled):
                s.prime(v)

            def keep(t, p):
                v.wait_ge(turned.sem, turned.at(t))
                for k in range(KD):
                    hold(v, gate)
                    v.tensor_copy(xf_t[:, k, bass.ds(t * GP, GP)], ps[p][:, k, :]).then_inc(kept.sem, 1)
            staged(v, N, keep)
            v.wait_ge(consts_in, 16 * 6)
            for a in range(HALVES):
                layer_norm(v, a, norm, roots, se[:, a], sn[:, a], stats, mv, veps[:, :], rstd, gate)
                v.wait_ge(norm.sem, norm.at(a))
            for a in range(HALVES):
                v.wait_ge(affine.sem, affine.at(a))
                v.tensor_scalar(sn[:, a], sn[:, a], scale_col[:, 0:1], None, ALU.mult).then_inc(scaled.sem, 1)
            for a in range(HALVES):
                v.wait_ge(turned.sem, turned.at(N + a))
                for k in range(KD):
                    v.tensor_copy(se_t[:, k, a * GP:(a + 1) * GP], ps[a][:, k, :]).then_inc(kept.sem, 1)
            v.wait_ge(biases, 1)
            v.tensor_copy(bias_cols.rearrange("q a e f -> q (a e f)"), ps_b[:, :]).then_inc(biases, 1)

        @block.gpsimd
        def _(pool):
            for s in (roots, affine):
                s.prime(pool)
            pool.memset(neg_half[:, :], -0.5).then_inc(set_up, 1)
            pool.wait_ge(set_up, 1)
            pool.wait_ge(consts_in, 16 * 6)
            for a in range(HALVES):
                pool.wait_ge(norm.sem, norm.at(a, 2 * GT + 1))
                pool.tensor_tensor(rstd[:, :], veps[:, :], neg_half[:, :], ALU.pow).then_inc(roots.sem, 1)
            for a in range(HALVES):
                pool.wait_ge(norm.sem, norm.at(a))
                pool.tensor_tensor(sn[:, a], sn[:, a], rows[:, 0:1, :].to_broadcast([P, GT, D]), ALU.mult).then_inc(affine.sem, 1)
                pool.wait_ge(affine.sem, affine.at(a, 1))
                pool.tensor_tensor(sn[:, a], sn[:, a], rows[:, 1:2, :].to_broadcast([P, GT, D]), ALU.add).then_inc(affine.sem, 1)


def spread_column(pe, out, wide, ident):
    return pe.matmul(out, wide, ident[:, :], start=True, stop=True)


def phase_slot_stats(nc, sems, xf_t, se_t, neg_max, inv_sum, ident):
    TB = S // GP
    with Phase(nc, "sstat", sems) as ph:
        lhs = ph.sb("lhs", [P, 2, KD, P])
        logit = ph.sb("logit", [P, 2, TB, GP])
        max_col = ph.sb("max_col", [P, 2, 1])
        neg_col = ph.sb("neg_col", [P, 2, 1])
        inv_col = ph.sb("inv_col", [P, 2, 1])
        total = ph.sb("total", [P, 2, 1])
        wide = ph.sb("wide", [P, 2, 2, P])
        ps = [ph.ps(f"ps{i}", [P, GP]) for i in range(TB)]
        ps_r = [ph.ps(f"ps_r{i}", [P, GP]) for i in range(2)]

        gate = ph.sem("gate")
        fetched = ph.steps("fetched")
        logits = ph.steps("logits", TB)
        kept = ph.steps("kept", TB)
        maxima = ph.steps("maxima", 2)
        sums = ph.steps("sums")
        inverted = ph.steps("inverted")
        widened = ph.steps("widened", 2)
        spread = ph.steps("spread")
        rows_kept = ph.steps("rows_kept", 2)
        block = ph.block()

        def idle(t, p):
            pass

        def per_sequence(eng, *stages):
            for b in range(B):
                staged(eng, JT, *[lambda t, p, s=s: s(t, p, b) for s in stages], first=b * JT)

        @block.tensor
        def _(pe):
            for s in (logits, spread):
                s.prime(pe)

            def multiply(t, p, b):
                pe.wait_ge(fetched.sem, fetched.at(t))
                for i in range(TB):
                    pe.wait_ge(kept.sem, kept.at(t, i + 1 - TB))
                    for k in range(KD):
                        c = b * S + i * GP
                        mm = pe.matmul(ps[i][:, :], lhs[:, p, k, :], xf_t[:, k, c:c + GP], start=(k == 0), stop=(k == KD - 1))
                    mm.then_inc(logits.sem, 1)

            def turn(t, p, b):
                pe.wait_ge(widened.sem, widened.at(t))
                pe.wait_ge(rows_kept.sem, rows_kept.before(t))
                for i in range(2):
                    mm = spread_column(pe, ps_r[p][:, i * P:(i + 1) * P], wide[:, p, i, :], ident)
                mm.then_inc(spread.sem, 1)
            per_sequence(pe, multiply, lambda t, p, b: None, turn)

        @block.gpsimd
        def _(pool):
            for s in (fetched, widened):
                s.prime(pool)

            def fetch(t, p, b):
                pool.wait_ge(logits.sem, logits.before(t))
                hold(pool, gate)
                pool.tensor_copy(lhs[:, p, :, :], se_t[:, :, bass.ds(t * P - b * NS, P)]).then_inc(fetched.sem, 1)

            def widen(t, p, b):
                pool.wait_ge(spread.sem, spread.before(t))
                pool.wait_ge(inverted.sem, inverted.at(t))
                hold(pool, gate)
                pool.tensor_copy(wide[:, p, 0, :], neg_col[:, p, :].to_broadcast([P, P])).then_inc(widened.sem, 1)
                pool.tensor_copy(wide[:, p, 1, :], inv_col[:, p, :].to_broadcast([P, P])).then_inc(widened.sem, 1)
            per_sequence(pool, fetch, widen)

        @block.vector
        def _(v):
            for s in (maxima, inverted):
                s.prime(v)

            def find_max(t, p, b):
                v.wait_ge(kept.sem, kept.at(t))
                hold(v, gate)
                v.tensor_reduce(max_col[:, p, :], logit[:, p, :, :].rearrange("q i c -> q (i c)"), X, ALU.max).then_inc(maxima.sem, 1)
                v.wait_ge(maxima.sem, maxima.at(t, 1))
                v.wait_ge(widened.sem, widened.before(t))
                v.tensor_scalar(neg_col[:, p, :], max_col[:, p, :], -1.0, None, ALU.mult).then_inc(maxima.sem, 1)

            def invert(t, p, b):
                v.wait_ge(sums.sem, sums.at(t))
                v.reciprocal(inv_col[:, p, :], total[:, p, :]).then_inc(inverted.sem, 1)
            per_sequence(v, find_max, invert)

        @block.scalar
        def _(act):
            for s in (kept, sums, rows_kept):
                s.prime(act)

            def keep(t, p, b):
                act.wait_ge(sums.sem, sums.before(t))
                for i in range(TB):
                    act.wait_ge(logits.sem, logits.at(t, i + 1))
                    nc.scalar.copy(logit[:, p, i, :], ps[i][:, :]).then_inc(kept.sem, 1)

            def add_up(t, p, b):
                act.wait_ge(maxima.sem, maxima.at(t))
                act.wait_ge(inverted.sem, inverted.before(t))
                act.wait_ge(kept.sem, kept.at(t))
                tile = logit[:, p, :, :].rearrange("q i c -> q (i c)")
                nc.scalar.activation(tile, tile, ACT.Exp,
                                     bias=neg_col[:, p, :], accum_out=total[:, p, :]).then_inc(sums.sem, 1)

            def keep_rows(t, p, b):
                act.wait_ge(spread.sem, spread.at(t))
                hold(act, gate)
                nc.scalar.copy(neg_max[:, bass.ds(t * P, P)], ps_r[p][:, 0:P]).then_inc(rows_kept.sem, 1)
                nc.scalar.copy(inv_sum[:, bass.ds(t * P, P)], ps_r[p][:, P:2 * P]).then_inc(rows_kept.sem, 1)
            per_sequence(act, keep, add_up, keep_rows)


def phase_dispatch(nc, sems, xf_sb, xf_t, se_t, neg_max, inv_sum, slots, token_neg_max, token_inv_sum):
    NB = NS // GP
    with Phase(nc, "disp", sems) as ph:
        lhs = ph.sb("lhs", [P, 2, KD, P])
        xs = ph.sb("xs", [P, 2, D])
        shifted = ph.sb("shifted", [P, 2, NS])
        probs = ph.sb("probs", [P, 2, NS])
        junk = ph.sb("junk", [P, NS])
        max_col = ph.sb("max_col", [P, 2, 1])
        neg_col = ph.sb("neg_col", [P, 2, 1])
        total = ph.sb("total", [P, 2, 1])
        ps_l = [ph.ps(f"ps_l{i}", [P, NS]) for i in range(2)]
        ps_s = ph.ps("ps_s", [P, KD, NS])

        gate = ph.sem("gate")
        fetched = ph.steps("fetched", 2)
        logits = ph.steps("logits")
        shifts = ph.steps("shifts")
        exps = ph.steps("exps")
        maxima = ph.steps("maxima", 3)
        sums = ph.steps("sums")
        inverted = ph.steps("inverted")
        added = ph.steps("added")
        slots_kept = ph.sem("slots_kept")
        block = ph.block()

        def per_sequence(eng, *stages):
            for b in range(B):
                staged(eng, ST, *[lambda t, p, s=s: s(t, p, b) for s in stages], first=b * ST)

        def idle(t, p, b):
            pass

        @block.gpsimd
        def _(pool):
            fetched.prime(pool)

            def fetch(t, p, b):
                pool.wait_ge(added.sem, added.before(t))
                hold(pool, gate)
                pool.tensor_copy(lhs[:, p, :, :], xf_t[:, :, bass.ds(t * P, P)]).then_inc(fetched.sem, 1)
                pool.tensor_copy(xs[:, p, :], flat(xf_sb[:, bass.ds(t, 1), :])).then_inc(fetched.sem, 1)
            per_sequence(pool, fetch)

        @block.tensor
        def _(pe):
            for s in (logits, added):
                s.prime(pe)

            def multiply(t, p, b):
                pe.wait_ge(fetched.sem, fetched.at(t))
                pe.wait_ge(shifts.sem, shifts.before(t))
                pe.wait_ge(sums.sem, sums.before(t))
                for n in range(NB):
                    for k in range(KD):
                        mm = pe.matmul(ps_l[p][:, n * GP:(n + 1) * GP], lhs[:, p, k, :], se_t[:, k, n * GP:(n + 1) * GP],
                                       start=(k == 0), stop=(k == KD - 1))
                mm.then_inc(logits.sem, 1)

            def add(t, p, b):
                first, last = [isinstance(t, int) and t == b * ST + n for n in (0, ST - 1)]
                pe.wait_ge(exps.sem, exps.at(t))
                if first and b:
                    pe.wait_ge(slots_kept, KD * b)
                for k in range(KD):
                    for n in range(NB):
                        mm = pe.matmul(ps_s[:, k, n * GP:(n + 1) * GP], xs[:, p, k * P:(k + 1) * P],
                                       probs[:, p, n * GP:(n + 1) * GP], start=first, stop=last)
                mm.then_inc(added.sem, 1)
            per_sequence(pe, multiply, add, idle)

        @block.vector
        def _(v):
            for s in (shifts, maxima, inverted):
                s.prime(v)

            def shift(t, p, b):
                v.wait_ge(logits.sem, logits.at(t))
                v.wait_ge(exps.sem, exps.before(t))
                v.tensor_tensor(shifted[:, p, :], ps_l[p][:, :], neg_max[:, b * NS:(b + 1) * NS], ALU.add).then_inc(shifts.sem, 1)
                v.tensor_reduce(max_col[:, p, :], ps_l[p][:, :], X, ALU.max).then_inc(maxima.sem, 1)
                v.wait_ge(maxima.sem, maxima.at(t, 1))
                v.wait_ge(sums.sem, sums.before(t))
                hold(v, gate)
                v.tensor_scalar(neg_col[:, p, :], max_col[:, p, :], -1.0, None, ALU.mult).then_inc(maxima.sem, 1)
                v.wait_ge(maxima.sem, maxima.at(t, 2))
                hold(v, gate)
                v.tensor_copy(token_neg_max[:, bass.ds(t, 1)], neg_col[:, p, :]).then_inc(maxima.sem, 1)

            def invert(t, p, b):
                v.wait_ge(sums.sem, sums.at(t))
                hold(v, gate)
                v.reciprocal(token_inv_sum[:, bass.ds(t, 1)], total[:, p, :]).then_inc(inverted.sem, 1)
            for b in range(B):
                staged(v, ST, *[lambda t, p, s=s: s(t, p, b) for s in (shift, invert)], first=b * ST)
                v.wait_ge(added.sem, added.at((b + 1) * ST - 1))
                for k in range(KD):
                    v.tensor_tensor(slots[:, k, :, b, :], ps_s[:, k, :].rearrange("q (e s) -> q e s", e=SE),
                                    inv_sum[:, b * NS:(b + 1) * NS].rearrange("q (e s) -> q e s", e=SE), ALU.mult).then_inc(slots_kept, 1)

        @block.scalar
        def _(act):
            for s in (exps, sums):
                s.prime(act)

            def exponent(t, p, b):
                act.wait_ge(shifts.sem, shifts.at(t))
                act.wait_ge(added.sem, added.before(t))
                nc.scalar.activation(probs[:, p, :], shifted[:, p, :], ACT.Exp).then_inc(exps.sem, 1)
                act.wait_ge(maxima.sem, maxima.at(t, 2))
                act.wait_ge(inverted.sem, inverted.before(t))
                act.wait_ge(sums.sem, sums.before(t, 1))
                nc.scalar.activation(junk[:, :], ps_l[p][:, :], ACT.Exp, bias=neg_col[:, p, :],
                                     accum_out=total[:, p, :]).then_inc(sums.sem, 1)
            per_sequence(act, exponent)


def phase_soft_experts(nc, sems, slots, bias_cols, wg, wu, wd, bd, slots_out):
    with Phase(nc, "sexp", sems) as ph:
        wg_sb = ph.sb("wg_sb", [P, 2, KD, F])
        wu_sb = ph.sb("wu_sb", [P, 2, KD, F])
        wd_sb = ph.sb("wd_sb", [P, 2, FT, D])
        bd_sb = ph.sb("bd_sb", [P, JT, D])
        cols = ph.sb("cols", [P, 2, 2, FT])
        gated = ph.sb("gated", [P, 2, FT, P])
        hidden = ph.sb("hidden", [P, 2, FT, P])
        ps_g = [ph.ps(f"ps_g{i}", [P, FT, P]) for i in range(2)]
        ps_u = [ph.ps(f"ps_u{i}", [P, FT, P]) for i in range(2)]
        ps_o = [ph.ps(f"ps_o{i}", [P, B, D]) for i in range(2)]

        gate = ph.sem("gate")
        bd_in = ph.sem("bd_in")
        landed = ph.transfers("landed", 3)
        fetched = ph.steps("fetched")
        up = ph.steps("up", 2)
        gelu = ph.steps("gelu", FT)
        hiddens = ph.steps("hiddens", FT)
        down = ph.steps("down")
        kept = ph.steps("kept", B)
        block = ph.block()

        @block.sync
        def _(sp):
            landed.prime(sp)

            def load(t, p):
                sp.wait_ge(down.sem, down.before(t))
                hold(sp, gate)
                for dst, src in ((wg_sb, wg), (wu_sb, wu), (wd_sb, wd)):
                    sp.dma_start(dst[:, p], src[bass.ds(t, 1), :, :].rearrange("a (k p) c -> p (a k) c", p=P)).then_inc(landed.sems[p], 32)
            for i in range(2):
                sp.dma_start(bd_sb[i * SPE:(i + 1) * SPE, :, :],
                             bd.rearrange("(j i) d -> i j d", i=2)[i:i + 1].to_broadcast([SPE, JT, D])).then_inc(bd_in, 16)
            staged(sp, SE, load)

        @block.gpsimd
        def _(pool):
            fetched.prime(pool)

            def fetch(t, p):
                pool.wait_ge(hiddens.sem, hiddens.before(t))
                hold(pool, gate)
                pool.tensor_copy(cols[:, p, :, :], bias_cols[:, :, bass.ds(t, 1), :].rearrange("q i a f -> q i (a f)")).then_inc(fetched.sem, 1)
            staged(pool, SE, fetch)

        @block.tensor
        def _(pe):
            for s in (up, down):
                s.prime(pe)

            def gate_up(t, p):
                pe.wait_ge(landed.sems[p], landed.at(t, p))
                pe.wait_ge(hiddens.sem, hiddens.before(t))
                for ps, w in ((ps_g, wg_sb), (ps_u, wu_sb)):
                    for f in range(FT):
                        for k in range(KD):
                            mm = pe.matmul(ps[p][:, f, :], w[:, p, k, f * P:(f + 1) * P],
                                           slots[:, k, bass.ds(t, 1), :, :].rearrange("q a b s -> q (a b s)"),
                                           start=(k == 0), stop=(k == KD - 1))
                    mm.then_inc(up.sem, 1)

            def go_down(t, p):
                pe.wait_ge(hiddens.sem, hiddens.at(t))
                pe.wait_ge(kept.sem, kept.before(t))
                for b in range(B):
                    for f in range(FT):
                        mm = pe.matmul(ps_o[p][p * SPE:(p + 1) * SPE, b, :], hidden[:, p, f, b * SPE:(b + 1) * SPE],
                                       wd_sb[:, p, f, :], start=(f == 0), stop=(f == FT - 1))
                mm.then_inc(down.sem, 1)
            staged(pe, SE, gate_up, go_down)

        @block.scalar
        def _(act):
            gelu.prime(act)

            def activate(t, p):
                act.wait_ge(fetched.sem, fetched.at(t))
                act.wait_ge(hiddens.sem, hiddens.before(t))
                for f in range(FT):
                    if f == 0:
                        act.wait_ge(up.sem, up.at(t, 1))
                    nc.scalar.activation(gated[:, p, f, :], ps_g[p][:, f, :], ACT.Gelu, bias=cols[:, p, 0, f:f + 1]).then_inc(gelu.sem, 1)
            staged(act, SE, activate)

        @block.vector
        def _(v):
            for s in (hiddens, kept):
                s.prime(v)
            v.wait_ge(bd_in, 32)

            def multiply(t, p):
                v.wait_ge(down.sem, down.before(t))
                v.wait_ge(up.sem, up.at(t))
                hold(v, gate)
                for f in range(FT):
                    v.wait_ge(gelu.sem, gelu.at(t, f + 1))
                    v.scalar_tensor_tensor(hidden[:, p, f, :], ps_u[p][:, f, :], cols[:, p, 1, f:f + 1], gated[:, p, f, :],
                                           ALU.add, ALU.mult).then_inc(hiddens.sem, 1)

            def keep(t, p):
                own = slice(p * SPE, (p + 1) * SPE)
                v.wait_ge(down.sem, down.at(t))
                for b in range(B):
                    hold(v, gate)
                    tile = bass.ds((t - p) * (D // 2), D)
                    v.tensor_tensor(slots_out[own, b].rearrange("q j d -> q (j d)")[:, tile], ps_o[p][own, b, :],
                                    bd_sb[own].rearrange("q j d -> q (j d)")[:, tile], ALU.add).then_inc(kept.sem, 1)
            staged(v, SE, multiply, keep)


def phase_soft_combine(nc, sems, x_sb, xf_t, se_t, slots_out, token_neg_max, token_inv_sum, out, ident):
    N = NT // GT
    with Phase(nc, "scomb", sems) as ph:
        wide = ph.sb("wide", [P, 2, GT, P])
        row = ph.sb("row", [P, 2, GP])
        inv = ph.sb("inv", [P, 2, GT])
        shifted = ph.sb("shifted", [P, 2, GP])
        probs = ph.sb("probs", [P, 2, JT, GP])
        res = ph.sb("res", [P, 2, GT, D])
        ps_r = ph.ps("ps_r", [P, GP])
        ps_l = [ph.ps(f"ps_l{i}", [P, GP]) for i in range(2)]
        ps_o = [ph.ps(f"ps_o{i}", [P, GP]) for i in range(2)]

        gate = ph.sem("gate")
        widened = ph.steps("widened")
        spread = ph.steps("spread")
        row_kept = ph.steps("row_kept")
        inv_kept = ph.steps("inv_kept")
        logits = ph.steps("logits", JT)
        shifts = ph.steps("shifts", JT)
        exps = ph.steps("exps", JT)
        mixed = ph.steps("mixed", GT)
        summed = ph.steps("summed", GT)
        stored = ph.transfers("stored")
        block = ph.block()

        def idle(t, p, b):
            pass

        def per_sequence(eng, *stages):
            for b in range(B):
                staged(eng, N // B, *[lambda t, p, s=s: s(t, p, b) for s in stages], first=b * (N // B))

        @block.sync
        def _(sp):
            stored.prime(sp)

            def store(t, p):
                sp.wait_ge(summed.sem, summed.at(t))
                hold(sp, gate)
                sp.dma_start(out[bass.ds(t * GP, GP), :].rearrange("(n q) c -> q n c", q=P), res[:, p, :, :]).then_inc(stored.sems[p], 32)
            staged(sp, N, store)
            for t in (N - 2, N - 1):
                sp.wait_ge(stored.sems[t % 2], stored.at(t, t % 2))

        @block.gpsimd
        def _(pool):
            widened.prime(pool)

            def widen(t, p):
                pool.wait_ge(spread.sem, spread.before(t))
                hold(pool, gate)
                pool.tensor_copy(wide[:, p, :, :], token_neg_max[:, bass.ds(t * GT, GT)].unsqueeze(2).to_broadcast([P, GT, P])).then_inc(widened.sem, 1)
            staged(pool, N, widen)

        @block.tensor
        def _(pe):
            for s in (spread, logits, mixed):
                s.prime(pe)

            def turn(t, p, b):
                pe.wait_ge(widened.sem, widened.at(t))
                pe.wait_ge(row_kept.sem, row_kept.before(t, 1))
                for i in range(GT):
                    mm = spread_column(pe, ps_r[:, i * P:(i + 1) * P], wide[:, p, i, :], ident)
                mm.then_inc(spread.sem, 1)

            def multiply(t, p, b):
                for j in range(JT):
                    pe.wait_ge(shifts.sem, shifts.at(t, j - 1))
                    for k in range(KD):
                        mm = pe.matmul(ps_l[j % 2][:, :], se_t[:, k, j * P:(j + 1) * P], xf_t[:, k, bass.ds(t * GP, GP)],
                                       start=(k == 0), stop=(k == KD - 1))
                    mm.then_inc(logits.sem, 1)

            def mix(t, p, b):
                pe.wait_ge(exps.sem, exps.at(t))
                for i in range(GT):
                    pe.wait_ge(summed.sem, summed.at(t, i - 1))
                    for j in range(JT):
                        mm = pe.matmul(ps_o[i % 2][:, 0:D], probs[:, p, j, i * P:(i + 1) * P], slots_out[:, b, j, :],
                                       start=(j == 0), stop=(j == JT - 1))
                    mm.then_inc(mixed.sem, 1)
            per_sequence(pe, turn, multiply, mix)

        @block.scalar
        def _(act):
            for s in (row_kept, inv_kept, exps):
                s.prime(act)

            def keep(t, p, b):
                act.wait_ge(spread.sem, spread.at(t))
                act.wait_ge(shifts.sem, shifts.before(t))
                nc.scalar.copy(row[:, p, :], ps_r[:, :]).then_inc(row_kept.sem, 1)

            def exponent(t, p, b):
                act.wait_ge(summed.sem, summed.before(t))
                hold(act, gate)
                nc.scalar.copy(inv[:, p, :], token_inv_sum[:, bass.ds(t * GT, GT)]).then_inc(inv_kept.sem, 1)
                act.wait_ge(mixed.sem, mixed.before(t))
                for j in range(JT):
                    act.wait_ge(shifts.sem, shifts.at(t, j + 1))
                    nc.scalar.activation(probs[:, p, j, :], shifted[:, j % 2, :], ACT.Exp).then_inc(exps.sem, 1)
            per_sequence(act, keep, exponent)

        @block.vector
        def _(v):
            for s in (shifts, summed):
                s.prime(v)

            def shift(t, p, b):
                v.wait_ge(row_kept.sem, row_kept.at(t))
                for j in range(JT):
                    v.wait_ge(logits.sem, logits.at(t, j + 1))
                    v.wait_ge(exps.sem, exps.at(t, j - 1))
                    v.tensor_tensor(shifted[:, j % 2, :], ps_l[j % 2][:, :], row[:, p, :], ALU.add).then_inc(shifts.sem, 1)

            def finish(t, p, b):
                v.wait_ge(stored.sems[p], stored.before(t, p))
                v.wait_ge(inv_kept.sem, inv_kept.at(t))
                for i in range(GT):
                    v.wait_ge(mixed.sem, mixed.at(t, i + 1))
                    hold(v, gate)
                    v.scalar_tensor_tensor(res[:, p, i, :], ps_o[i % 2][:, 0:D], inv[:, p, i:i + 1],
                                           flat(x_sb[:, bass.ds(t * GT + i, 1), :]), ALU.mult, ALU.add).then_inc(summed.sem, 1)
            per_sequence(v, shift, finish)


def two_layers(nc, t, out):
    scratch = {}
    for name, shape in (("slots_x", [G * (SLOTS + P), D]), ("slots_y", [G * (SLOTS + P), D]), ("proj", [T, PW]),
                        ("rec1", [NBK, B, H, REC1]), ("rec2", [NBK, VQ, B, H, REC2]), ("delta_out", [T, D])):
        scratch[name] = nc.dram_tensor(name, shape, F32, kind="Internal").ap()
    slots_x, slots_y, proj, rec1, rec2, delta_out = scratch.values()
    x = t["L0_attn_x"].rearrange("b s d -> (b s) d")
    soft = {name[7:]: ap for name, ap in t.items() if name.startswith("L1_ffn_")}

    def attn1(*names):
        return [t["L1_attn_" + n] for n in names]

    with ExitStack() as sems, ExitStack() as whole:
        def held(ctx, name, shape, dt=F32):
            return ctx.enter_context(nc.sbuf_tensor(name, shape, dt))

        set_up, zeroed = [sems.enter_context(nc.semaphore(n)) for n in ("set_up", "zeroed")]
        w_landed = [sems.enter_context(nc.semaphore(f"w_landed{g}")) for g in range(G)]
        ident = held(whole, "ident", [P, P])
        ident_bf = held(whole, "ident_bf", [P, P], BF16)
        zeros = held(whole, "zeros", [P, 2 * D])
        layer = sems.enter_context(Semaphores(nc, sems))
        with Phase(nc, "id", layer) as ph:
            identity(nc, ph, ident)
        with nc.Block() as block:
            @block.vector
            def _(v):
                v.tensor_copy(ident_bf[:, :], ident[:, :]).then_inc(set_up, 1)
                v.memset(zeros[:, :], 0.0).then_inc(set_up, 1)
                v.wait_ge(set_up, 2)

            @block.sync
            def _(sp):
                sp.wait_ge(set_up, 2)
                zero_slots(nc, sp, zeros, slots_x, slots_y, zeroed)

        z_sb = held(whole, "z_sb", [P, NT, D])
        with ExitStack() as ctx:
            qk_sb = held(ctx, "qk_sb", [P, NT, 2 * D])
            v_sb = held(ctx, "v_sb", [P, NT, D])
            phase_qkv(nc, layer, x, t["L0_attn_qkv_w"], t["L0_attn_qkv_b"], t["rope"], qk_sb, v_sb, ident)
            phase_attention(nc, layer, qk_sb, v_sb, z_sb, ident, ident_bf)
        x_sb = held(whole, "x_sb", [P, NT, D])
        weight = held(whole, "weight", [P, NT, G, TOPK])
        pos = held(whole, "pos", [P, NT, G, TOPK], U32)
        tile_expert = held(whole, "tile_expert", [1, G, SLOT_TILES + 1], U32)

        with ExitStack() as ctx:
            w_gu = held(ctx, "w_gu", [P, KD, E, 2, HID])
            experts = [[t[f"L0_ffn_{n}{g}"] for n in ("wg", "wu", "wd")] for g in range(G)]
            with nc.Block() as block:
                @block.sync
                def _(sp):
                    load_gate_up(sp, w_gu, *experts[0][:2], w_landed[0])
                    sp.wait_ge(zeroed, 16 * ZEROINGS)
            with ExitStack() as routed:
                lg_sb = held(routed, "lg_sb", [P, NT, GE])
                top_val = held(routed, "top_val", [P, NT, G, TOPK])
                top_idx = held(routed, "top_idx", [P, NT, G, TOPK])
                phase_route(nc, layer, x, z_sb, t["L0_attn_out_w"], t["L0_attn_out_b"],
                            [t[f"L0_ffn_router_w{g}"] for g in range(G)], x_sb, z_sb, lg_sb, top_val, top_idx, ident)
                phase_slots(nc, layer, z_sb, lg_sb, top_val, top_idx, weight, pos, tile_expert, slots_x)
            w_d = held(ctx, "w_d", [P, E, D])
            for g in range(G):
                phase_experts(nc, layer, g, w_gu, w_d, experts[g], w_landed[g],
                              slots_x, slots_y, tile_expert, ident)
        phase_combine(nc, layer, x_sb, z_sb, weight, pos, slots_y, attn1("Wq", "Wk", "Wv"), attn1("Wb", "Wg"),
                      *attn1("ln1_g", "ln1_b"), proj, ident)

        layer.clear()
        phase_blocks(nc, layer, proj, rec1, rec2)
        phase_chain(nc, layer, rec1, rec2, delta_out, ident)
        phase_mlp(nc, layer, delta_out, x_sb, z_sb, *attn1("Wo", "bo", "ln2_g", "ln2_b", "w1", "b1", "w2", "b2"),
                  soft["norm_g"], soft["norm_b"], ident)

        xf_t = held(whole, "xf_t", [P, KD, T])
        se_t = held(whole, "se_t", [P, KD, NS])
        bias_cols = held(whole, "bias_cols", [P, 2, SE, FT])
        token_neg_max = held(whole, "token_neg_max", [P, NT])
        token_inv_sum = held(whole, "token_inv_sum", [P, NT])
        slots = held(whole, "slots", [P, KD, SE, B, SPE])
        slots_out = held(whole, "slots_out", [P, B, JT, D])
        phase_soft_turn(nc, layer, z_sb, xf_t, soft["slot_embeds"], soft["slot_g"], soft["slot_b"], soft["scale"],
                        soft["bg"], soft["bu"], se_t, bias_cols[:, :, :, :], ident)
        with ExitStack() as ctx:
            neg_max = held(ctx, "neg_max", [P, B * NS])
            inv_sum = held(ctx, "inv_sum", [P, B * NS])
            phase_slot_stats(nc, layer, xf_t, se_t, neg_max, inv_sum, ident)
            phase_dispatch(nc, layer, z_sb, xf_t, se_t, neg_max, inv_sum, slots, token_neg_max, token_inv_sum)
        phase_soft_experts(nc, layer, slots, bias_cols, soft["Wg"], soft["Wu"], soft["Wd"], soft["bd"], slots_out)
        phase_soft_combine(nc, layer, x_sb, xf_t, se_t, slots_out, token_neg_max, token_inv_sum, out, ident)


def kernel(**inputs):
    import concourse.bacc as _bacc
    from concourse.bass_utils import run_bass_kernel_spmd as _run

    nc = _bacc.Bacc("TRN2", target_bir_lowering=False, num_devices=1)
    inputs["rope"] = rope_tables()
    arrays, tensors = {}, {}
    for name, a in inputs.items():
        arrays[f"in_{name}"] = np.ascontiguousarray(a)
        tensors[name] = nc.dram_tensor(f"in_{name}", arrays[f"in_{name}"].shape,
                                       mybir.dt.from_np(arrays[f"in_{name}"].dtype), kind="ExternalInput").ap()
    out = nc.dram_tensor("out", [T, D], F32, kind="ExternalOutput").ap()
    two_layers(nc, tensors, out)
    r = _run(nc, [arrays], core_ids=[0])
    return r.results[0]["out"].reshape(B, S, D)
```

```python
from contextlib import ExitStack

import numpy as np

import concourse.bass as bass
from concourse import mybir

F32 = mybir.dt.float32
BF16 = mybir.dt.bfloat16
I32 = mybir.dt.int32
U32 = mybir.dt.uint32
ALU = mybir.AluOpType
ACT = mybir.ActivationFunctionType
X = mybir.AxisListType.X

P = 128
D = 256
KD = D // P
B = 2
S = 2048
T = B * S
NT = T // P
ST = S // P
H = 16
HD = D // H
EPS = 1e-5


class Steps:

    def __init__(self, sem, per=1, ahead=2):
        self.sem, self.per, self.ahead = sem, per, ahead

    def prime(self, eng):
        eng.sem_inc(self.sem, self.per * self.ahead)

    def at(self, t, j=None):
        return t * self.per + (self.ahead * self.per + (self.per if j is None else j))

    def before(self, t, back=None):
        back = self.ahead if back is None else back
        return t * self.per + (self.ahead - back + 1) * self.per


class Transfers:

    def __init__(self, sems, per=1, soft=False):
        self.sems, self.per, self.primed, self.ring = sems, per, 0 if soft else 32, len(sems)

    def prime(self, eng):
        for s in self.sems:
            eng.sem_inc(s, 32 * self.per)

    def at(self, t, p):
        step = 32 // self.ring
        return t * (step * self.per) + (self.primed + 32 - step * p) * self.per

    def at_tile(self, t, p):
        return (t - p % GT) * (16 * self.per // GT) + (self.primed + 32 - 16 * (p // GT)) * self.per

    def before_tile(self, t, p):
        return (t - p % GT) * (16 * self.per // GT) + (32 - 16 * (p // GT)) * self.per

    def before(self, t, p):
        return t * (16 * self.per) + (32 - 16 * p) * self.per


def hold(eng, gate):
    eng.sem_inc(gate, 1)


def staged(eng, n, *stages, first=0, unroll=2):
    lag = len(stages) - 1

    def peeled(r):
        for s, stage in enumerate(stages):
            if 0 <= r - s < n:
                stage(first + r - s, (r - s) % unroll)

    passes = (n - lag) // unroll
    for r in range(lag):
        peeled(r)
    with eng.Fori(0, passes) as i:
        for r in range(lag, lag + unroll):
            for s, stage in enumerate(stages):
                stage(i * unroll + (first + r - s), (r - s) % unroll)
    for r in range(lag + unroll * passes, n + lag):
        peeled(r)


class Semaphores:

    def __init__(self, nc, lasting):
        self.nc, self.lasting, self.ctx, self.taken = nc, lasting, ExitStack(), []

    def __enter__(self):
        return self

    def __exit__(self, *a):
        return self.ctx.__exit__(*a)

    def take(self, name, soft=False):
        if soft:
            return self.lasting.enter_context(self.nc.semaphore(name))
        self.taken.append(self.ctx.enter_context(self.nc.semaphore(name)))
        return self.taken[-1]

    def clear(self):
        with self.nc.Block() as block:
            @block.sync
            def _(sp):
                for sem in self.taken:
                    sp.sem_clear(sem)
        self.ctx.close()
        self.taken = []


class Phase:

    def __init__(self, nc, name, sems):
        self.nc, self.name, self.sems, self.ctx = nc, name, sems, ExitStack()

    def __enter__(self):
        self.ctx.__enter__()
        return self

    def __exit__(self, *a):
        return self.ctx.__exit__(*a)

    def sb(self, name, shape, dt=F32):
        return self.ctx.enter_context(self.nc.sbuf_tensor(f"{self.name}_{name}", shape, dt))

    def ps(self, name, shape, dt=F32):
        return self.ctx.enter_context(self.nc.psum_tensor(f"{self.name}_{name}", shape, dt))

    def sem(self, name, soft=False):
        return self.sems.take(f"{self.name}_{name}", soft)

    def steps(self, name, per=1, ahead=2):
        return Steps(self.sem(name), per, ahead)

    def transfers(self, name, per=1, soft=False):
        return Transfers([self.sem(f"{name}{p}", soft) for p in range(2)], per, soft)

    def block(self):
        return self.ctx.enter_context(self.nc.Block())


def row_broadcast(vec, parts=P):
    return vec.rearrange("(a n) -> a n", a=1).to_broadcast([parts, vec.shape[0]])


def identity(nc, ph, ident):
    zeroed, made = ph.sem("ident_zeroed"), ph.sem("ident_made")
    with nc.Block() as block:
        @block.gpsimd
        def _(pool):
            pool.memset(ident[:, :], 0.0).then_inc(zeroed, 1)
            pool.wait_ge(zeroed, 1)
            pool.affine_select(out=ident[:, :], in_=ident[:, :], compare_op=ALU.not_equal, fill=1.0,
                               base=0, pattern=[[-1, P]], channel_multiplier=1).then_inc(made, 1)
            pool.wait_ge(made, 1)


GT = 4
GP = GT * P
LN = 3 * GT + 1


def flat(x):
    return x.rearrange("q a c -> q (a c)")


def layer_norm(v, t, steps, roots, src, dst, stats, mv, veps, rstd, gate):
    for i in range(GT):
        v.bn_stats(stats[:, i, :], src[:, i, :]).then_inc(steps.sem, 1)
    for i in range(GT):
        v.wait_ge(steps.sem, steps.at(t, i + 1))
        hold(v, gate)
        v.bn_aggr(mv[:, i, :], stats[:, i, :]).then_inc(steps.sem, 1)
    v.wait_ge(steps.sem, steps.at(t, 2 * GT))
    v.tensor_scalar(veps, mv[:, :, 1], EPS, None, ALU.add).then_inc(steps.sem, 1)
    v.wait_ge(roots.sem, roots.at(t))
    for i in range(GT):
        v.tensor_scalar(dst[:, i, :], src[:, i, :], mv[:, i, 0:1], rstd[:, i:i + 1],
                        ALU.subtract, ALU.mult).then_inc(steps.sem, 1)


def rope_tables():
    inv = (1.0 / np.float32(10000.0) ** (np.arange(0, HD, 2, dtype=np.float32) / np.float32(HD))).astype(np.float32)
    freqs = np.arange(S, dtype=np.float32)[:, None] * inv[None, :]
    emb = np.concatenate([np.sin(freqs), np.cos(freqs)], axis=-1).astype(np.float32)
    sin, cos = emb[:, ::2], emb[:, 1::2]
    lay = lambda a: a.reshape(ST, P, HD // 2).transpose(1, 0, 2)
    both = np.stack([lay(cos), lay(sin)], axis=1)
    return np.ascontiguousarray(np.concatenate([both, both], axis=2))


def phase_qkv(nc, sems, x, qkv_w, qkv_b, rope, qk_sb, v_sb, ident):
    C3 = 3 * D
    WC = C3 // P
    H2 = 2 * H
    HE = HD // 2
    N = NT // GT
    with Phase(nc, "qkv", sems) as ph:
        w_in = ph.sb("w_in", [P, WC, D])
        w_t = ph.sb("w_t", [P, KD, C3])
        bias = ph.sb("bias", [P, C3])
        rope_sb = ph.sb("rope", [P, 2, NT, HE])
        x_in = ph.sb("x_in", [P, 2, GT, D])
        stats = ph.sb("stats", [P, GT, 6])
        mv = ph.sb("mv", [P, GT, 2])
        veps = ph.sb("veps", [P, GT])
        rstd = ph.sb("rstd", [P, GT])
        neg_half = ph.sb("neg_half", [P, GT])
        xn = ph.sb("xn", [P, 2, GT, D])
        xn_t = ph.sb("xn_t", [P, KD, GP])
        qk_raw = ph.sb("qk_raw", [P, 2, GT, H2, HE, 2])
        prod = ph.sb("prod", [P, 4, GT, H2, HE])
        ps_t = [ph.ps(f"ps_t{k}", [P, GP]) for k in range(KD)]
        ps_q = [ph.ps(f"ps_q{i}", [P, 1024]) for i in range(2)]

        gate = ph.sem("gate")
        w_in_landed = ph.sem("w_in_landed")
        consts_in = ph.sem("consts_in")
        set_up = ph.sem("set_up")
        w_turned = ph.steps("w_turned")
        w_kept = ph.steps("w_kept")
        x_landed = ph.transfers("x_landed")
        norm = ph.steps("norm", LN)
        roots = ph.steps("roots")
        turned = ph.steps("turned", KD)
        xn_t_ready = ph.steps("xn_t_ready", KD)
        projected = ph.steps("projected", GT)
        biased = ph.steps("biased", 2 * GT)
        first_half = ph.steps("first_half", 3)
        second_half = ph.steps("second_half", 3)
        block = ph.block()

        @block.sync
        def _(sp):
            x_landed.prime(sp)
            sp.dma_start(w_in[:, :, :], qkv_w.rearrange("(c p) d -> p c d", p=P)).then_inc(w_in_landed, 16)
            sp.dma_start(bias[:, :], row_broadcast(qkv_b)).then_inc(consts_in, 16)
            sp.dma_start(rope_sb[:, :, :, :], rope).then_inc(consts_in, 16)

            def load(t, p):
                sp.wait_ge(norm.sem, norm.before(t))
                hold(sp, gate)
                sp.dma_start(x_in[:, p, :, :], x[bass.ds(t * GP, GP), :].rearrange("(n q) c -> q n c", q=P)).then_inc(x_landed.sems[p], 32)
            staged(sp, N, load)

        def rotary(t, which):
            return rope_sb[:, which, bass.ds(t * GT, GT), :].unsqueeze(2).to_broadcast([P, GT, H2, HE])

        @block.vector
        def _(v):
            norm.prime(v)
            biased.prime(v)
            first_half.prime(v)

            def normalise(t, p):
                v.wait_ge(x_landed.sems[p], x_landed.at(t, p))
                v.wait_ge(turned.sem, turned.before(t))
                hold(v, gate)
                layer_norm(v, t, norm, roots, x_in[:, p], xn[:, p], stats, mv, veps[:, :], rstd, gate)

            def rotate(t, p):
                v.wait_ge(consts_in, 32)
                v.wait_ge(second_half.sem, second_half.before(t))
                for i in range(GT):
                    v.wait_ge(projected.sem, projected.at(t, i + 1))
                    v.tensor_tensor(qk_raw[:, p, i, :, :, :].rearrange("q h d e -> q (h d e)"),
                                    ps_q[i % 2][:, 0:2 * D], bias[:, 0:2 * D], ALU.add).then_inc(biased.sem, 1)
                    v.tensor_tensor(flat(v_sb[:, bass.ds(t * GT + i, 1), :]), ps_q[i % 2][:, 2 * D:C3],
                                    bias[:, 2 * D:C3], ALU.add).then_inc(biased.sem, 1)
                v.wait_ge(biased.sem, biased.at(t))
                v.wait_ge(first_half.sem, first_half.before(t, 1))
                hold(v, gate)
                v.tensor_tensor(prod[:, 0, :, :, :], qk_raw[:, p, :, :, :, 0], rotary(t, 0), ALU.mult).then_inc(first_half.sem, 1)
                v.tensor_tensor(prod[:, 1, :, :, :], qk_raw[:, p, :, :, :, 1], rotary(t, 1), ALU.mult).then_inc(first_half.sem, 1)
                v.wait_ge(first_half.sem, first_half.at(t, 2))
                hold(v, gate)
                out = qk_sb[:, bass.ds(t * GT, GT), :].rearrange("q n (h e) -> q n h e", h=H2)
                v.tensor_tensor(out[:, :, :, 0:HE], prod[:, 0, :, :, :], prod[:, 1, :, :, :],
                                ALU.subtract).then_inc(first_half.sem, 1)
            staged(v, N, normalise, rotate)

        @block.gpsimd
        def _(pool):
            roots.prime(pool)
            second_half.prime(pool)
            pool.memset(neg_half[:, :], -0.5).then_inc(set_up, 1)
            pool.wait_ge(set_up, 1)
            pool.wait_ge(consts_in, 32)

            def root(t, p):
                pool.wait_ge(norm.sem, norm.at(t, 2 * GT + 1))
                pool.tensor_tensor(rstd[:, :], veps[:, :], neg_half[:, :], ALU.pow).then_inc(roots.sem, 1)

            def rotate(t, p):
                pool.wait_ge(biased.sem, biased.at(t))
                pool.wait_ge(second_half.sem, second_half.before(t, 1))
                hold(pool, gate)
                pool.tensor_tensor(prod[:, 2, :, :, :], qk_raw[:, p, :, :, :, 0], rotary(t, 1), ALU.mult).then_inc(second_half.sem, 1)
                pool.tensor_tensor(prod[:, 3, :, :, :], qk_raw[:, p, :, :, :, 1], rotary(t, 0), ALU.mult).then_inc(second_half.sem, 1)
                pool.wait_ge(second_half.sem, second_half.at(t, 2))
                hold(pool, gate)
                out = qk_sb[:, bass.ds(t * GT, GT), :].rearrange("q n (h e) -> q n h e", h=H2)
                pool.tensor_tensor(out[:, :, :, HE:HD], prod[:, 2, :, :, :], prod[:, 3, :, :, :],
                                   ALU.add).then_inc(second_half.sem, 1)
            staged(pool, N, root, rotate)

        @block.tensor
        def _(pe):
            w_turned.prime(pe)
            turned.prime(pe)
            projected.prime(pe)
            pe.wait_ge(w_in_landed, 16)
            for c in range(WC):
                pe.wait_ge(w_kept.sem, w_kept.before(c))
                for k in range(KD):
                    mm = pe.transpose(ps_t[c % 2][:, k * P:(k + 1) * P], w_in[:, c, k * P:(k + 1) * P], ident[:, :])
                mm.then_inc(w_turned.sem, 1)
            pe.wait_ge(w_kept.sem, w_kept.at(WC - 1))

            def turn_and_project(t, p):
                pe.wait_ge(norm.sem, norm.at(t))
                pe.wait_ge(xn_t_ready.sem, xn_t_ready.before(t, 1))
                for k in range(KD):
                    for i in range(GT):
                        mm = pe.transpose(ps_t[k][:, i * P:(i + 1) * P], xn[:, p, i, k * P:(k + 1) * P], ident[:, :])
                    mm.then_inc(turned.sem, 1)
                pe.wait_ge(xn_t_ready.sem, xn_t_ready.at(t))
                for i in range(GT):
                    pe.wait_ge(biased.sem, biased.at(t, 2 * i - 2))
                    for a, b in ((0, 512), (512, C3)):
                        for k in range(KD):
                            mm = pe.matmul(ps_q[i % 2][:, a:b], xn_t[:, k, i * P:(i + 1) * P], w_t[:, k, a:b],
                                           start=(k == 0), stop=(k == KD - 1))
                    mm.then_inc(projected.sem, 1)
            staged(pe, N, turn_and_project)

        @block.scalar
        def _(act):
            w_kept.prime(act)
            xn_t_ready.prime(act)
            for c in range(WC):
                act.wait_ge(w_turned.sem, w_turned.at(c))
                nc.scalar.copy(w_t[:, :, c * P:(c + 1) * P],
                               ps_t[c % 2][:, 0:D].rearrange("q (k n) -> q k n", k=KD)).then_inc(w_kept.sem, 1)

            def keep(t, p):
                act.wait_ge(projected.sem, projected.before(t, 1))
                for k in range(KD):
                    act.wait_ge(turned.sem, turned.at(t, k + 1))
                    nc.scalar.copy(xn_t[:, k, :], ps_t[k][:, :]).then_inc(xn_t_ready.sem, 1)
            staged(act, N, keep)


def phase_attention(nc, sems, qk_sb, v_sb, o_sb, ident, ident_bf):
    PARTS = 3
    PAIRS = 6 * HD
    ROWS = PAIRS + PARTS
    W = 512
    CH = S // W
    NH = 2
    GK = 4
    VW = 32
    STEPS = S // W * (ST // GK)
    GS = ST // GK
    WT = W // P
    TG = 1024 // P
    GR = ST // TG
    RING = 4
    SCALE = float(HD) ** -0.5
    LATE = 2
    SEEK = STEPS - LATE - 1
    share = [ST * CH * (j + 1) // SEEK for j in range(-1, SEEK)]
    plan = [[]] * LATE + [list(range(a, b)) for a, b in zip(share, share[1:])] + [[]]

    with Phase(nc, "att", sems) as ph:
        k_stack = ph.sb("k_stack", [P, 2, ST, ROWS], BF16)
        q_stack = ph.sb("q_stack", [P, 2, ST, PAIRS], BF16)
        rest = ph.sb("rest", [P, 2, ST, HD])
        k_t = ph.sb("k_t", [P, 2, S], BF16)
        q_t = ph.sb("q_t", [P, 2, S], BF16)
        prob = ph.sb("prob", [P, RING, 2, W])
        v_h = ph.sb("v_h", [P, 2, ST, VW])
        o_t = ph.sb("o_t", [P, W])
        o_sum = ph.sb("o_sum", [P, WT, HD + 1])
        maxes = ph.sb("maxes", [P, 2, ST, CH])
        neg_max = ph.sb("neg_max", [P, ST])
        max_rest = ph.sb("max_rest", [P, ST])
        max_parts = ph.sb("max_parts", [P, ST, 4], BF16)
        sums_inv = ph.sb("sums_inv", [P, WT, 1])
        ps_m = [ph.ps(f"ps_m{i}", [P, W]) for i in range(2)]
        ps_s = [ph.ps(f"ps_s{i}", [P, 2 * W]) for i in range(NH)]
        ps_o = ph.ps("ps_o", [P, W])
        ps_tro = ph.ps("ps_tr", [P, W])
        ps_tr = ps_tro[:, :].bitcast(BF16)

        set_up = ph.sem("set_up")
        split_k = ph.steps("split_k", 6)
        split_q = ph.steps("split_q", 6)
        v_copied = ph.steps("v_copied")
        gate = ph.sem("gate")
        turned = ph.steps("turned", 3 * GR)
        kept = ph.steps("kept", 3 * GR)
        max_scores = ph.steps("max_scores", ST * CH)
        reduced = ph.steps("reduced", ST * CH)
        max_split = ph.steps("max_split", 5)
        scores = ph.steps("scores", STEPS * NH)
        expd = ph.steps("expd", STEPS * NH)
        pv = ph.steps("pv", STEPS)
        o_kept = ph.steps("o_kept", CH)
        o_turned = ph.steps("o_turned", CH)
        o_out = ph.steps("o_out", 3 * CH)
        block = ph.block()

        def heads(eng, turn):
            with eng.Fori(0, H - 1) as h:
                turn(h * 2, h, 0, False)
                turn(h * 2 + 1, h, 1, False)
            turn(2 * H - 2, H - 1, 0, False)
            turn(2 * H - 1, H - 1, 1, True)

        @block.gpsimd
        def _(pool):
            split_k.prime(pool)
            split_q.prime(pool)
            v_copied.prime(pool)
            pool.wait_ge(set_up, 4)

            def split(n, h, p, last=False):
                tiles = slice(p * ST, (p + 1) * ST)
                k = qk_sb[:, tiles, bass.ds(h * HD + D, HD)]
                q = qk_sb[:, tiles, bass.ds(h * HD, HD)]
                ks = k_stack[:, p, :, 0:PAIRS].rearrange("q n (s e) -> q n s e", e=HD)
                qs = q_stack[:, p, :, :].rearrange("q n (s e) -> q n s e", e=HD)
                pool.wait_ge(turned.sem, turned.before(n))
                hold(pool, gate)
                pool.tensor_copy(ks[:, :, 0, :], k).then_inc(split_k.sem, 1)
                pool.tensor_copy(qs[:, :, 0, :], q).then_inc(split_q.sem, 1)
                pool.wait_ge(split_k.sem, split_k.at(n, 1))
                hold(pool, gate)
                pool.tensor_tensor(rest[:, 0, :, :], k, ks[:, :, 0, :], ALU.subtract).then_inc(split_k.sem, 1)
                pool.wait_ge(split_q.sem, split_q.at(n, 1))
                hold(pool, gate)
                pool.tensor_tensor(rest[:, 1, :, :], q, qs[:, :, 0, :], ALU.subtract).then_inc(split_q.sem, 1)
                pool.wait_ge(split_k.sem, split_k.at(n, 2))
                hold(pool, gate)
                pool.tensor_copy(ks[:, :, 2, :], rest[:, 0, :, :]).then_inc(split_k.sem, 1)
                pool.wait_ge(split_q.sem, split_q.at(n, 2))
                hold(pool, gate)
                pool.tensor_copy(qs[:, :, 1, :], rest[:, 1, :, :]).then_inc(split_q.sem, 1)
                pool.wait_ge(split_k.sem, split_k.at(n, 3))
                hold(pool, gate)
                pool.tensor_tensor(ks[:, :, 4, :], rest[:, 0, :, :], ks[:, :, 2, :], ALU.subtract).then_inc(split_k.sem, 1)
                pool.tensor_copy(ks[:, :, 1:6:4, :], ks[:, :, 0:1, :].to_broadcast([P, ST, 2, HD])).then_inc(split_k.sem, 1)
                pool.tensor_copy(ks[:, :, 3, :], ks[:, :, 2, :]).then_inc(split_k.sem, 1)
                pool.wait_ge(split_q.sem, split_q.at(n, 3))
                hold(pool, gate)
                pool.tensor_tensor(qs[:, :, 5, :], rest[:, 1, :, :], qs[:, :, 1, :], ALU.subtract).then_inc(split_q.sem, 1)
                pool.tensor_copy(qs[:, :, 2:4, :], qs[:, :, 0:2, :]).then_inc(split_q.sem, 1)
                pool.tensor_copy(qs[:, :, 4, :], qs[:, :, 0, :]).then_inc(split_q.sem, 1)
                pool.wait_ge(pv.sem, pv.before(n))
                hold(pool, gate)
                pool.tensor_copy(v_h[:, p, :, 0:HD], v_sb[:, tiles, bass.ds(h * HD, HD)]).then_inc(v_copied.sem, 1)
            heads(pool, split)

        @block.tensor
        def _(pe):
            turned.prime(pe)
            max_scores.prime(pe)
            scores.prime(pe)
            pv.prime(pe)
            o_turned.prime(pe)
            pe.wait_ge(set_up, 4)

            def turn_group(n, p, g, outs):
                kind, g0 = divmod(g, GR)
                if g == 0:
                    pe.wait_ge(split_k.sem, split_k.at(n))
                if g == GR:
                    pe.wait_ge(split_q.sem, split_q.at(n))
                if g == 2 * GR:
                    pe.wait_ge(max_split.sem, max_split.at(n))
                pe.wait_ge(kept.sem, kept.at(n, g))
                pe.wait_ge(o_out.sem, o_out.at(n - 1, 3 * outs))
                for j in range(TG):
                    tile = g0 * TG + j
                    if kind == 0:
                        mm = pe.transpose(ps_tr[0:ROWS, j * P:(j + 1) * P], k_stack[:, p, tile, :], ident_bf[:, :])
                    elif kind == 1:
                        mm = pe.transpose(ps_tr[0:PAIRS, j * P:(j + 1) * P], q_stack[:, p, tile, :], ident_bf[:, :])
                    else:
                        mm = pe.transpose(ps_tr[PAIRS:ROWS, j * P:(j + 1) * P], max_parts[:, tile, 0:PARTS], ident_bf[:, :])
                mm.then_inc(turned.sem, 1)

            def first_pass(n, p, i):
                tile, c = divmod(i, CH)
                if i == 0:
                    pe.wait_ge(kept.sem, kept.at(n, 2 * GR))
                pe.wait_ge(reduced.sem, reduced.at(n, i - 1))
                pe.matmul(ps_m[i % 2][:, :], q_t[0:PAIRS, p, tile * P:(tile + 1) * P],
                          k_t[0:PAIRS, p, c * W:(c + 1) * W], start=True, stop=True).then_inc(max_scores.sem, 1)

            def score(n, p, j, half):
                if j == 0 and half == 0:
                    pe.wait_ge(kept.sem, kept.at(n))
                chunk, group = divmod(j, GS)
                pe.wait_ge(expd.sem, expd.at(n, j * NH + half - NH + 1))
                for i in range(2):
                    tile = group * GK + half * 2 + i
                    mm = pe.matmul(ps_s[half][:, i * W:(i + 1) * W], k_t[0:ROWS, p, tile * P:(tile + 1) * P],
                                   q_t[0:ROWS, p, chunk * W:(chunk + 1) * W], start=True, stop=True)
                mm.then_inc(scores.sem, 1)

            def against_v(n, p, j, half):
                chunk, group = divmod(j, GS)
                if j == 0 and half == 0:
                    pe.wait_ge(v_copied.sem, v_copied.at(n))
                if group == 0 and half == 0:
                    pe.wait_ge(o_kept.sem, o_kept.at(n, chunk))
                pe.wait_ge(expd.sem, expd.at(n, j * NH + half + 1))
                for i in (2 * half, 2 * half + 1):
                    mm = pe.matmul(ps_o[i * VW:(i + 1) * VW, :], v_h[:, p, group * GK + i, :],
                                   prob[:, (j * NH + half) % RING, i % 2, :],
                                   start=(group == 0), stop=(group == GS - 1), skip_group_check=True)
                if half == NH - 1:
                    mm.then_inc(pv.sem, 1)

            def turn_output(n, chunk, groups):
                pe.wait_ge(o_kept.sem, o_kept.at(n, chunk + 1))
                pe.wait_ge(o_out.sem, o_out.at(n, 3 * chunk))
                pe.wait_ge(kept.sem, kept.at(n + 1, groups))
                for i in range(WT):
                    mm = pe.transpose(ps_tro[:, i * P:(i + 1) * P], o_t[:, i * P:(i + 1) * P], ident[:, :])
                mm.then_inc(o_turned.sem, 1)

            def turn(n, h, p, last):
                for j in range(STEPS):
                    def seek(quarter):
                        if not last:
                            n_j = len(plan[j])
                            for i in plan[j][n_j * quarter // 4:n_j * (quarter + 1) // 4]:
                                first_pass(n + 1, 1 - p, i)
                    for half in range(NH):
                        if not last and j < GR:
                            turn_group(n + 1, 1 - p, j * 2 + half, 0)
                        score(n, p, j, half)
                        seek(half)
                    if j % GS == 1 and j > GS:
                        turn_output(n, j // GS - 1, 0 if last else 2 * GR)
                    for half in range(NH):
                        if j:
                            against_v(n, p, j - 1, half)
                        seek(NH + half)
                for half in range(NH):
                    if not last:
                        turn_group(n + 1, 1 - p, 2 * GR + half, CH - 1)
                    against_v(n, p, STEPS - 1, half)
                turn_output(n, CH - 1, 0 if last else 3 * GR)

            for g in range(2 * GR):
                turn_group(0, 0, g, 0)
            for i in range(ST * CH):
                first_pass(0, 0, i)
            for g in range(2 * GR, 3 * GR):
                turn_group(0, 0, g, 0)
            heads(pe, turn)

        @block.scalar
        def _(act):
            kept.prime(act)
            expd.prime(act)
            o_kept.prime(act)

            def keep(n, p, g):
                kind, g0 = divmod(g, GR)
                act.wait_ge(turned.sem, turned.at(n, g + 1))
                cols = slice(g0 * TG * P, (g0 + 1) * TG * P)
                if kind == 0:
                    nc.scalar.copy(k_t[0:ROWS, p, cols], ps_tr[0:ROWS, :]).then_inc(kept.sem, 1)
                elif kind == 1:
                    nc.scalar.copy(q_t[0:PAIRS, p, cols], ps_tr[0:PAIRS, :]).then_inc(kept.sem, 1)
                else:
                    nc.scalar.copy(q_t[PAIRS:ROWS, p, cols], ps_tr[PAIRS:ROWS, :]).then_inc(kept.sem, 1)

            def keep_output(n, chunk):
                act.wait_ge(pv.sem, pv.at(n, (chunk + 1) * GS))
                act.wait_ge(o_turned.sem, o_turned.at(n, chunk))
                nc.scalar.copy(o_t[:, :], ps_o[:, :]).then_inc(o_kept.sem, 1)

            def turn(n, h, p, last):
                for j in range(STEPS):
                    for half in range(NH):
                        if not last and j < GR:
                            keep(n + 1, 1 - p, j * 2 + half)
                        i = j * NH + half
                        act.wait_ge(scores.sem, scores.at(n, i + 1))
                        act.wait_ge(pv.sem, pv.at(n, j - RING // NH + 1))
                        nc.scalar.activation(prob[:, i % RING, :, :].rearrange("q a w -> q (a w)"), ps_s[half][:, :],
                                             ACT.Exp, scale=SCALE).then_inc(expd.sem, 1)
                    if j % GS == 0 and j:
                        keep_output(n, j // GS - 1)
                if not last:
                    for g in range(2 * GR, 3 * GR):
                        keep(n + 1, 1 - p, g)
                keep_output(n, CH - 1)

            for g in range(3 * GR):
                keep(0, 0, g)
            heads(act, turn)

        @block.vector
        def _(v):
            reduced.prime(v)
            max_split.prime(v)
            o_out.prime(v)
            v.memset(k_stack[:, 0, :, PAIRS:ROWS], 1.0).then_inc(set_up, 1)
            v.memset(k_stack[:, 1, :, PAIRS:ROWS], 1.0).then_inc(set_up, 1)
            v.memset(v_h[:, :, :, HD:VW], 0.0).then_inc(set_up, 1)
            v.wait_ge(set_up, 3)
            v.memset(v_h[:, :, :, HD:HD + 1], 1.0).then_inc(set_up, 1)

            def reduce(n, p, i):
                tile, c = divmod(i, CH)
                v.wait_ge(max_scores.sem, max_scores.at(n, i + 1))
                v.tensor_reduce(maxes[:, p, tile, c:c + 1], ps_m[i % 2][:, :], X, ALU.max).then_inc(reduced.sem, 1)

            def split_max(n, p):
                v.wait_ge(reduced.sem, reduced.at(n))
                v.tensor_reduce(neg_max[:, :], maxes[:, p, :, :], X, ALU.max, negate=True).then_inc(max_split.sem, 1)
                v.wait_ge(max_split.sem, max_split.at(n, 1))
                v.wait_ge(turned.sem, turned.at(n, 0))
                v.tensor_copy(max_parts[:, :, 0], neg_max[:, :]).then_inc(max_split.sem, 1)
                v.wait_ge(max_split.sem, max_split.at(n, 2))
                v.tensor_tensor(max_rest[:, :], neg_max[:, :], max_parts[:, :, 0], ALU.subtract).then_inc(max_split.sem, 1)
                v.wait_ge(max_split.sem, max_split.at(n, 3))
                v.tensor_copy(max_parts[:, :, 1], max_rest[:, :]).then_inc(max_split.sem, 1)
                v.wait_ge(max_split.sem, max_split.at(n, 4))
                v.tensor_tensor(max_parts[:, :, 2], max_rest[:, :], max_parts[:, :, 1], ALU.subtract).then_inc(max_split.sem, 1)

            def output(n, h, p, chunk):
                v.wait_ge(o_turned.sem, o_turned.at(n, chunk + 1))
                v.tensor_reduce(o_sum[:, :, :],
                                ps_tro[:, :].rearrange("q (t g e) -> q t e g", t=WT, g=GK)[:, :, 0:HD + 1, :],
                                X, ALU.add).then_inc(o_out.sem, 1)
                v.wait_ge(o_out.sem, o_out.at(n, 3 * chunk + 1))
                v.reciprocal(sums_inv[:, :, :], o_sum[:, :, HD:HD + 1]).then_inc(o_out.sem, 1)
                v.wait_ge(o_out.sem, o_out.at(n, 3 * chunk + 2))
                tiles = slice(p * ST + chunk * WT, p * ST + (chunk + 1) * WT)
                v.tensor_tensor(o_sb[:, tiles, bass.ds(h * HD, HD)], o_sum[:, :, 0:HD],
                                sums_inv[:, :, :].to_broadcast([P, WT, HD]), ALU.mult).then_inc(o_out.sem, 1)

            def turn(n, h, p, last):
                for j in range(STEPS):
                    if not last:
                        for i in plan[j]:
                            reduce(n + 1, 1 - p, i)
                    if not last and j == STEPS - 1:
                        split_max(n + 1, 1 - p)
                    if j % GS == 1 and j > GS:
                        output(n, h, p, j // GS - 1)
                output(n, h, p, CH - 1)

            for i in range(ST * CH):
                reduce(0, 0, i)
            split_max(0, 0)
            heads(v, turn)


E = 32
G = 2
GE = G * E
TOPK = 2
HID = 128
SLOT_TILES = T * TOPK // P + E
SLOTS = SLOT_TILES * P


def phase_route(nc, sems, x, o_sb, out_w, out_b, routers, x1_sb, xn_sb, lg_sb, top_val, top_idx, ident):
    N = NT // GT
    with Phase(nc, "route", sems) as ph:
        w_in = ph.sb("w_in", [P, KD, D])
        w_t = ph.sb("w_t", [P, KD, D])
        r_w = ph.sb("r_w", [P, KD, GE])
        bias = ph.sb("bias", [P, 1, D])
        x_in = ph.sb("x_in", [P, 2, GT, D])
        o_c = ph.sb("o_c", [P, 2, GT, D])
        turn_t = ph.sb("turn_t", [P, 2, KD, GP])
        x1 = ph.sb("x1", [P, 2, GT, D])
        xn = ph.sb("xn", [P, 2, GT, D])
        stats = ph.sb("stats", [P, GT, 6])
        mv = ph.sb("mv", [P, GT, 2])
        veps = ph.sb("veps", [P, GT])
        rstd = ph.sb("rstd", [P, GT])
        neg_half = ph.sb("neg_half", [P, GT])
        val8 = ph.sb("val8", [P, GT, G, 8])
        idx8 = ph.sb("idx8", [P, GT, G, 8], U32)
        ps_o = [ph.ps(f"ps_o{k}", [P, GP]) for k in range(KD)]
        ps_x = [ph.ps(f"ps_x{k}", [P, GP]) for k in range(KD)]
        ps_y = ph.ps("ps_y", [P, GT, D])
        ps_l = [ph.ps(f"ps_l{i}", [P, GT, 2 * GE]) for i in range(2)]

        gate = ph.sem("gate")
        consts_in = ph.sem("consts_in")
        half_set = ph.sem("half_set")
        w_turned = ph.steps("w_turned")
        w_kept = ph.steps("w_kept")
        x_landed = ph.transfers("x_landed")
        copied = ph.steps("copied")
        x_b_ready = ph.steps("x_b_ready")
        roots = ph.steps("roots")
        o_turned = ph.steps("o_turned", KD)
        o_t_ready = ph.steps("o_t_ready", KD)
        projected = ph.steps("projected")
        x1_ready = ph.steps("x1_ready")
        norm = ph.steps("norm", LN)
        xn_turned = ph.steps("xn_turned", KD)
        xn_t_ready = ph.steps("xn_t_ready", KD)
        kept_xn = ph.steps("kept_xn", 2)
        routed = ph.steps("routed")
        topped = ph.steps("topped", 3 + 2 * G * GT)
        block = ph.block()

        @block.sync
        def _(sp):
            x_landed.prime(sp)
            sp.dma_start(w_in[:, :, :], out_w.rearrange("(c p) d -> p c d", p=P)).then_inc(consts_in, 16)
            sp.dma_start(bias[:, 0, :], row_broadcast(out_b)).then_inc(consts_in, 16)
            for g, r in enumerate(routers):
                sp.dma_start(r_w[:, :, g * E:(g + 1) * E], r.rearrange("(k p) e -> p k e", p=P)).then_inc(consts_in, 16)

            def load(t, p):
                sp.wait_ge(x1_ready.sem, x1_ready.before(t))
                hold(sp, gate)
                sp.dma_start(x_in[:, p, :, :], x[bass.ds(t * GP, GP), :].rearrange("(n q) c -> q n c", q=P)).then_inc(x_landed.sems[p], 32)
            staged(sp, N, load)

        @block.gpsimd
        def _(pool):
            for s in (x_b_ready, roots):
                s.prime(pool)
            pool.memset(neg_half[:, :], -0.5).then_inc(half_set, 1)
            pool.wait_ge(half_set, 1)
            pool.wait_ge(consts_in, 16 * (2 + G))

            def add_bias(t, p):
                pool.wait_ge(x_landed.sems[p], x_landed.at(t, p))
                pool.tensor_tensor(x_in[:, p, :, :], x_in[:, p, :, :], bias[:, :, :].to_broadcast([P, GT, D]), ALU.add).then_inc(x_b_ready.sem, 1)

            def root(t, p):
                pool.wait_ge(norm.sem, norm.at(t, 2 * GT + 1))
                pool.tensor_tensor(rstd[:, :], veps[:, :], neg_half[:, :], ALU.pow).then_inc(roots.sem, 1)
            staged(pool, N, add_bias, root)

        @block.tensor
        def _(pe):
            for s in (w_turned, o_turned, projected, xn_turned, routed):
                s.prime(pe)
            pe.wait_ge(consts_in, 16 * (2 + G))
            for c in range(KD):
                for k in range(KD):
                    mm = pe.transpose(ps_o[c % 2][:, k * P:(k + 1) * P], w_in[:, c, k * P:(k + 1) * P], ident[:, :])
                mm.then_inc(w_turned.sem, 1)
            pe.wait_ge(w_kept.sem, w_kept.at(KD - 1))

            def project(t, p):
                pe.wait_ge(copied.sem, copied.at(t))
                pe.wait_ge(o_t_ready.sem, o_t_ready.before(t, 1))
                for k in range(KD):
                    for i in range(GT):
                        mm = pe.transpose(ps_o[k][:, i * P:(i + 1) * P], o_c[:, p, i, k * P:(k + 1) * P], ident[:, :])
                    mm.then_inc(o_turned.sem, 1)
                pe.wait_ge(o_t_ready.sem, o_t_ready.at(t))
                pe.wait_ge(x1_ready.sem, x1_ready.before(t, 1))
                for i in range(GT):
                    for k in range(KD):
                        mm = pe.matmul(ps_y[:, i, :], turn_t[:, 0, k, i * P:(i + 1) * P], w_t[:, k, :], start=(k == 0), stop=(k == KD - 1))
                mm.then_inc(projected.sem, 1)

            def route(t, p):
                pe.wait_ge(norm.sem, norm.at(t))
                pe.wait_ge(xn_t_ready.sem, xn_t_ready.before(t, 1))
                for k in range(KD):
                    for i in range(GT):
                        mm = pe.transpose(ps_x[k][:, i * P:(i + 1) * P], xn[:, p, i, k * P:(k + 1) * P], ident[:, :])
                    mm.then_inc(xn_turned.sem, 1)
                pe.wait_ge(xn_t_ready.sem, xn_t_ready.at(t))
                pe.wait_ge(topped.sem, topped.before(t))
                for i in range(GT):
                    for k in range(KD):
                        mm = pe.matmul(ps_l[p][:, i, 0:GE], turn_t[:, 1, k, i * P:(i + 1) * P], r_w[:, k, :], start=(k == 0), stop=(k == KD - 1))
                mm.then_inc(routed.sem, 1)
            staged(pe, N, project, route)

        @block.scalar
        def _(act):
            for s in (w_kept, copied, o_t_ready, xn_t_ready, kept_xn):
                s.prime(act)
            for c in range(KD):
                act.wait_ge(w_turned.sem, w_turned.at(c))
                nc.scalar.copy(w_t[:, :, c * P:(c + 1) * P],
                               ps_o[c % 2][:, 0:D].rearrange("q (k n) -> q k n", k=KD)).then_inc(w_kept.sem, 1)

            def fetch(t, p):
                act.wait_ge(o_turned.sem, o_turned.before(t))
                hold(act, gate)
                nc.scalar.copy(flat(o_c[:, p, :, :]), flat(o_sb[:, bass.ds(t * GT, GT), :])).then_inc(copied.sem, 1)

            def keep_o(t, p):
                act.wait_ge(projected.sem, projected.before(t, 1))
                for k in range(KD):
                    act.wait_ge(o_turned.sem, o_turned.at(t, k + 1))
                    nc.scalar.copy(turn_t[:, 0, k, :], ps_o[k][:, :]).then_inc(o_t_ready.sem, 1)

            def keep_x(t, p):
                act.wait_ge(routed.sem, routed.before(t, 1))
                for k in range(KD):
                    act.wait_ge(xn_turned.sem, xn_turned.at(t, k + 1))
                    nc.scalar.copy(turn_t[:, 1, k, :], ps_x[k][:, :]).then_inc(xn_t_ready.sem, 1)
                hold(act, gate)
                nc.scalar.copy(flat(x1_sb[:, bass.ds(t * GT, GT), :]), flat(x1[:, p, :, :])).then_inc(kept_xn.sem, 1)
                nc.scalar.copy(flat(xn_sb[:, bass.ds(t * GT, GT), :]), flat(xn[:, p, :, :])).then_inc(kept_xn.sem, 1)
            staged(act, N, fetch, keep_o, keep_x)

        @block.vector
        def _(v):
            for s in (x1_ready, norm, topped):
                s.prime(v)

            def normalise(t, p):
                v.wait_ge(projected.sem, projected.at(t))
                v.wait_ge(x_b_ready.sem, x_b_ready.at(t))
                v.wait_ge(kept_xn.sem, kept_xn.before(t))
                v.tensor_tensor(flat(x1[:, p, :, :]), flat(ps_y[:, :, :]), flat(x_in[:, p, :, :]), ALU.add).then_inc(x1_ready.sem, 1)
                v.wait_ge(x1_ready.sem, x1_ready.at(t))
                layer_norm(v, t, norm, roots, x1[:, p], xn[:, p], stats, mv, veps[:, :], rstd, gate)

            def top(t, p):
                v.wait_ge(routed.sem, routed.at(t))
                hold(v, gate)
                v.tensor_copy(lg_sb[:, bass.ds(t * GT, GT), :], ps_l[p][:, :, 0:GE]).then_inc(topped.sem, 1)
                v.wait_ge(topped.sem, topped.before(t, 1))
                hold(v, gate)
                for i in range(GT):
                    for g in range(G):
                        v.max(val8[:, i, g, :], ps_l[p][:, i, g * E:(g + 1) * E]).then_inc(topped.sem, 1)
                v.wait_ge(topped.sem, topped.at(t, 1 + G * GT))
                hold(v, gate)
                for i in range(GT):
                    for g in range(G):
                        v.max_index(idx8[:, i, g, :], val8[:, i, g, :], ps_l[p][:, i, g * E:(g + 1) * E]).then_inc(topped.sem, 1)
                v.wait_ge(topped.sem, topped.at(t, 1 + 2 * G * GT))
                hold(v, gate)
                v.tensor_copy(top_val[:, bass.ds(t * GT, GT), :, :].rearrange("q n g k -> q (n g) k"),
                              val8[:, :, :, 0:TOPK].rearrange("q n g k -> q (n g) k")).then_inc(topped.sem, 1)
                v.tensor_copy(top_idx[:, bass.ds(t * GT, GT), :, :].rearrange("q n g k -> q (n g) k"),
                              idx8[:, :, :, 0:TOPK].rearrange("q n g k -> q (n g) k")).then_inc(topped.sem, 1)
            staged(v, N, normalise, top)


def phase_slots(nc, sems, xn_sb, lg_sb, top_val, top_idx, weight, pos, tile_expert, slots_x):
    TE = SLOT_TILES + 1
    with Phase(nc, "slots", sems) as ph:
        iota_e = ph.sb("iota_e", [P, E])
        iota_t = ph.sb("iota_t", [1, TE])
        idx_f = ph.sb("idx_f", [P, NT, G, TOPK])
        hot = [ph.sb(f"hot{r}", [P, NT, G, E]) for r in range(TOPK)]
        both = ph.sb("both", [P, NT, GE], BF16)
        before = ph.sb("before", [P, NT + 1, GE], BF16)
        tri = ph.sb("tri", [P, P], BF16)
        ones = ph.sb("ones", [P, P], BF16)
        work = ph.sb("work", [P, NT, G, E])
        gap = ph.sb("gap", [P, NT, G, TOPK])
        total = ph.sb("total", [P, NT, G, 1])
        inverse = ph.sb("inverse", [P, NT, G, 1])
        tiles_i = ph.sb("tiles_i", [P, GE], I32)
        tiles_f = ph.sb("tiles_f", [P, GE])
        ones_f = ph.sb("ones_f", [P, E])
        ends = ph.sb("ends", [P, GE])
        starts = ph.sb("starts", [P, G, E])
        pos_f = ph.sb("pos_f", [P, NT, G, TOPK])
        past = ph.sb("past", [1, TE, E])
        count_f = ph.sb("count_f", [1, G, TE])
        ps_w = [ph.ps(f"ps_w{i}", [P, 512]) for i in range(NT * GE // 512)]
        ps_n = ph.ps("ps_n", [P, 512])

        made = ph.sem("made")
        step = ph.sem("step")
        exped = ph.sem("exped")
        counted = ph.sem("counted")
        scattered = ph.sem("scattered", soft=True)
        n = {}
        block = ph.block()

        @block.vector
        def _(v):
            done = [0]

            def did(ins, name=None):
                ins.then_inc(step, 1)
                done[0] += 1
                if name:
                    n[name] = done[0]

            def settle():
                v.wait_ge(step, done[0])

            did(v.memset(before[:, 0, :], 0.0))
            did(v.memset(ones_f[:, :], 1.0))
            did(v.tensor_tensor(work[:, :, :, :].rearrange("q t g e -> q (t g) e"),
                                lg_sb[:, :, :].rearrange("q t (g e) -> q (t g) e", g=G),
                                top_val[:, :, :, 0:1].rearrange("q t g k -> q (t g) k").to_broadcast([P, NT * G, E]),
                                ALU.subtract))
            did(v.tensor_tensor(gap[:, :, :, :].rearrange("q t g k -> q (t g) k"),
                                top_val[:, :, :, :].rearrange("q t g k -> q (t g) k"),
                                top_val[:, :, :, 0:1].rearrange("q t g k -> q (t g) k").to_broadcast([P, NT * G, TOPK]),
                                ALU.subtract), "shifted")
            v.wait_ge(made, 6)
            for r in range(TOPK):
                did(v.tensor_tensor(hot[r][:, :, :, :].rearrange("q t g e -> q (t g) e"),
                                    top_idx[:, :, :, r:r + 1].rearrange("q t g k -> q (t g) k").to_broadcast([P, NT * G, E]),
                                    iota_e[:, :].unsqueeze(1).to_broadcast([P, NT * G, E]), ALU.is_equal))
            settle()
            did(v.tensor_tensor(both[:, :, :], hot[0][:, :, :, :].rearrange("q t g e -> q t (g e)"),
                                hot[1][:, :, :, :].rearrange("q t g e -> q t (g e)"), ALU.add))
            for t in range(NT):
                settle()
                did(v.tensor_tensor(before[:, t + 1, :], before[:, t, :], both[:, t, :], ALU.add))
            n["before"] = done[0]
            v.wait_ge(exped, 2)
            did(v.tensor_reduce(total[:, :, :, :].rearrange("q t g a -> q (t g) a"),
                                work[:, :, :, :].rearrange("q t g e -> q (t g) e"), X, ALU.add))
            settle()
            did(v.reciprocal(inverse[:, :, :, :].rearrange("q t g a -> q (t g) a"),
                             total[:, :, :, :].rearrange("q t g a -> q (t g) a")))
            settle()
            did(v.tensor_scalar(inverse[:, :, :, :].rearrange("q t g a -> q (t g a)"),
                                inverse[:, :, :, :].rearrange("q t g a -> q (t g a)"), 1.0 / G, None, ALU.mult))
            settle()
            did(v.tensor_tensor(weight[:, :, :, :].rearrange("q t g k -> q (t g) k"),
                                gap[:, :, :, :].rearrange("q t g k -> q (t g) k"),
                                inverse[:, :, :, :].rearrange("q t g a -> q (t g) a").to_broadcast([P, NT * G, TOPK]),
                                ALU.mult))
            v.wait_ge(counted, 1)
            did(v.tensor_scalar(tiles_f[:, :], ps_n[:, 0:GE], float(P - 1), None, ALU.add))
            settle()
            did(v.tensor_copy(tiles_i[:, :], tiles_f[:, :]))
            settle()
            did(v.tensor_scalar(tiles_i[:, :], tiles_i[:, :], P.bit_length() - 1, None, ALU.logical_shift_right))
            settle()
            did(v.tensor_copy(tiles_f[:, :], tiles_i[:, :]))
            settle()
            for g in range(G):
                did(v.tensor_tensor_scan(ends[:, g * E:(g + 1) * E], ones_f[:, :], tiles_f[:, g * E:(g + 1) * E],
                                         0.0, ALU.mult, ALU.add))
            settle()
            did(v.tensor_tensor(starts[:, :, :].rearrange("q g e -> q (g e)"), ends[:, :], tiles_f[:, :], ALU.subtract))
            settle()
            for g in range(G):
                did(v.tensor_scalar(starts[:, g, :], starts[:, g, :], float(P), float(g * (SLOTS + P)), ALU.mult, ALU.add))
            for g in range(G):
                settle()
                did(v.tensor_tensor(past[:, :, :], ends[0:1, g * E:(g + 1) * E].unsqueeze(1).to_broadcast([1, TE, E]),
                                    iota_t[:, :].unsqueeze(2).to_broadcast([1, TE, E]), ALU.is_le))
                settle()
                did(v.tensor_reduce(count_f[:, g, :], past[:, :, :], X, ALU.add))
            settle()
            did(v.tensor_scalar(tile_expert[:, :, :], count_f[:, :, :], float(E - 1), None, ALU.min))
            NB = 512 // GE
            v.wait_ge(counted, 2)
            for i, ps in enumerate(ps_w):
                did(v.tensor_tensor(work[:, i * NB:(i + 1) * NB, :, :].rearrange("q t g e -> q t (g e)"),
                                    ps[:, :].rearrange("q (t e) -> q t e", t=NB),
                                    starts[:, :, :].rearrange("q g e -> q (g e)").unsqueeze(1).to_broadcast([P, NB, GE]),
                                    ALU.add))
            settle()
            for r in range(TOPK):
                did(v.tensor_tensor(hot[r][:, :, :, :].rearrange("q t g e -> q (t g e)"),
                                    hot[r][:, :, :, :].rearrange("q t g e -> q (t g e)"),
                                    work[:, :, :, :].rearrange("q t g e -> q (t g e)"), ALU.mult))
            settle()
            for r in range(TOPK):
                did(v.tensor_reduce(pos_f[:, :, :, r:r + 1].rearrange("q t g a -> q (t g) a"),
                                    hot[r][:, :, :, :].rearrange("q t g e -> q (t g) e"), X, ALU.add))
            settle()
            did(v.tensor_copy(pos[:, :, :, :], pos_f[:, :, :, :]), "pos")
            settle()

        @block.scalar
        def _(act):
            act.wait_ge(step, n["shifted"])
            nc.scalar.activation(work[:, :, :, :], work[:, :, :, :], ACT.Exp).then_inc(exped, 1)
            nc.scalar.activation(gap[:, :, :, :], gap[:, :, :, :], ACT.Exp).then_inc(exped, 1)

        @block.tensor
        def _(pe):
            pe.wait_ge(made, 6)
            pe.wait_ge(step, n["before"])
            pe.matmul(ps_n[:, 0:GE], ones[:, :], before[:, NT, :], start=True, stop=True).then_inc(counted, 1)
            NB = 512 // GE
            for i, ps in enumerate(ps_w):
                pe.matmul(ps[:, :], tri[:, :], both[:, i * NB:(i + 1) * NB, :].rearrange("q t e -> q (t e)"),
                          start=True, stop=False)
                mm = pe.matmul(ps[:, :], ones[:, :], before[:, i * NB:(i + 1) * NB, :].rearrange("q t e -> q (t e)"),
                               start=False, stop=True)
            mm.then_inc(counted, 1)

        @block.gpsimd
        def _(pool):
            pool.iota(iota_e[:, :], pattern=[[1, E]], base=0, channel_multiplier=0,
                      allow_small_or_imprecise_dtypes=True).then_inc(made, 1)
            pool.iota(iota_t[:, :], pattern=[[1, TE]], base=0, channel_multiplier=0,
                      allow_small_or_imprecise_dtypes=True).then_inc(made, 1)
            pool.memset(ones[:, :], 1.0).then_inc(made, 1)
            pool.memset(tri[:, :], 1.0).then_inc(made, 1)
            pool.wait_ge(made, 4)
            pool.affine_select(out=tri[:, :], in_=tri[:, :], compare_op=ALU.is_gt, fill=0.0, base=0,
                               pattern=[[1, P]], channel_multiplier=-1).then_inc(made, 1)
            pool.nop().then_inc(made, 1)
            pool.wait_ge(step, n["pos"])
            for t in range(NT):
                for g in range(G):
                    for r in range(TOPK):
                        pool.indirect_dma_start(out=slots_x, out_offset=bass.IndirectOffsetOnAxis(ap=pos[:, t, g, r:r + 1], axis=0),
                                                in_=xn_sb[:, t, :], in_offset=None).then_inc(scattered, 16)
            pool.wait_ge(scattered, 16 * NT * G * TOPK)


def zero_slots(nc, sp, zeros, slots_x, slots_y, zeroed):
    rows = slots_x.shape[0]
    view = slots_x.rearrange("(n p r) c -> n p (r c)", p=P, r=2)
    for n in range(rows // (2 * P)):
        sp.dma_start(view[n], zeros[:, 0:2 * D]).then_inc(zeroed, 16)
    for g in range(G):
        end = (g + 1) * (SLOTS + P)
        sp.dma_start(slots_y[end - P:end, :], zeros[:, 0:D]).then_inc(zeroed, 16)


ZEROINGS = G * (SLOTS + P) // (2 * P) + G


def load_gate_up(sp, w_gu, wg, wu, landed):
    for k in range(KD):
        for i, w in enumerate((wg, wu)):
            sp.dma_start(w_gu[:, k, :, i, :], w[:, k * P:(k + 1) * P, :].rearrange("e p h -> p e h")).then_inc(landed, 16)


def phase_experts(nc, sems, g, w_gu, w_d, weights, w_landed, slots_x, slots_y, tile_expert, ident):
    N = SLOT_TILES
    base = g * (SLOTS + P)
    with Phase(nc, f"experts{g}", sems) as ph:
        xs = ph.sb("xs", [P, 2 * GT, D])
        x_t = ph.sb("x_t", [P, 2, KD, P])
        gs = ph.sb("gs", [P, 2, HID])
        h = ph.sb("h", [P, 2, HID])
        h_t = ph.sb("h_t", [P, 2, P])
        y = ph.sb("y", [P, 2 * GT, D])
        ps_t = [ph.ps(f"ps_t{i}", [P, 512]) for i in range(2)]
        ps_g = [ph.ps(f"ps_g{i}", [P, 512]) for i in range(2)]
        ps_h = [ph.ps(f"ps_h{i}", [P, 512]) for i in range(2)]
        ps_y = [ph.ps(f"ps_y{i}", [P, 512]) for i in range(2)]

        gate = ph.sem("gate")
        down_landed = ph.sem("down_landed")
        x_landed = ph.transfers("x_landed")
        turned = ph.steps("turned", ahead=2 * GT)
        x_ready = ph.steps("x_ready")
        gated = ph.steps("gated")
        silu = ph.steps("silu")
        h_ready = ph.steps("h_ready")
        h_turned = ph.steps("h_turned")
        h_t_ready = ph.steps("h_t_ready")
        down = ph.steps("down")
        y_ready = ph.steps("y_ready", ahead=2 * GT)
        stored = ph.transfers("stored")
        block = ph.block()

        @block.sync
        def _(sp):
            x_landed.prime(sp)
            stored.prime(sp)
            wg, wu, wd = weights
            if g:
                load_gate_up(sp, w_gu, wg, wu, w_landed)
            sp.dma_start(w_d[:, :, :], wd.rearrange("e h d -> h e d")).then_inc(down_landed, 16)

            def load(t, p):
                sp.wait_ge(turned.sem, turned.at(t * GT - GT - 1))
                hold(sp, gate)
                sp.dma_start(xs[:, p * GT:(p + 1) * GT, :],
                             slots_x[bass.ds(t * GP + base, GP), :].rearrange("(n q) c -> q n c", q=P)).then_inc(x_landed.sems[p], 32)

            def store(t, p):
                sp.wait_ge(y_ready.sem, y_ready.at(t * GT + GT - 1))
                hold(sp, gate)
                sp.dma_start(slots_y[bass.ds(t * GP + base, GP), :].rearrange("(n q) c -> q n c", q=P),
                             y[:, p * GT:(p + 1) * GT, :]).then_inc(stored.sems[p], 32)
            def idle(t, p):
                pass
            staged(sp, N // GT, load, idle, store)
            for t in (N // GT - 2, N // GT - 1):
                sp.wait_ge(stored.sems[t % 2], stored.at(t, t % 2))

        @block.tensor
        def _(pe):
            for s in (turned, gated, h_turned, down):
                s.prime(pe)
            pe.wait_ge(w_landed, 16 * 2 * KD)
            pe.wait_ge(down_landed, 16)

            def expert(t):
                return pe.value_load(tile_expert[0:1, g, bass.ds(t, 1)], min_val=0, max_val=E - 1)

            def turn_x(t, p):
                pe.wait_ge(x_landed.sems[p // GT], x_landed.at_tile(t, p))
                for k in range(KD):
                    mm = pe.transpose(ps_t[p % 2][:, k * P:(k + 1) * P], xs[:, p, k * P:(k + 1) * P], ident[:, :])
                mm.then_inc(turned.sem, 1)

            def gate_up(t, p):
                e = expert(t)
                pe.wait_ge(x_ready.sem, x_ready.at(t))
                for k in range(KD):
                    mm = pe.matmul(ps_g[p % 2][:, 0:2 * HID], x_t[:, p % 2, k, :],
                                   w_gu[:, k, bass.ds(e, 1), :, :].rearrange("q a i h -> q (a i h)"),
                                   start=(k == 0), stop=(k == KD - 1))
                mm.then_inc(gated.sem, 1)

            def turn_h(t, p):
                pe.wait_ge(h_ready.sem, h_ready.at(t))
                pe.transpose(ps_h[p % 2][:, 0:P], h[:, p % 2, :], ident[:, :]).then_inc(h_turned.sem, 1)

            def go_down(t, p):
                e = expert(t)
                pe.wait_ge(h_t_ready.sem, h_t_ready.at(t))
                pe.wait_ge(y_ready.sem, y_ready.before(t, 2))
                pe.matmul(ps_y[p % 2][:, 0:D], h_t[:, p % 2, :], w_d[:, bass.ds(e, 1), :].rearrange("q a c -> q (a c)"),
                          start=True, stop=True).then_inc(down.sem, 1)
            staged(pe, N, turn_x, gate_up, turn_h, go_down, unroll=2 * GT)

        @block.scalar
        def _(act):
            for s in (x_ready, silu, y_ready):
                s.prime(act)

            def keep_x(t, p):
                act.wait_ge(turned.sem, turned.at(t))
                nc.scalar.copy(x_t[:, p % 2, :, :].rearrange("q k n -> q (k n)"), ps_t[p % 2][:, 0:D]).then_inc(x_ready.sem, 1)

            def activate(t, p):
                act.wait_ge(gated.sem, gated.at(t))
                nc.scalar.activation(gs[:, p % 2, :], ps_g[p % 2][:, 0:HID], ACT.Silu).then_inc(silu.sem, 1)

            def idle(t, p):
                pass

            def keep_y(t, p):
                act.wait_ge(down.sem, down.at(t))
                if p % GT == 0:
                    act.wait_ge(stored.sems[p // GT], stored.before_tile(t, p))
                nc.scalar.copy(y[:, p, :], ps_y[p % 2][:, 0:D]).then_inc(y_ready.sem, 1)
            staged(act, N, keep_x, activate, idle, keep_y, unroll=2 * GT)

        @block.vector
        def _(v):
            for s in (h_ready, h_t_ready):
                s.prime(v)

            def multiply(t, p):
                v.wait_ge(silu.sem, silu.at(t))
                v.tensor_tensor(h[:, p % 2, :], gs[:, p % 2, :], ps_g[p % 2][:, HID:2 * HID], ALU.mult).then_inc(h_ready.sem, 1)

            def keep_h(t, p):
                v.wait_ge(h_turned.sem, h_turned.at(t))
                v.tensor_copy(h_t[:, p % 2, :], ps_h[p % 2][:, 0:P]).then_inc(h_t_ready.sem, 1)
            staged(v, N, multiply, keep_h, unroll=2 * GT)


GN = 8
NBK = S // GN
PW = 3 * D + 2 * H


def phase_combine(nc, sems, x1_sb, z_sb, weight, pos, slots_y, w_qkv, w_bg, ln_g, ln_b, proj, ident):
    HALVES = ((0, 512), (512, PW))
    N = NT // GT
    NY = G * TOPK
    with Phase(nc, "comb", sems) as ph:
        w_in = ph.sb("w_in", [P, KD, PW])
        w_s = ph.sb("w_s", [P, KD, PW])
        g_col = ph.sb("g_col", [P, KD])
        b_col = ph.sb("b_col", [P, KD])
        b_wide = ph.sb("b_wide", [P, KD, P])
        bias = ph.sb("bias", [P, PW])
        y_in = ph.sb("y_in", [P, 2, GT, NY, D])
        w_c = ph.sb("w_c", [P, 2, GT * NY])
        x2 = ph.sb("x2", [P, 2, GT, D])
        z = ph.sb("z", [P, 2, GT, D])
        hn = ph.sb("hn", [P, 2, GT, D])
        stats = ph.sb("stats", [P, 2, GT, 6])
        mv = ph.sb("mv", [P, 2, GT, 2])
        veps = ph.sb("veps", [P, 2, GT])
        rstd = ph.sb("rstd", [P, 2, GT])
        neg_half = ph.sb("neg_half", [P, GT])
        h_t = ph.sb("h_t", [P, KD, GP])
        pr = ph.sb("pr", [P, 2, GT, PW])
        sq = ph.sb("sq", [P, GT, D])
        norm2 = ph.sb("norm2", [P, GT * H])
        root0 = ph.sb("root0", [P, GT * H])
        length = ph.sb("length", [P, GT * H])
        inv_len = ph.sb("inv_len", [P, GT * H])
        ps_t = [ph.ps(f"ps_t{k}", [P, GP]) for k in range(KD)]
        ps_p = [ph.ps(f"ps_p{i}", [P, 1024]) for i in range(2)]

        gate = ph.sem("gate")
        consts_in = ph.sem("consts_in")
        set_up = ph.sem("set_up")
        scaled = ph.sem("scaled")
        biased = ph.sem("biased")
        bias_kept = ph.sem("bias_kept")
        y_landed = ph.transfers("y_landed", GT * NY, soft=True)
        weights_at = ph.steps("weights_at")
        added = ph.steps("added", GT * NY)
        norm_z = ph.steps("norm_z", LN)
        norm_h = ph.steps("norm_h", LN)
        root_z = ph.steps("root_z")
        root_h = ph.steps("root_h")
        kept = ph.steps("kept", 2)
        turned = ph.steps("turned", KD)
        h_ready = ph.steps("h_ready", KD)
        projected = ph.steps("projected", GT)
        proj_kept = ph.steps("proj_kept", GT)
        squared = ph.steps("squared")
        root_k = ph.steps("root_k")
        k_done = ph.steps("k_done", 8)
        sigmoid = ph.steps("sigmoid")
        stored = ph.transfers("stored")
        block = ph.block()

        @block.sync
        def _(sp):
            stored.prime(sp)
            for i, w in enumerate(w_qkv):
                sp.dma_start(w_in[:, :, i * D:(i + 1) * D], w.rearrange("(k p) c -> p k c", p=P)).then_inc(consts_in, 16)
            for i, w in enumerate(w_bg):
                sp.dma_start(w_in[:, :, 3 * D + i * H:3 * D + (i + 1) * H], w.rearrange("(k p) c -> p k c", p=P)).then_inc(consts_in, 16)
            with nc.allow_non_contiguous_dma("two short columns"):
                sp.dma_start(g_col[:, :], ln_g.rearrange("(k p) -> p k", p=P)).then_inc(consts_in, 16)
                sp.dma_start(b_col[:, :], ln_b.rearrange("(k p) -> p k", p=P)).then_inc(consts_in, 16)

            def store(t, p):
                sp.wait_ge(k_done.sem, k_done.at(t))
                hold(sp, gate)
                sp.wait_ge(sigmoid.sem, sigmoid.at(t))
                hold(sp, gate)
                sp.dma_start(proj[bass.ds(t * GP, GP), :].rearrange("(n q) c -> q n c", q=P), pr[:, p, :, :]).then_inc(stored.sems[p], 32)
            staged(sp, N, store)
            for t in (N - 2, N - 1):
                sp.wait_ge(stored.sems[t % 2], stored.at(t, t % 2))

        @block.gpsimd
        def _(pool):
            for s in (root_z, root_h, squared):
                s.prime(pool)
            pool.memset(neg_half[:, :], -0.5).then_inc(set_up, 1)
            pool.wait_ge(set_up, 1)

            def fetch(t, tiles):
                p = t % 2
                pool.wait_ge(added.sem, added.before(t))
                for i in tiles:
                    for y in range(NY):
                        g, k = divmod(y, TOPK)
                        pool.indirect_dma_start(
                            out=y_in[:, p, i, y, :], out_offset=None, in_=slots_y,
                            in_offset=bass.IndirectOffsetOnAxis(ap=pos[:, t * GT + i, g, k:k + 1], axis=0)
                        ).then_inc(y_landed.sems[p], 32)

            def square(t):
                k = pr[:, t % 2, :, D:2 * D]
                pool.wait_ge(proj_kept.sem, proj_kept.at(t))
                pool.wait_ge(k_done.sem, k_done.before(t, 1))
                pool.tensor_tensor(sq[:, :, :], k, k, ALU.mult).then_inc(squared.sem, 1)

            fetch(0, range(GT))
            for t in range(N + 1):
                if t + 1 < N:
                    fetch(t + 1, range(GT // 2))
                if t < N:
                    pool.wait_ge(norm_z.sem, norm_z.at(t, 2 * GT + 1))
                    pool.tensor_tensor(rstd[:, 0, :], veps[:, 0, :], neg_half[:, :], ALU.pow).then_inc(root_z.sem, 1)
                    pool.wait_ge(norm_h.sem, norm_h.at(t, 2 * GT + 1))
                    pool.tensor_tensor(rstd[:, 1, :], veps[:, 1, :], neg_half[:, :], ALU.pow).then_inc(root_h.sem, 1)
                if t + 1 < N:
                    fetch(t + 1, range(GT // 2, GT))
                if t:
                    square(t - 1)

        @block.vector
        def _(v):
            for s in (added, norm_z, norm_h, proj_kept, k_done):
                s.prime(v)
            v.wait_ge(consts_in, 16 * 7)
            for k in range(KD):
                v.tensor_scalar(w_s[:, k, :], w_in[:, k, :], g_col[:, k:k + 1], None, ALU.mult).then_inc(scaled, 1)
                v.tensor_copy(b_wide[:, k, :], b_col[:, k:k + 1].to_broadcast([P, P])).then_inc(scaled, 1)
            v.wait_ge(scaled, 2 * KD)
            v.tensor_scalar(w_s[:, :, 0:D], w_s[:, :, 0:D], float(HD) ** -0.5, None, ALU.mult).then_inc(scaled, 1)
            v.tensor_scalar(w_in[:, :, 0:D], w_in[:, :, 0:D], float(HD) ** -0.5, None, ALU.mult).then_inc(scaled, 1)
            v.wait_ge(biased, 1)
            for a, b in HALVES:
                v.tensor_copy(bias[:, a:b], ps_p[0][:, a:b]).then_inc(bias_kept, 1)
            v.wait_ge(bias_kept, 2)

            def combine(t, p):
                v.wait_ge(y_landed.sems[p], y_landed.at(t, p))
                v.wait_ge(weights_at.sem, weights_at.at(t))
                v.wait_ge(kept.sem, kept.before(t))
                hold(v, gate)
                for y in range(NY):
                    for i in range(GT):
                        if y:
                            v.wait_ge(added.sem, added.at(t, (y - 1) * GT + i + 1))
                        before = x2[:, p, i, :] if y else flat(x1_sb[:, bass.ds(t * GT + i, 1), :])
                        v.scalar_tensor_tensor(x2[:, p, i, :], y_in[:, p, i, y, :], w_c[:, p, i * NY + y:i * NY + y + 1],
                                               before, ALU.mult, ALU.add).then_inc(added.sem, 1)
                v.wait_ge(added.sem, added.at(t))
                layer_norm(v, t, norm_z, root_z, x2[:, p], z[:, p], stats[:, 0], mv[:, 0], veps[:, 0, :], rstd[:, 0, :], gate)
                v.wait_ge(norm_z.sem, norm_z.at(t))
                v.wait_ge(turned.sem, turned.before(t))
                layer_norm(v, t, norm_h, root_h, z[:, p], hn[:, p], stats[:, 1], mv[:, 1], veps[:, 1, :], rstd[:, 1, :], gate)

            def finish(t, p):
                v.wait_ge(stored.sems[p], stored.before(t, p))
                for i in range(GT):
                    v.wait_ge(projected.sem, projected.at(t, i + 1))
                    v.tensor_tensor(pr[:, p, i, :], ps_p[i % 2][:, 0:PW], bias[:, :], ALU.add).then_inc(proj_kept.sem, 1)
                v.wait_ge(squared.sem, squared.at(t))
                v.tensor_reduce(norm2[:, :], sq[:, :, :].rearrange("q n (h d) -> q (n h) d", h=H), X, ALU.add).then_inc(k_done.sem, 1)
                v.wait_ge(root_k.sem, root_k.at(t))
                v.tensor_scalar(root0[:, :], length[:, :], 1e-18, None, ALU.max).then_inc(k_done.sem, 1)
                v.wait_ge(k_done.sem, k_done.at(t, 2))
                v.reciprocal(inv_len[:, :], root0[:, :]).then_inc(k_done.sem, 1)
                v.wait_ge(k_done.sem, k_done.at(t, 3))
                v.tensor_tensor(length[:, :], norm2[:, :], inv_len[:, :], ALU.mult).then_inc(k_done.sem, 1)
                v.wait_ge(k_done.sem, k_done.at(t, 4))
                v.tensor_tensor(length[:, :], length[:, :], root0[:, :], ALU.add).then_inc(k_done.sem, 1)
                v.wait_ge(k_done.sem, k_done.at(t, 5))
                v.tensor_scalar(length[:, :], length[:, :], 0.5, 1e-6, ALU.mult, ALU.add).then_inc(k_done.sem, 1)
                v.wait_ge(k_done.sem, k_done.at(t, 6))
                v.reciprocal(inv_len[:, :], length[:, :]).then_inc(k_done.sem, 1)
                v.wait_ge(k_done.sem, k_done.at(t, 7))
                k = pr[:, p, :, D:2 * D].rearrange("q n (h d) -> q n h d", h=H)
                v.tensor_tensor(k, k, inv_len[:, :].rearrange("q (n h) -> q n h", n=GT).unsqueeze(3).to_broadcast([P, GT, H, HD]),
                                ALU.mult).then_inc(k_done.sem, 1)
            staged(v, N, combine, finish)

        @block.tensor
        def _(pe):
            for s in (turned, projected):
                s.prime(pe)
            pe.wait_ge(scaled, 2 * KD + 2)
            for a, b in HALVES:
                for k in range(KD):
                    mm = pe.matmul(ps_p[0][:, a:b], b_wide[:, k, :], w_in[:, k, a:b], start=(k == 0), stop=(k == KD - 1))
            mm.then_inc(biased, 1)
            pe.wait_ge(bias_kept, 2)

            def turn_and_project(t, p):
                pe.wait_ge(norm_h.sem, norm_h.at(t))
                pe.wait_ge(h_ready.sem, h_ready.before(t, 1))
                for k in range(KD):
                    for i in range(GT):
                        mm = pe.transpose(ps_t[k][:, i * P:(i + 1) * P], hn[:, p, i, k * P:(k + 1) * P], ident[:, :])
                    mm.then_inc(turned.sem, 1)
                pe.wait_ge(h_ready.sem, h_ready.at(t))
                for i in range(GT):
                    pe.wait_ge(proj_kept.sem, proj_kept.at(t, i - 1))
                    for a, b in HALVES:
                        for k in range(KD):
                            mm = pe.matmul(ps_p[i % 2][:, a:b], h_t[:, k, i * P:(i + 1) * P], w_s[:, k, a:b],
                                           start=(k == 0), stop=(k == KD - 1))
                    mm.then_inc(projected.sem, 1)
            staged(pe, N, turn_and_project)

        @block.scalar
        def _(act):
            for s in (weights_at, kept, h_ready, root_k, sigmoid):
                s.prime(act)

            def fetch(t, p):
                act.wait_ge(added.sem, added.before(t))
                hold(act, gate)
                nc.scalar.copy(w_c[:, p, :], weight[:, bass.ds(t * GT, GT), :, :].rearrange("q n g k -> q (n g k)")).then_inc(weights_at.sem, 1)

            def keep(t, p):
                act.wait_ge(norm_z.sem, norm_z.at(t))
                hold(act, gate)
                nc.scalar.copy(flat(x1_sb[:, bass.ds(t * GT, GT), :]), flat(x2[:, p, :, :])).then_inc(kept.sem, 1)
                act.wait_ge(norm_h.sem, norm_h.at(t))
                hold(act, gate)
                nc.scalar.copy(flat(z_sb[:, bass.ds(t * GT, GT), :]), flat(z[:, p, :, :])).then_inc(kept.sem, 1)
                act.wait_ge(projected.sem, projected.before(t, 1))
                for k in range(KD):
                    act.wait_ge(turned.sem, turned.at(t, k + 1))
                    nc.scalar.copy(h_t[:, k, :], ps_t[k][:, :]).then_inc(h_ready.sem, 1)

            def squash(t, p):
                act.wait_ge(proj_kept.sem, proj_kept.at(t))
                act.wait_ge(k_done.sem, k_done.at(t, 1))
                nc.scalar.activation(length[:, :], norm2[:, :], ACT.Sqrt).then_inc(root_k.sem, 1)
                nc.scalar.activation(pr[:, p, :, 3 * D:PW], pr[:, p, :, 3 * D:PW], ACT.Sigmoid).then_inc(sigmoid.sem, 1)
            staged(act, N, fetch, keep, squash)


VQ = 4
V4 = HD // VQ
HH = H // 2
HW = HH * HD
REC1 = 3 * GN * HD
REC2 = 2 * GN * V4 + 1
UW = GN * V4


def phase_blocks(nc, sems, proj, rec1, rec2):
    ROUNDS = 2 * T // (GN * P)
    with Phase(nc, "blocks", sems) as ph:
        raw = ph.sb("raw", [P, 2, GN, 3, HW])
        bg = ph.sb("bg", [P, 2, GN, 2, HH])
        decay = ph.sb("decay", [P, GN, GN, HH])
        neg_b = ph.sb("neg_b", [P, GN, HH])
        neg_bd = ph.sb("neg_bd", [P, GN, GN, HH])
        gam = ph.sb("gam", [P, GN, HH])
        b_gam = ph.sb("b_gam", [P, GN, HH])
        kk = ph.sb("kk", [P, GN, GN, HH])
        a_neg = ph.sb("a_neg", [P, GN, GN, HH])
        qk = ph.sb("qk", [P, GN, GN, HH])
        qd = ph.sb("qd", [P, GN, GN, HH])
        z = ph.sb("z", [P, GN, HH, 2, HD])
        total = ph.sb("total", [P, HH * 2 * HD])
        oq = ph.sb("oq", [P, GN, HH, 2, HD])
        dprod = ph.sb("dprod", [P, GN * 2 * HW])
        pprod = ph.sb("pprod", [P, 2, GN * 2 * HW])
        out1 = ph.sb("out1", [P, 2, HH, 3, GN, HD])
        out2 = ph.sb("out2", [P, 2, VQ, HH, REC2])

        gate = ph.sem("gate")
        cleared = ph.sem("cleared")
        landed = ph.transfers("landed", 5)
        decays = ph.steps("decays", GN + 3)
        kks = ph.steps("kks", 2 * (GN - 1) + 1)
        qks = ph.steps("qks", GN + 1)
        zs = ph.steps("zs", 3 * (GN - 1))
        oqs = ph.steps("oqs", GN)
        qk_prods = ph.steps("qk_prods", GN)
        rhs = ph.steps("rhs", 2)
        o_prods = ph.steps("o_prods", GN)
        kqs = ph.steps("kqs", 3)
        packed = ph.steps("packed", 2 + 2 * VQ)
        stored = ph.transfers("stored", 2)
        block = ph.block()

        @block.sync
        def _(sp):
            for s in (landed, stored):
                s.prime(sp)

            def load(r):
                p = r % 2
                sp.wait_ge(kqs.sem, kqs.before(r))
                rows = proj[r // 2 * GN * P:(r // 2 + 1) * GN * P, :].rearrange("(n t) c -> n t c", t=GN)
                for i in range(3):
                    sp.dma_start(raw[:, p, :, i, :], rows[:, :, i * D + p * HW:i * D + (p + 1) * HW]).then_inc(landed.sems[p], 32)
                for i in range(2):
                    c = 3 * D + i * H + p * HH
                    sp.dma_start(bg[:, p, :, i, :], rows[:, :, c:c + HH]).then_inc(landed.sems[p], 32)

            def store(r):
                p = r % 2
                sp.wait_ge(kqs.sem, kqs.at(r))
                sp.wait_ge(packed.sem, packed.at(r))
                b, first = r // 2 // (NBK // P), r // 2 % (NBK // P) * P
                sp.dma_start(rec1[first:first + P, b, p * HH:(p + 1) * HH, :],
                                            out1[:, p, :, :, :, :].rearrange("q h a t k -> q h (a t k)")).then_inc(stored.sems[p], 32)
                sp.dma_start(rec2[first:first + P, :, b, p * HH:(p + 1) * HH, :], out2[:, p, :, :, :]).then_inc(stored.sems[p], 32)
            load(0)
            for r in range(ROUNDS):
                if r + 1 < ROUNDS:
                    load(r + 1)
                store(r)
            for r in (ROUNDS - 2, ROUNDS - 1):
                sp.wait_ge(stored.sems[r % 2], stored.at(r, r % 2))

        @block.vector
        def _(v):
            for s in (decays, kks, qks, zs, oqs):
                s.prime(v)
            v.memset(decay[:, :, :, :], 0.0).then_inc(cleared, 1)
            v.memset(kk[:, :, :, :], 0.0).then_inc(cleared, 1)
            v.memset(qk[:, :, :, :], 0.0).then_inc(cleared, 1)
            v.wait_ge(cleared, 3)
            for t in range(GN):
                v.memset(decay[:, t, t, :], 1.0).then_inc(cleared, 1)
            v.wait_ge(cleared, 3 + GN)

            def one_round(r, p):
                k = raw[:, p, :, 1, :]
                beta, g = bg[:, p, :, 0, :], bg[:, p, :, 1, :]
                v.wait_ge(landed.sems[p], landed.at(r, p))
                v.wait_ge(kqs.sem, kqs.before(r, 1))
                v.wait_ge(packed.sem, packed.before(r, 1))
                for t in range(1, GN):
                    if t > 1:
                        v.wait_ge(decays.sem, decays.at(r, t - 1))
                    v.tensor_tensor(decay[:, t, 0:t, :], decay[:, t - 1, 0:t, :],
                                    g[:, t:t + 1, :].to_broadcast([P, t, HH]), ALU.mult).then_inc(decays.sem, 1)
                v.wait_ge(decays.sem, decays.at(r, GN - 1))
                v.tensor_tensor(gam[:, :, :], decay[:, :, 0, :], g[:, 0:1, :].to_broadcast([P, GN, HH]),
                                ALU.mult).then_inc(decays.sem, 1)
                v.wait_ge(decays.sem, decays.at(r, GN))
                v.tensor_tensor(b_gam[:, :, :], gam[:, :, :], beta, ALU.mult).then_inc(decays.sem, 1)
                v.tensor_scalar(neg_b[:, :, :], beta, -1.0, None, ALU.mult).then_inc(decays.sem, 1)
                v.wait_ge(decays.sem, decays.at(r, GN + 2))
                v.tensor_tensor(neg_bd[:, :, :, :], decay[:, :, :, :],
                                neg_b[:, :, :].unsqueeze(2).to_broadcast([P, GN, GN, HH]), ALU.mult).then_inc(decays.sem, 1)
                for t in range(1, GN):
                    if t > 1:
                        v.wait_ge(kks.sem, kks.at(r, 2 * (t - 1)))
                    prod = dprod[:, 0:t * HW].rearrange("q (i c) -> q i c", i=t)
                    v.tensor_tensor(prod, k[:, 0:t, :], k[:, t:t + 1, :].to_broadcast([P, t, HW]), ALU.mult).then_inc(kks.sem, 1)
                    v.wait_ge(kks.sem, kks.at(r, 2 * t - 1))
                    v.tensor_reduce(kk[:, t, 0:t, :], dprod[:, 0:t * HW].rearrange("q (i h d) -> q i h d", i=t, h=HH),
                                    X, ALU.add).then_inc(kks.sem, 1)
                v.wait_ge(decays.sem, decays.at(r))
                v.wait_ge(kks.sem, kks.at(r, 2 * (GN - 1)))
                v.tensor_tensor(a_neg[:, :, :, :], kk[:, :, :, :], neg_bd[:, :, :, :], ALU.mult).then_inc(kks.sem, 1)
                for t in range(GN):
                    v.wait_ge(qk_prods.sem, qk_prods.at(r, t + 1))
                    v.tensor_reduce(qk[:, t, 0:t + 1, :],
                                    pprod[:, t % 2, 0:(t + 1) * HW].rearrange("q (i h d) -> q i h d", i=t + 1, h=HH),
                                    X, ALU.add).then_inc(qks.sem, 1)
                v.wait_ge(qks.sem, qks.at(r, GN))
                v.tensor_tensor(qd[:, :, :, :], qk[:, :, :, :], decay[:, :, :, :], ALU.mult).then_inc(qks.sem, 1)

                def sum_outputs(t):
                    v.wait_ge(o_prods.sem, o_prods.at(r, t + 1))
                    v.tensor_reduce(oq[:, t, :, :, :].rearrange("q h a d -> q (h a d)"),
                                    pprod[:, t % 2, 0:(t + 1) * 2 * HW].rearrange("q (i c) -> q c i", i=t + 1),
                                    X, ALU.add).then_inc(oqs.sem, 1)
                v.wait_ge(rhs.sem, rhs.at(r))
                v.wait_ge(kks.sem, kks.at(r))
                for t in range(1, GN):
                    if t > 1:
                        v.wait_ge(zs.sem, zs.at(r, 3 * (t - 1)))
                    v.tensor_tensor(dprod[:, 0:t * 2 * HW].rearrange("q (i h c) -> q i h c", i=t, h=HH),
                                    z[:, 0:t, :, :, :].rearrange("q i h a d -> q i h (a d)"),
                                    a_neg[:, t, 0:t, :].unsqueeze(3).to_broadcast([P, t, HH, 2 * HD]),
                                    ALU.mult).then_inc(zs.sem, 1)
                    v.wait_ge(zs.sem, zs.at(r, 3 * t - 2))
                    v.tensor_reduce(total[:, :], dprod[:, 0:t * 2 * HW].rearrange("q (i c) -> q c i", i=t),
                                    X, ALU.add).then_inc(zs.sem, 1)
                    v.wait_ge(zs.sem, zs.at(r, 3 * t - 1))
                    row = z[:, t, :, :, :].rearrange("q h a d -> q (h a d)")
                    v.tensor_tensor(row, row, total[:, :], ALU.add).then_inc(zs.sem, 1)
                    if t > 1:
                        sum_outputs(t - 2)
                sum_outputs(GN - 2)
                sum_outputs(GN - 1)
            staged(v, ROUNDS, one_round)

        @block.gpsimd
        def _(pool):
            for s in (qk_prods, rhs, o_prods, kqs):
                s.prime(pool)

            def one_round(r, p):
                q, k, v_in = raw[:, p, :, 0, :], raw[:, p, :, 1, :], raw[:, p, :, 2, :]
                beta = bg[:, p, :, 0, :]
                pool.wait_ge(landed.sems[p], landed.at(r, p))

                def multiply_qk(t):
                    if t < 2:
                        pool.wait_ge(oqs.sem, oqs.before(r, 1))
                    else:
                        pool.wait_ge(qks.sem, qks.at(r, t - 1))
                    pool.tensor_tensor(pprod[:, t % 2, 0:(t + 1) * HW].rearrange("q (i c) -> q i c", i=t + 1),
                                       k[:, 0:t + 1, :], q[:, t:t + 1, :].to_broadcast([P, t + 1, HW]),
                                       ALU.mult).then_inc(qk_prods.sem, 1)

                def by_head(x):
                    return x.rearrange("q t (h d) -> q t h d", h=HH)

                def wide(x):
                    return x.unsqueeze(3).to_broadcast([P, GN, HH, HD])
                multiply_qk(0)
                multiply_qk(1)
                pool.wait_ge(packed.sem, packed.before(r, 1))
                pool.tensor_tensor(z[:, :, :, 0, :], by_head(v_in), wide(beta), ALU.mult).then_inc(rhs.sem, 1)
                pool.wait_ge(decays.sem, decays.at(r))
                pool.tensor_tensor(z[:, :, :, 1, :], by_head(k), wide(b_gam[:, :, :]), ALU.mult).then_inc(rhs.sem, 1)
                for t in range(2, GN):
                    multiply_qk(t)
                pool.wait_ge(stored.sems[p], stored.before(r, p))
                pool.tensor_tensor(out1[:, p, :, 1, :, :].rearrange("q h t d -> q t h d"), by_head(k),
                                   wide(decay[:, GN - 1, :, :]), ALU.mult).then_inc(kqs.sem, 1)
                q_out = out1[:, p, :, 2, :, :].rearrange("q h t d -> q t h d")
                pool.tensor_tensor(q_out, by_head(q), wide(gam[:, :, :]), ALU.mult).then_inc(kqs.sem, 1)
                pool.wait_ge(qks.sem, qks.at(r))
                pool.wait_ge(rhs.sem, rhs.at(r))
                for t in range(GN):
                    if t:
                        pool.wait_ge(zs.sem, zs.at(r, 3 * t))
                    if t > 1:
                        pool.wait_ge(oqs.sem, oqs.at(r, t - 1))
                    pool.tensor_tensor(pprod[:, t % 2, 0:(t + 1) * 2 * HW].rearrange("q (i h c) -> q i h c", i=t + 1, h=HH),
                                       z[:, 0:t + 1, :, :, :].rearrange("q i h a d -> q i h (a d)"),
                                       qd[:, t, 0:t + 1, :].unsqueeze(3).to_broadcast([P, t + 1, HH, 2 * HD]),
                                       ALU.mult).then_inc(o_prods.sem, 1)
                pool.wait_ge(oqs.sem, oqs.at(r))
                pool.wait_ge(kqs.sem, kqs.at(r, 2))
                pool.tensor_tensor(q_out, q_out, oq[:, :, :, 1, :], ALU.subtract).then_inc(kqs.sem, 1)
            staged(pool, ROUNDS, one_round)

        @block.scalar
        def _(act):
            packed.prime(act)

            def pack(r, p):
                act.wait_ge(stored.sems[p], stored.before(r, p))
                act.wait_ge(decays.sem, decays.at(r))
                nc.scalar.copy(out2[:, p, :, :, UW], gam[:, GN - 1:GN, :].to_broadcast([P, VQ, HH])).then_inc(packed.sem, 1)
                act.wait_ge(zs.sem, zs.at(r))
                act.wait_ge(rhs.sem, rhs.at(r))
                nc.scalar.mul(out1[:, p, :, 0, :, :], z[:, :, :, 1, :].rearrange("q t h d -> q h t d"), -1.0).then_inc(packed.sem, 1)
                for a, src in ((0, z), (1, oq)):
                    if a:
                        act.wait_ge(oqs.sem, oqs.at(r))
                    for w in range(VQ):
                        nc.scalar.copy(
                            out2[:, p, w, :, a * (UW + 1):a * (UW + 1) + UW].rearrange("q h (t v) -> q h t v", t=GN),
                            src[:, :, :, 0, w * V4:(w + 1) * V4].rearrange("q t h v -> q h t v")).then_inc(packed.sem, 1)
            staged(act, ROUNDS, pack)


CB = P // GN


def phase_chain(nc, sems, rec1, rec2, o_dram, ident):
    N = NBK // CB
    V2 = V4 // 2
    with Phase(nc, "chain", sems) as ph:
        r1 = ph.sb("r1", [P, 2, CB, 3, GN, HD])
        r2 = ph.sb("r2", [P, 2, CB, UW + 1])
        own = ph.sb("own", [P, 2, CB * GN, V4])
        state = ph.sb("state", [P, 2, V4, HD])
        terms1 = ph.sb("terms1", [P, 2, GN, V4, HD + 1])
        terms2 = ph.sb("terms2", [P, 2, GN + 1, V4, HD])
        u = ph.sb("u", [P, GN, V4])
        terms3 = ph.sb("terms3", [P, 2, CB * GN, V4, HD])
        o_out = ph.sb("o_out", [P, 2, B, D])
        ps = [ph.ps(f"ps{i}", [P, 512]) for i in range(2)]

        gate = ph.sem("gate")
        cleared = ph.sem("cleared")
        landed = ph.transfers("landed", VQ + 2)
        chain = ph.steps("chain", 8 * CB)
        u_put = ph.steps("u_put", CB)
        decayed = ph.steps("decayed", CB)
        q_prods = ph.steps("q_prods", CB)
        summed = ph.steps("summed")
        o_ready = ph.steps("o_ready", B)
        stored = ph.transfers("stored", B)
        block = ph.block()

        @block.sync
        def _(sp):
            for s in (landed, stored):
                s.prime(sp)

            def load(t, p):
                sp.wait_ge(chain.sem, chain.before(t))
                hold(sp, gate)
                sp.wait_ge(summed.sem, summed.before(t))
                hold(sp, gate)
                rows = bass.ds(t * CB, CB)
                for w in range(VQ):
                    sp.dma_start(r1[w * B * H:(w + 1) * B * H, p, :, :, :, :].rearrange("q n a t k -> q n (a t k)"),
                                                rec1[rows, :, :, :].rearrange("n b h c -> (b h) n c")).then_inc(landed.sems[p], 32)
                sp.dma_start(r2[:, p, :, :], rec2[rows, :, :, :, 0:UW + 1].rearrange("n w b h c -> (w b h) n c")).then_inc(landed.sems[p], 32)
                sp.dma_start(own[:, p, :, :].rearrange("q (n t) v -> q n (t v)", n=CB),
                                            rec2[rows, :, :, :, UW + 1:REC2].rearrange("n w b h c -> (w b h) n c")).then_inc(landed.sems[p], 32)

            def idle(t, p):
                pass

            def store(t, p):
                sp.wait_ge(o_ready.sem, o_ready.at(t))
                hold(sp, gate)
                for b in range(B):
                    sp.dma_start(o_dram[bass.ds(t * P + b * S, P), :], o_out[:, p, b, :]).then_inc(stored.sems[p], 32)
            staged(sp, N, load, idle, store)
            for t in (N - 2, N - 1):
                sp.wait_ge(stored.sems[t % 2], stored.at(t, t % 2))

        @block.vector
        def _(v):
            chain.prime(v)
            v.memset(state[:, 0, :, :], 0.0).then_inc(cleared, 1)
            v.wait_ge(cleared, 1)

            def chunk(t, p):
                v.wait_ge(landed.sems[p], landed.at(t, p))
                for c in range(CB):
                    i = c % 2
                    halves = [slice(s * V2, (s + 1) * V2) for s in range(2)]
                    for s, vs in enumerate(halves):
                        if c:
                            v.wait_ge(chain.sem, chain.at(t, 8 * c - 1 + s))
                        else:
                            v.wait_ge(chain.sem, chain.before(t, 1) - 1 + s)
                        v.tensor_tensor(terms1[:, i, :, vs, 0:HD],
                                        state[:, i, vs, :].unsqueeze(1).to_broadcast([P, GN, V2, HD]),
                                        r1[:, p, c, 0, :, :].unsqueeze(2).to_broadcast([P, GN, V2, HD]),
                                        ALU.mult).then_inc(chain.sem, 1)
                    for s, vs in enumerate(halves):
                        v.wait_ge(chain.sem, chain.at(t, 8 * c + 1 + s))
                        v.wait_ge(u_put.sem, u_put.at(t, c + 1))
                        v.tensor_reduce(u[:, :, vs], terms1[:, i, :, vs, :], X, ALU.add).then_inc(chain.sem, 1)
                    for s, vs in enumerate(halves):
                        v.wait_ge(chain.sem, chain.at(t, 8 * c + 3 + s))
                        v.tensor_tensor(terms2[:, i, 0:GN, vs, :],
                                        u[:, :, vs].unsqueeze(3).to_broadcast([P, GN, V2, HD]),
                                        r1[:, p, c, 1, :, :].unsqueeze(2).to_broadcast([P, GN, V2, HD]),
                                        ALU.mult).then_inc(chain.sem, 1)
                    for s, vs in enumerate(halves):
                        v.wait_ge(chain.sem, chain.at(t, 8 * c + 5 + s))
                        v.wait_ge(decayed.sem, decayed.at(t, c + 1))
                        if c:
                            v.wait_ge(q_prods.sem, q_prods.at(t, c))
                        else:
                            v.wait_ge(q_prods.sem, q_prods.before(t, 1))
                        v.tensor_reduce(state[:, 1 - i, vs, :].rearrange("q v k -> q (v k)"),
                                        terms2[:, i, :, vs, :].rearrange("q t v k -> q (v k) t"), X, ALU.add).then_inc(chain.sem, 1)
            staged(v, N, chunk)

        @block.gpsimd
        def _(pool):
            q_prods.prime(pool)
            pool.wait_ge(cleared, 1)

            def chunk(t, p):
                pool.wait_ge(landed.sems[p], landed.at(t, p))
                pool.wait_ge(summed.sem, summed.before(t))
                for c in range(CB):
                    if c:
                        pool.wait_ge(chain.sem, chain.at(t, 8 * c))
                    else:
                        pool.wait_ge(chain.sem, chain.before(t, 1))
                    pool.tensor_tensor(terms3[:, p, c * GN:(c + 1) * GN, :, :],
                                       state[:, c % 2, :, :].unsqueeze(1).to_broadcast([P, GN, V4, HD]),
                                       r1[:, p, c, 2, :, :].unsqueeze(2).to_broadcast([P, GN, V4, HD]),
                                       ALU.mult).then_inc(q_prods.sem, 1)
            staged(pool, N, chunk)

        @block.tensor
        def _(pe):
            summed.prime(pe)

            def chunk(t, p):
                pe.wait_ge(q_prods.sem, q_prods.at(t))
                pe.wait_ge(o_ready.sem, o_ready.before(t))
                for j in range(V4):
                    out = ps[p][:, j * P:(j + 1) * P]
                    for k in range(HD):
                        pe.matmul(out, terms3[:, p, :, j, k], ident[:, :], start=(k == 0), stop=False)
                    mm = pe.matmul(out, own[:, p, :, j], ident[:, :], start=False, stop=True)
                mm.then_inc(summed.sem, 1)
            staged(pe, N, chunk)

        @block.scalar
        def _(act):
            for s in (u_put, decayed, o_ready):
                s.prime(act)
            act.wait_ge(cleared, 1)

            def chunk(t, p):
                act.wait_ge(landed.sems[p], landed.at(t, p))
                for c in range(CB):
                    i = c % 2
                    if c > 1:
                        act.wait_ge(chain.sem, chain.at(t, 8 * (c - 1) - 4))
                    elif c:
                        act.wait_ge(chain.sem, chain.at(t, 0))
                    else:
                        act.wait_ge(chain.sem, chain.before(t, 1))
                    nc.scalar.copy(terms1[:, i, :, :, HD], r2[:, p, c, 0:UW].rearrange("q (t v) -> q t v", t=GN)).then_inc(u_put.sem, 1)
                    if c:
                        act.wait_ge(chain.sem, chain.at(t, 8 * c))
                    nc.scalar.activation(terms2[:, i, GN, :, :], state[:, i, :, :], ACT.Copy,
                                         scale=r2[:, p, c, UW:UW + 1]).then_inc(decayed.sem, 1)

            def keep(t, p):
                act.wait_ge(summed.sem, summed.at(t))
                act.wait_ge(stored.sems[p], stored.before(t, p))
                for b in range(B):
                    nc.scalar.copy(o_out[:, p, b, :].rearrange("q (h w v) -> q h w v", h=H, w=VQ),
                                   ps[p][:, :].rearrange("q (v w b h) -> q b h w v", v=V4, w=VQ, b=B)[:, b]).then_inc(o_ready.sem, 1)
            staged(act, N, chunk, keep)


FB = 4 * D // P


def phase_mlp(nc, sems, o_dram, x_sb, z_sb, wo, bo, ln_g, ln_b, w1, b1, w2, b2, norm_g, norm_b, ident):
    N = NT // GT
    with Phase(nc, "mlp", sems) as ph:
        wo_sb = ph.sb("wo_sb", [P, KD, D])
        w1_sb = ph.sb("w1_sb", [P, KD, FB, P])
        w2_sb = ph.sb("w2_sb", [P, FB, D])
        g_col = ph.sb("g_col", [P, KD])
        b_col = ph.sb("b_col", [P, KD])
        b1_col = ph.sb("b1_col", [P, FB])
        rows = ph.sb("rows", [P, 4, D])
        neg_half = ph.sb("neg_half", [P, GT])
        o_in = ph.sb("o_in", [P, 2, GT, D])
        o_t = ph.sb("o_t", [P, 2, KD, GP])
        y = ph.sb("y", [P, 2, GT, D])
        base = ph.sb("base", [P, 2, GT, D])
        hn = ph.sb("hn", [P, 2, GT, D])
        h_t = ph.sb("h_t", [P, 2, KD, GP])
        hidden = ph.sb("hidden", [P, FB, GP])
        x3 = ph.sb("x3", [P, 2, GT, D])
        w = ph.sb("w", [P, 2, GT, D])
        xn = ph.sb("xn", [P, 2, GT, D])
        stats = ph.sb("stats", [P, 3, GT, 6])
        mv = ph.sb("mv", [P, 3, GT, 2])
        veps = ph.sb("veps", [P, 3, GT])
        rstd = ph.sb("rstd", [P, 3, GT])
        ps_ot = ph.ps("ps_ot", [P, GP])
        ps_ht = ph.ps("ps_ht", [P, GP])
        ps_y = ph.ps("ps_y", [P, GT, D])
        ps_1 = [ph.ps(f"ps_1{i}", [P, GP]) for i in range(2)]
        ps_2 = ph.ps("ps_2", [P, GT, D])

        gate = ph.sem("gate")
        consts_in = ph.sem("consts_in")
        set_up = ph.sem("set_up")
        shifted = ph.sem("shifted")
        b1_ready = ph.sem("b1_ready")
        scaled = ph.sem("scaled")
        o_landed = ph.transfers("o_landed")
        o_turned = ph.steps("o_turned", KD)
        o_kept = ph.steps("o_kept", KD)
        wo_done = ph.steps("wo_done")
        ys = ph.steps("ys", 2)
        bases = ph.steps("bases", 2)
        norm_h = ph.steps("norm_h", LN)
        norm_w = ph.steps("norm_w", LN)
        norm_x = ph.steps("norm_x", LN)
        root_h = ph.steps("root_h")
        root_w = ph.steps("root_w")
        root_x = ph.steps("root_x")
        h_turned = ph.steps("h_turned", KD)
        h_kept = ph.steps("h_kept", KD)
        up = ph.steps("up", FB)
        gelu = ph.steps("gelu", FB)
        down = ph.steps("down")
        x3s = ph.steps("x3s")
        x3_kept = ph.steps("x3_kept")
        affine = ph.steps("affine", 2)
        block = ph.block()

        @block.sync
        def _(sp):
            o_landed.prime(sp)
            sp.dma_start(w1_sb[:, :, :, :].rearrange("q k f c -> q k (f c)"), w1.rearrange("(k p) c -> p k c", p=P)).then_inc(consts_in, 16)
            sp.dma_start(wo_sb[:, :, :], wo.rearrange("(k p) c -> p k c", p=P)).then_inc(consts_in, 16)
            sp.dma_start(w2_sb[:, :, :], w2.rearrange("(f p) c -> p f c", p=P)).then_inc(consts_in, 16)
            for i, vec in enumerate((bo, b2, norm_g, norm_b)):
                sp.dma_start(rows[:, i, :], row_broadcast(vec)).then_inc(consts_in, 16)
            with nc.allow_non_contiguous_dma("short columns"):
                sp.dma_start(g_col[:, :], ln_g.rearrange("(k p) -> p k", p=P)).then_inc(consts_in, 16)
                sp.dma_start(b_col[:, :], ln_b.rearrange("(k p) -> p k", p=P)).then_inc(consts_in, 16)
                sp.dma_start(b1_col[:, :], b1.rearrange("(f p) -> p f", p=P)).then_inc(consts_in, 16)

            def load(t, p):
                sp.wait_ge(o_turned.sem, o_turned.before(t))
                hold(sp, gate)
                sp.dma_start(o_in[:, p, :, :], o_dram[bass.ds(t * GP, GP), :].rearrange("(n q) c -> q n c", q=P)).then_inc(o_landed.sems[p], 32)
            staged(sp, N, load)

        @block.tensor
        def _(pe):
            for s in (o_turned, wo_done, h_turned, up, down):
                s.prime(pe)
            pe.wait_ge(consts_in, 16 * 10)
            for f in range(FB):
                for k in range(KD):
                    mm = pe.matmul(ps_1[0][:, f:f + 1], w1_sb[:, k, f, :], b_col[:, k:k + 1], start=(k == 0), stop=(k == KD - 1))
            mm.then_inc(shifted, 1)
            pe.wait_ge(scaled, KD)

            def turn_o(t, p):
                pe.wait_ge(o_landed.sems[p], o_landed.at(t, p))
                for k in range(KD):
                    if k:
                        pe.wait_ge(o_kept.sem, o_kept.at(t, k))
                    else:
                        pe.wait_ge(o_kept.sem, o_kept.before(t, 1))
                    for i in range(GT):
                        mm = pe.transpose(ps_ot[:, i * P:(i + 1) * P], o_in[:, p, i, k * P:(k + 1) * P], ident[:, :])
                    mm.then_inc(o_turned.sem, 1)

            def project(t, p):
                pe.wait_ge(o_kept.sem, o_kept.at(t))
                pe.wait_ge(ys.sem, ys.before(t, 1))
                for i in range(GT):
                    for k in range(KD):
                        mm = pe.matmul(ps_y[:, i, :], o_t[:, p, k, i * P:(i + 1) * P], wo_sb[:, k, :], start=(k == 0), stop=(k == KD - 1))
                mm.then_inc(wo_done.sem, 1)

            def turn_h(t, p):
                pe.wait_ge(norm_h.sem, norm_h.at(t))
                for k in range(KD):
                    if k:
                        pe.wait_ge(h_kept.sem, h_kept.at(t, k))
                    else:
                        pe.wait_ge(h_kept.sem, h_kept.before(t, 1))
                    for i in range(GT):
                        mm = pe.transpose(ps_ht[:, i * P:(i + 1) * P], hn[:, p, i, k * P:(k + 1) * P], ident[:, :])
                    mm.then_inc(h_turned.sem, 1)

            def mlp(t, p):
                pe.wait_ge(h_kept.sem, h_kept.at(t))
                for f in range(FB):
                    if f > 1:
                        pe.wait_ge(gelu.sem, gelu.at(t, f - 1))
                    else:
                        pe.wait_ge(gelu.sem, gelu.before(t, 1))
                    for k in range(KD):
                        mm = pe.matmul(ps_1[f % 2][:, :], w1_sb[:, k, f, :], h_t[:, p, k, :], start=(k == 0), stop=(k == KD - 1))
                    mm.then_inc(up.sem, 1)
                pe.wait_ge(gelu.sem, gelu.at(t))
                pe.wait_ge(x3s.sem, x3s.before(t, 1))
                for i in range(GT):
                    for f in range(FB):
                        mm = pe.matmul(ps_2[:, i, :], hidden[:, f, i * P:(i + 1) * P], w2_sb[:, f, :], start=(f == 0), stop=(f == FB - 1))
                mm.then_inc(down.sem, 1)
            staged(pe, N, turn_o, project, turn_h, mlp)

        @block.scalar
        def _(act):
            for s in (o_kept, h_kept, gelu, x3_kept):
                s.prime(act)
            act.wait_ge(b1_ready, 1)

            def keep_o(t, p):
                act.wait_ge(wo_done.sem, wo_done.before(t))
                for k in range(KD):
                    act.wait_ge(o_turned.sem, o_turned.at(t, k + 1))
                    nc.scalar.copy(o_t[:, p, k, :], ps_ot[:, :]).then_inc(o_kept.sem, 1)

            def idle(t, p):
                pass

            def keep_h(t, p):
                act.wait_ge(up.sem, up.before(t))
                for k in range(KD):
                    act.wait_ge(h_turned.sem, h_turned.at(t, k + 1))
                    nc.scalar.copy(h_t[:, p, k, :], ps_ht[:, :]).then_inc(h_kept.sem, 1)

            def activate(t, p):
                act.wait_ge(down.sem, down.before(t, 1))
                for f in range(FB):
                    act.wait_ge(up.sem, up.at(t, f + 1))
                    nc.scalar.activation(hidden[:, f, :], ps_1[f % 2][:, :], ACT.Gelu, bias=b1_col[:, f:f + 1]).then_inc(gelu.sem, 1)

            def keep_x(t, p):
                act.wait_ge(x3s.sem, x3s.at(t))
                hold(act, gate)
                nc.scalar.copy(flat(x_sb[:, bass.ds(t * GT, GT), :]), flat(x3[:, p, :, :])).then_inc(x3_kept.sem, 1)
            staged(act, N, keep_o, idle, keep_h, activate, keep_x)

        @block.vector
        def _(v):
            for s in (ys, norm_h, norm_w, norm_x, x3s):
                s.prime(v)
            v.wait_ge(shifted, 1)
            v.tensor_tensor(b1_col[:, :], ps_1[0][:, 0:FB], b1_col[:, :], ALU.add).then_inc(b1_ready, 1)
            for k in range(KD):
                part = w1_sb[:, k, :, :].rearrange("q f c -> q (f c)")
                v.tensor_scalar(part, part, g_col[:, k:k + 1], None, ALU.mult).then_inc(scaled, 1)

            def idle(t, p):
                pass

            def first(t, p):
                v.wait_ge(wo_done.sem, wo_done.at(t))
                v.wait_ge(bases.sem, bases.before(t))
                hold(v, gate)
                v.tensor_tensor(flat(y[:, p, :, :]), flat(ps_y[:, :, :]), flat(z_sb[:, bass.ds(t * GT, GT), :]), ALU.add).then_inc(ys.sem, 1)
                v.wait_ge(ys.sem, ys.at(t, 1))
                v.tensor_tensor(y[:, p, :, :], y[:, p, :, :], rows[:, 0:1, :].to_broadcast([P, GT, D]), ALU.add).then_inc(ys.sem, 1)
                v.wait_ge(ys.sem, ys.at(t))
                v.wait_ge(h_turned.sem, h_turned.before(t))
                layer_norm(v, t, norm_h, root_h, y[:, p], hn[:, p], stats[:, 0], mv[:, 0], veps[:, 0, :], rstd[:, 0, :], gate)

            def last(t, p):
                v.wait_ge(down.sem, down.at(t))
                v.wait_ge(bases.sem, bases.at(t))
                v.wait_ge(x3_kept.sem, x3_kept.before(t))
                v.tensor_tensor(flat(x3[:, p, :, :]), flat(ps_2[:, :, :]), flat(base[:, p, :, :]), ALU.add).then_inc(x3s.sem, 1)
                v.wait_ge(x3s.sem, x3s.at(t))
                layer_norm(v, t, norm_w, root_w, x3[:, p], w[:, p], stats[:, 1], mv[:, 1], veps[:, 1, :], rstd[:, 1, :], gate)
                v.wait_ge(norm_w.sem, norm_w.at(t))
                v.wait_ge(affine.sem, affine.before(t))
                layer_norm(v, t, norm_x, root_x, w[:, p], xn[:, p], stats[:, 2], mv[:, 2], veps[:, 2, :], rstd[:, 2, :], gate)
            staged(v, N, idle, first, idle, last)

        @block.gpsimd
        def _(pool):
            for s in (bases, root_h, root_w, root_x, affine):
                s.prime(pool)
            pool.memset(neg_half[:, :], -0.5).then_inc(set_up, 1)
            pool.wait_ge(set_up, 1)
            pool.wait_ge(consts_in, 16 * 10)

            def root(t, i, norm, roots):
                pool.wait_ge(norm.sem, norm.at(t, 2 * GT + 1))
                pool.tensor_tensor(rstd[:, i, :], veps[:, i, :], neg_half[:, :], ALU.pow).then_inc(roots.sem, 1)

            def idle(t, p):
                pass

            def first(t, p):
                root(t, 0, norm_h, root_h)
                pool.wait_ge(ys.sem, ys.at(t))
                pool.wait_ge(x3s.sem, x3s.before(t))
                hold(pool, gate)
                pool.tensor_tensor(flat(base[:, p, :, :]), flat(y[:, p, :, :]), flat(x_sb[:, bass.ds(t * GT, GT), :]), ALU.add).then_inc(bases.sem, 1)
                pool.wait_ge(bases.sem, bases.at(t, 1))
                pool.tensor_tensor(base[:, p, :, :], base[:, p, :, :], rows[:, 1:2, :].to_broadcast([P, GT, D]), ALU.add).then_inc(bases.sem, 1)

            def last(t, p):
                root(t, 1, norm_w, root_w)
                root(t, 2, norm_x, root_x)
                pool.wait_ge(norm_x.sem, norm_x.at(t))
                pool.tensor_tensor(xn[:, p, :, :], xn[:, p, :, :], rows[:, 2:3, :].to_broadcast([P, GT, D]), ALU.mult).then_inc(affine.sem, 1)
                pool.wait_ge(affine.sem, affine.at(t, 1))
                hold(pool, gate)
                pool.tensor_tensor(z_sb[:, bass.ds(t * GT, GT), :], xn[:, p, :, :], rows[:, 3:4, :].to_broadcast([P, GT, D]), ALU.add).then_inc(affine.sem, 1)
            staged(pool, N, idle, first, idle, last)


SE = 16
SPE = 64
NS = SE * SPE
JT = NS // P
F = 512
FT = F // P


def phase_soft_turn(nc, sems, xf_sb, xf_t, slot_embeds, slot_g, slot_b, scale, bg, bu, se_t, bias_cols, ident):
    N = NT // GT
    with Phase(nc, "sturn", sems) as ph:
        xs = ph.sb("xs", [P, 2, GT, D])
        se = ph.sb("se", [P, 2, GT, D])
        sn = ph.sb("sn", [P, 2, GT, D])
        rows = ph.sb("rows", [P, 2, D])
        scale_col = ph.sb("scale_col", [P, 1])
        neg_half = ph.sb("neg_half", [P, GT])
        bias_rows = ph.sb("bias_rows", [P, P])
        stats = ph.sb("stats", [P, GT, 6])
        mv = ph.sb("mv", [P, GT, 2])
        veps = ph.sb("veps", [P, GT])
        rstd = ph.sb("rstd", [P, GT])
        ps = [ph.ps(f"ps{i}", [P, KD, GP]) for i in range(2)]
        ps_b = ph.ps("ps_b", [P, P])

        gate = ph.sem("gate")
        consts_in = ph.sem("consts_in")
        set_up = ph.sem("set_up")
        fetched = ph.steps("fetched")
        turned = ph.steps("turned")
        kept = ph.steps("kept", KD)
        norm = ph.steps("norm", LN)
        roots = ph.steps("roots")
        affine = ph.steps("affine", 2)
        scaled = ph.steps("scaled")
        biases = ph.sem("biases")
        block = ph.block()
        HALVES = JT // GT

        @block.sync
        def _(sp):
            sp.dma_start(se[:, :, :, :].rearrange("q a n c -> q (a n) c"),
                         slot_embeds.rearrange("e s d -> (e s) d").rearrange("(n p) c -> p n c", p=P)).then_inc(consts_in, 16)
            sp.dma_start(rows[:, 0, :], row_broadcast(slot_g)).then_inc(consts_in, 16)
            sp.dma_start(rows[:, 1, :], row_broadcast(slot_b)).then_inc(consts_in, 16)
            sp.dma_start(scale_col[:, :], row_broadcast(scale)).then_inc(consts_in, 16)
            for i, vec in enumerate((bg, bu)):
                sp.dma_start(bias_rows[i * SE * FT:(i + 1) * SE * FT, :], vec.rearrange("e (f p) -> (e f) p", p=P)).then_inc(consts_in, 16)

        @block.scalar
        def _(act):
            fetched.prime(act)

            def fetch(t, p):
                act.wait_ge(turned.sem, turned.before(t))
                hold(act, gate)
                nc.scalar.copy(flat(xs[:, p]), flat(xf_sb[:, bass.ds(t * GT, GT), :])).then_inc(fetched.sem, 1)
            staged(act, N, fetch)

        @block.tensor
        def _(pe):
            turned.prime(pe)

            def turn_from(src, t, p):
                pe.wait_ge(kept.sem, kept.before(t))
                for k in range(KD):
                    for i in range(GT):
                        mm = pe.transpose(ps[p][:, k, i * P:(i + 1) * P], src[:, i, k * P:(k + 1) * P], ident[:, :])
                mm.then_inc(turned.sem, 1)

            def turn(t, p):
                pe.wait_ge(fetched.sem, fetched.at(t))
                turn_from(xs[:, p], t, p)
            staged(pe, N, turn)
            for a in range(HALVES):
                pe.wait_ge(scaled.sem, scaled.at(a))
                turn_from(sn[:, a], N + a, a)
            pe.wait_ge(consts_in, 16 * 6)
            pe.transpose(ps_b[:, :], bias_rows[:, :], ident[:, :]).then_inc(biases, 1)

        @block.vector
        def _(v):
            for s in (kept, norm, scaled):
                s.prime(v)

            def keep(t, p):
                v.wait_ge(turned.sem, turned.at(t))
                for k in range(KD):
                    hold(v, gate)
                    v.tensor_copy(xf_t[:, k, bass.ds(t * GP, GP)], ps[p][:, k, :]).then_inc(kept.sem, 1)
            staged(v, N, keep)
            v.wait_ge(consts_in, 16 * 6)
            for a in range(HALVES):
                layer_norm(v, a, norm, roots, se[:, a], sn[:, a], stats, mv, veps[:, :], rstd, gate)
                v.wait_ge(norm.sem, norm.at(a))
            for a in range(HALVES):
                v.wait_ge(affine.sem, affine.at(a))
                v.tensor_scalar(sn[:, a], sn[:, a], scale_col[:, 0:1], None, ALU.mult).then_inc(scaled.sem, 1)
            for a in range(HALVES):
                v.wait_ge(turned.sem, turned.at(N + a))
                for k in range(KD):
                    v.tensor_copy(se_t[:, k, a * GP:(a + 1) * GP], ps[a][:, k, :]).then_inc(kept.sem, 1)
            v.wait_ge(biases, 1)
            v.tensor_copy(bias_cols.rearrange("q a e f -> q (a e f)"), ps_b[:, :]).then_inc(biases, 1)

        @block.gpsimd
        def _(pool):
            for s in (roots, affine):
                s.prime(pool)
            pool.memset(neg_half[:, :], -0.5).then_inc(set_up, 1)
            pool.wait_ge(set_up, 1)
            pool.wait_ge(consts_in, 16 * 6)
            for a in range(HALVES):
                pool.wait_ge(norm.sem, norm.at(a, 2 * GT + 1))
                pool.tensor_tensor(rstd[:, :], veps[:, :], neg_half[:, :], ALU.pow).then_inc(roots.sem, 1)
            for a in range(HALVES):
                pool.wait_ge(norm.sem, norm.at(a))
                pool.tensor_tensor(sn[:, a], sn[:, a], rows[:, 0:1, :].to_broadcast([P, GT, D]), ALU.mult).then_inc(affine.sem, 1)
                pool.wait_ge(affine.sem, affine.at(a, 1))
                pool.tensor_tensor(sn[:, a], sn[:, a], rows[:, 1:2, :].to_broadcast([P, GT, D]), ALU.add).then_inc(affine.sem, 1)


def spread_column(pe, out, wide, ident):
    return pe.matmul(out, wide, ident[:, :], start=True, stop=True)


def phase_slot_stats(nc, sems, xf_t, se_t, neg_max, inv_sum, ident):
    TB = S // GP
    with Phase(nc, "sstat", sems) as ph:
        lhs = ph.sb("lhs", [P, 2, KD, P])
        logit = ph.sb("logit", [P, 2, TB, GP])
        max_col = ph.sb("max_col", [P, 2, 1])
        neg_col = ph.sb("neg_col", [P, 2, 1])
        inv_col = ph.sb("inv_col", [P, 2, 1])
        total = ph.sb("total", [P, 2, 1])
        wide = ph.sb("wide", [P, 2, 2, P])
        ps = [ph.ps(f"ps{i}", [P, GP]) for i in range(TB)]
        ps_r = [ph.ps(f"ps_r{i}", [P, GP]) for i in range(2)]

        gate = ph.sem("gate")
        fetched = ph.steps("fetched")
        logits = ph.steps("logits", TB)
        kept = ph.steps("kept", TB)
        maxima = ph.steps("maxima", 2)
        sums = ph.steps("sums")
        inverted = ph.steps("inverted")
        widened = ph.steps("widened", 2)
        spread = ph.steps("spread")
        rows_kept = ph.steps("rows_kept", 2)
        block = ph.block()

        def idle(t, p, b):
            pass

        def per_sequence(eng, *stages):
            for b in range(B):
                staged(eng, JT, *[lambda t, p, s=s: s(t, p, b) for s in stages], first=b * JT)

        @block.tensor
        def _(pe):
            for s in (logits, spread):
                s.prime(pe)

            def multiply(t, p, b):
                pe.wait_ge(fetched.sem, fetched.at(t))
                for i in range(TB):
                    pe.wait_ge(kept.sem, kept.at(t, i + 1 - TB))
                    for k in range(KD):
                        c = b * S + i * GP
                        mm = pe.matmul(ps[i][:, :], lhs[:, p, k, :], xf_t[:, k, c:c + GP], start=(k == 0), stop=(k == KD - 1))
                    mm.then_inc(logits.sem, 1)

            def turn(t, p, b):
                pe.wait_ge(widened.sem, widened.at(t))
                pe.wait_ge(rows_kept.sem, rows_kept.before(t))
                for i in range(2):
                    mm = spread_column(pe, ps_r[p][:, i * P:(i + 1) * P], wide[:, p, i, :], ident)
                mm.then_inc(spread.sem, 1)
            per_sequence(pe, multiply, idle, turn)

        @block.gpsimd
        def _(pool):
            for s in (fetched, widened):
                s.prime(pool)

            def fetch(t, p, b):
                pool.wait_ge(logits.sem, logits.before(t))
                hold(pool, gate)
                pool.tensor_copy(lhs[:, p, :, :], se_t[:, :, bass.ds(t * P - b * NS, P)]).then_inc(fetched.sem, 1)

            def widen(t, p, b):
                pool.wait_ge(spread.sem, spread.before(t))
                pool.wait_ge(inverted.sem, inverted.at(t))
                hold(pool, gate)
                pool.tensor_copy(wide[:, p, 0, :], neg_col[:, p, :].to_broadcast([P, P])).then_inc(widened.sem, 1)
                pool.tensor_copy(wide[:, p, 1, :], inv_col[:, p, :].to_broadcast([P, P])).then_inc(widened.sem, 1)
            per_sequence(pool, fetch, idle, widen)

        @block.vector
        def _(v):
            for s in (maxima, inverted):
                s.prime(v)

            def find_max(t, p, b):
                v.wait_ge(kept.sem, kept.at(t))
                hold(v, gate)
                v.tensor_reduce(max_col[:, p, :], logit[:, p, :, :].rearrange("q i c -> q (i c)"), X, ALU.max).then_inc(maxima.sem, 1)
                v.wait_ge(maxima.sem, maxima.at(t, 1))
                v.wait_ge(widened.sem, widened.before(t))
                v.tensor_scalar(neg_col[:, p, :], max_col[:, p, :], -1.0, None, ALU.mult).then_inc(maxima.sem, 1)

            def invert(t, p, b):
                v.wait_ge(sums.sem, sums.at(t))
                v.reciprocal(inv_col[:, p, :], total[:, p, :]).then_inc(inverted.sem, 1)
            per_sequence(v, find_max, invert)

        @block.scalar
        def _(act):
            for s in (kept, sums, rows_kept):
                s.prime(act)

            def keep(t, p, b):
                act.wait_ge(sums.sem, sums.before(t))
                for i in range(TB):
                    act.wait_ge(logits.sem, logits.at(t, i + 1))
                    nc.scalar.copy(logit[:, p, i, :], ps[i][:, :]).then_inc(kept.sem, 1)

            def add_up(t, p, b):
                act.wait_ge(maxima.sem, maxima.at(t))
                act.wait_ge(inverted.sem, inverted.before(t))
                act.wait_ge(kept.sem, kept.at(t))
                tile = logit[:, p, :, :].rearrange("q i c -> q (i c)")
                nc.scalar.activation(tile, tile, ACT.Exp,
                                     bias=neg_col[:, p, :], accum_out=total[:, p, :]).then_inc(sums.sem, 1)

            def keep_rows(t, p, b):
                act.wait_ge(spread.sem, spread.at(t))
                hold(act, gate)
                nc.scalar.copy(neg_max[:, bass.ds(t * P, P)], ps_r[p][:, 0:P]).then_inc(rows_kept.sem, 1)
                nc.scalar.copy(inv_sum[:, bass.ds(t * P, P)], ps_r[p][:, P:2 * P]).then_inc(rows_kept.sem, 1)
            per_sequence(act, keep, add_up, keep_rows)


def phase_dispatch(nc, sems, xf_sb, xf_t, se_t, neg_max, inv_sum, slots, token_neg_max, token_inv_sum):
    NB = NS // GP
    with Phase(nc, "disp", sems) as ph:
        lhs = ph.sb("lhs", [P, 2, KD, P])
        xs = ph.sb("xs", [P, 2, D])
        shifted = ph.sb("shifted", [P, 2, NS])
        probs = ph.sb("probs", [P, 2, NS])
        max_col = ph.sb("max_col", [P, 2, 1])
        neg_col = ph.sb("neg_col", [P, 2, 1])
        total = ph.sb("total", [P, 2, 1])
        ps_l = [ph.ps(f"ps_l{i}", [P, NS]) for i in range(2)]
        ps_s = ph.ps("ps_s", [P, KD, NS])

        gate = ph.sem("gate")
        fetched = ph.steps("fetched")
        xs_ready = ph.steps("xs_ready")
        logits = ph.steps("logits")
        shifts = ph.steps("shifts")
        exps = ph.steps("exps")
        maxima = ph.steps("maxima", 3)
        sums = ph.steps("sums")
        inverted = ph.steps("inverted")
        added = ph.steps("added")
        slots_kept = ph.sem("slots_kept")
        block = ph.block()

        def per_sequence(eng, *stages):
            for b in range(B):
                staged(eng, ST, *[lambda t, p, s=s: s(t, p, b) for s in stages], first=b * ST)

        def idle(t, p, b):
            pass

        @block.gpsimd
        def _(pool):
            fetched.prime(pool)
            xs_ready.prime(pool)

            def fetch(t, p, b):
                pool.wait_ge(logits.sem, logits.before(t))
                hold(pool, gate)
                pool.tensor_copy(lhs[:, p, :, :], xf_t[:, :, bass.ds(t * P, P)]).then_inc(fetched.sem, 1)
                pool.wait_ge(added.sem, added.before(t))
                hold(pool, gate)
                pool.tensor_copy(xs[:, p, :], flat(xf_sb[:, bass.ds(t, 1), :])).then_inc(xs_ready.sem, 1)
            per_sequence(pool, fetch)

        @block.tensor
        def _(pe):
            for s in (logits, added):
                s.prime(pe)

            def multiply(t, p, b):
                pe.wait_ge(fetched.sem, fetched.at(t))
                pe.wait_ge(shifts.sem, shifts.before(t))
                pe.wait_ge(sums.sem, sums.before(t))
                for n in range(NB):
                    for k in range(KD):
                        mm = pe.matmul(ps_l[p][:, n * GP:(n + 1) * GP], lhs[:, p, k, :], se_t[:, k, n * GP:(n + 1) * GP],
                                       start=(k == 0), stop=(k == KD - 1))
                mm.then_inc(logits.sem, 1)

            def add(t, p, b):
                first, last = [isinstance(t, int) and t == b * ST + n for n in (0, ST - 1)]
                pe.wait_ge(xs_ready.sem, xs_ready.at(t))
                pe.wait_ge(exps.sem, exps.at(t))
                if first and b:
                    pe.wait_ge(slots_kept, KD * b)
                for k in range(KD):
                    for n in range(NB):
                        mm = pe.matmul(ps_s[:, k, n * GP:(n + 1) * GP], xs[:, p, k * P:(k + 1) * P],
                                       probs[:, p, n * GP:(n + 1) * GP], start=first, stop=last)
                mm.then_inc(added.sem, 1)
            per_sequence(pe, multiply, add, idle)

        @block.vector
        def _(v):
            for s in (shifts, maxima, inverted):
                s.prime(v)

            def shift(t, p, b):
                v.wait_ge(logits.sem, logits.at(t))
                v.wait_ge(exps.sem, exps.before(t))
                v.tensor_tensor(shifted[:, p, :], ps_l[p][:, :], neg_max[:, b * NS:(b + 1) * NS], ALU.add).then_inc(shifts.sem, 1)
                v.tensor_reduce(max_col[:, p, :], ps_l[p][:, :], X, ALU.max).then_inc(maxima.sem, 1)
                v.wait_ge(maxima.sem, maxima.at(t, 1))
                v.wait_ge(sums.sem, sums.before(t))
                hold(v, gate)
                v.tensor_scalar(neg_col[:, p, :], max_col[:, p, :], -1.0, None, ALU.mult).then_inc(maxima.sem, 1)
                v.wait_ge(maxima.sem, maxima.at(t, 2))
                hold(v, gate)
                v.tensor_copy(token_neg_max[:, bass.ds(t, 1)], neg_col[:, p, :]).then_inc(maxima.sem, 1)

            def invert(t, p, b):
                v.wait_ge(sums.sem, sums.at(t))
                hold(v, gate)
                v.reciprocal(token_inv_sum[:, bass.ds(t, 1)], total[:, p, :]).then_inc(inverted.sem, 1)
            for b in range(B):
                staged(v, ST, *[lambda t, p, s=s: s(t, p, b) for s in (shift, invert)], first=b * ST)
                v.wait_ge(added.sem, added.at((b + 1) * ST - 1))
                for k in range(KD):
                    v.tensor_tensor(slots[:, k, :, b, :], ps_s[:, k, :].rearrange("q (e s) -> q e s", e=SE),
                                    inv_sum[:, b * NS:(b + 1) * NS].rearrange("q (e s) -> q e s", e=SE), ALU.mult).then_inc(slots_kept, 1)

        @block.scalar
        def _(act):
            for s in (exps, sums):
                s.prime(act)

            def exponent(t, p, b):
                act.wait_ge(shifts.sem, shifts.at(t))
                act.wait_ge(added.sem, added.before(t))
                nc.scalar.activation(probs[:, p, :], shifted[:, p, :], ACT.Exp).then_inc(exps.sem, 1)
                act.wait_ge(maxima.sem, maxima.at(t, 2))
                act.wait_ge(inverted.sem, inverted.before(t))
                nc.scalar.activation(ps_l[p][:, :], ps_l[p][:, :], ACT.Exp, bias=neg_col[:, p, :],
                                     accum_out=total[:, p, :]).then_inc(sums.sem, 1)
            per_sequence(act, exponent)


RING = 4


def load_soft_expert(sp, t, p, buffers, weights, landed):
    for dst, src in zip(buffers, weights):
        sp.dma_start(dst[:, p], src[bass.ds(t, 1), :, :].rearrange("a (k p) c -> p (a k) c", p=P)).then_inc(landed.sems[p], 32)


def phase_soft_experts(nc, sems, slots, bias_cols, buffers, weights, landed, bd, slots_out):
    wg_sb, wu_sb, wd_sb = buffers
    with Phase(nc, "sexp", sems) as ph:
        bd_sb = ph.sb("bd_sb", [P, JT, D])
        cols = ph.sb("cols", [P, 2, 2, FT])
        gated = ph.sb("gated", [P, 2, FT, P])
        hidden = ph.sb("hidden", [P, 2, FT, P])
        ps_g = [ph.ps(f"ps_g{i}", [P, FT, P]) for i in range(2)]
        ps_u = [ph.ps(f"ps_u{i}", [P, FT, P]) for i in range(2)]
        ps_o = [ph.ps(f"ps_o{i}", [P, B, D]) for i in range(2)]

        gate = ph.sem("gate")
        bd_in = ph.sem("bd_in")
        fetched = ph.steps("fetched")
        up = ph.steps("up", 2)
        gelu = ph.steps("gelu", FT)
        hiddens = ph.steps("hiddens", FT)
        down = ph.steps("down", ahead=RING)
        kept = ph.steps("kept", B)
        block = ph.block()

        @block.sync
        def _(sp):
            def load(t, p):
                sp.wait_ge(down.sem, down.before(t))
                hold(sp, gate)
                load_soft_expert(sp, t, p, buffers, weights, landed)
            for i in range(2):
                sp.dma_start(bd_sb[i * SPE:(i + 1) * SPE, :, :],
                             bd.rearrange("(j i) d -> i j d", i=2)[i:i + 1].to_broadcast([SPE, JT, D])).then_inc(bd_in, 16)
            staged(sp, SE - RING, load, first=RING, unroll=RING)

        @block.gpsimd
        def _(pool):
            fetched.prime(pool)

            def fetch(t, p):
                pool.wait_ge(hiddens.sem, hiddens.before(t))
                hold(pool, gate)
                pool.tensor_copy(cols[:, p, :, :], bias_cols[:, :, bass.ds(t, 1), :].rearrange("q i a f -> q i (a f)")).then_inc(fetched.sem, 1)
            staged(pool, SE, fetch)

        @block.tensor
        def _(pe):
            for s in (up, down):
                s.prime(pe)

            def gate_up(t, p):
                pe.wait_ge(landed.sems[p], landed.at(t, p))
                pe.wait_ge(hiddens.sem, hiddens.before(t))
                for ps, w in ((ps_g, wg_sb), (ps_u, wu_sb)):
                    for f in range(FT):
                        for k in range(KD):
                            mm = pe.matmul(ps[p % 2][:, f, :], w[:, p, k, f * P:(f + 1) * P],
                                           slots[:, k, bass.ds(t, 1), :, :].rearrange("q a b s -> q (a b s)"),
                                           start=(k == 0), stop=(k == KD - 1))
                    mm.then_inc(up.sem, 1)

            def go_down(t, p):
                q = p % 2
                pe.wait_ge(hiddens.sem, hiddens.at(t))
                pe.wait_ge(kept.sem, kept.before(t))
                for b in range(B):
                    for f in range(FT):
                        mm = pe.matmul(ps_o[q][q * SPE:(q + 1) * SPE, b, :], hidden[:, q, f, b * SPE:(b + 1) * SPE],
                                       wd_sb[:, p, f, :], start=(f == 0), stop=(f == FT - 1))
                mm.then_inc(down.sem, 1)
            staged(pe, SE, gate_up, go_down, unroll=RING)

        @block.scalar
        def _(act):
            gelu.prime(act)

            def activate(t, p):
                act.wait_ge(fetched.sem, fetched.at(t))
                act.wait_ge(hiddens.sem, hiddens.before(t))
                for f in range(FT):
                    if f == 0:
                        act.wait_ge(up.sem, up.at(t, 1))
                    nc.scalar.activation(gated[:, p, f, :], ps_g[p][:, f, :], ACT.Gelu, bias=cols[:, p, 0, f:f + 1]).then_inc(gelu.sem, 1)
            staged(act, SE, activate)

        @block.vector
        def _(v):
            for s in (hiddens, kept):
                s.prime(v)
            v.wait_ge(bd_in, 32)

            def multiply(t, p):
                v.wait_ge(down.sem, down.before(t, 2))
                v.wait_ge(up.sem, up.at(t))
                hold(v, gate)
                for f in range(FT):
                    v.wait_ge(gelu.sem, gelu.at(t, f + 1))
                    v.scalar_tensor_tensor(hidden[:, p, f, :], ps_u[p][:, f, :], cols[:, p, 1, f:f + 1], gated[:, p, f, :],
                                           ALU.add, ALU.mult).then_inc(hiddens.sem, 1)

            def keep(t, p):
                own = slice(p * SPE, (p + 1) * SPE)
                v.wait_ge(down.sem, down.at(t))
                for b in range(B):
                    hold(v, gate)
                    tile = bass.ds((t - p) * (D // 2), D)
                    v.tensor_tensor(slots_out[own, b].rearrange("q j d -> q (j d)")[:, tile], ps_o[p][own, b, :],
                                    bd_sb[own].rearrange("q j d -> q (j d)")[:, tile], ALU.add).then_inc(kept.sem, 1)
            staged(v, SE, multiply, keep)


def phase_soft_combine(nc, sems, x_sb, xf_t, se_t, slots_out, token_neg_max, token_inv_sum, out, ident):
    N = NT // GT
    with Phase(nc, "scomb", sems) as ph:
        wide = ph.sb("wide", [P, 2, GT, P])
        row = ph.sb("row", [P, 2, GP])
        inv = ph.sb("inv", [P, 2, GT])
        shifted = ph.sb("shifted", [P, 2, GP])
        probs = ph.sb("probs", [P, 2, JT, GP])
        res = ph.sb("res", [P, 2, GT, D])
        ps_r = ph.ps("ps_r", [P, GP])
        ps_l = [ph.ps(f"ps_l{i}", [P, GP]) for i in range(2)]
        ps_o = [ph.ps(f"ps_o{i}", [P, GP]) for i in range(2)]

        gate = ph.sem("gate")
        widened = ph.steps("widened")
        spread = ph.steps("spread")
        row_kept = ph.steps("row_kept")
        inv_kept = ph.steps("inv_kept")
        logits = ph.steps("logits", JT)
        shifts = ph.steps("shifts", JT)
        exps = ph.steps("exps", JT)
        mixed = ph.steps("mixed", GT)
        summed = ph.steps("summed", GT)
        stored = ph.transfers("stored")
        block = ph.block()

        def idle(t, p, b):
            pass

        def per_sequence(eng, *stages):
            for b in range(B):
                staged(eng, N // B, *[lambda t, p, s=s: s(t, p, b) for s in stages], first=b * (N // B))

        @block.sync
        def _(sp):
            stored.prime(sp)

            def store(t, p):
                sp.wait_ge(summed.sem, summed.at(t))
                hold(sp, gate)
                sp.dma_start(out[bass.ds(t * GP, GP), :].rearrange("(n q) c -> q n c", q=P), res[:, p, :, :]).then_inc(stored.sems[p], 32)
            staged(sp, N, store)
            for t in (N - 2, N - 1):
                sp.wait_ge(stored.sems[t % 2], stored.at(t, t % 2))

        @block.gpsimd
        def _(pool):
            widened.prime(pool)

            def widen(t, p):
                pool.wait_ge(spread.sem, spread.before(t))
                hold(pool, gate)
                pool.tensor_copy(wide[:, p, :, :], token_neg_max[:, bass.ds(t * GT, GT)].unsqueeze(2).to_broadcast([P, GT, P])).then_inc(widened.sem, 1)
            staged(pool, N, widen)

        @block.tensor
        def _(pe):
            for s in (spread, logits, mixed):
                s.prime(pe)

            def turn(t, p, b):
                pe.wait_ge(widened.sem, widened.at(t))
                pe.wait_ge(row_kept.sem, row_kept.before(t, 1))
                for i in range(GT):
                    mm = spread_column(pe, ps_r[:, i * P:(i + 1) * P], wide[:, p, i, :], ident)
                mm.then_inc(spread.sem, 1)

            def multiply(t, p, b):
                for j in range(JT):
                    pe.wait_ge(shifts.sem, shifts.at(t, j - 1))
                    for k in range(KD):
                        mm = pe.matmul(ps_l[j % 2][:, :], se_t[:, k, j * P:(j + 1) * P], xf_t[:, k, bass.ds(t * GP, GP)],
                                       start=(k == 0), stop=(k == KD - 1))
                    mm.then_inc(logits.sem, 1)

            def mix(t, p, b):
                pe.wait_ge(exps.sem, exps.at(t))
                for i in range(GT):
                    pe.wait_ge(summed.sem, summed.at(t, i - 1))
                    for j in range(JT):
                        mm = pe.matmul(ps_o[i % 2][:, 0:D], probs[:, p, j, i * P:(i + 1) * P], slots_out[:, b, j, :],
                                       start=(j == 0), stop=(j == JT - 1))
                    mm.then_inc(mixed.sem, 1)
            per_sequence(pe, turn, multiply, mix)

        @block.scalar
        def _(act):
            for s in (row_kept, inv_kept, exps):
                s.prime(act)

            def keep(t, p, b):
                act.wait_ge(spread.sem, spread.at(t))
                act.wait_ge(shifts.sem, shifts.before(t))
                nc.scalar.copy(row[:, p, :], ps_r[:, :]).then_inc(row_kept.sem, 1)

            def exponent(t, p, b):
                act.wait_ge(summed.sem, summed.before(t))
                hold(act, gate)
                nc.scalar.copy(inv[:, p, :], token_inv_sum[:, bass.ds(t * GT, GT)]).then_inc(inv_kept.sem, 1)
                act.wait_ge(mixed.sem, mixed.before(t))
                for j in range(JT):
                    act.wait_ge(shifts.sem, shifts.at(t, j + 1))
                    nc.scalar.activation(probs[:, p, j, :], shifted[:, j % 2, :], ACT.Exp).then_inc(exps.sem, 1)
            per_sequence(act, keep, exponent)

        @block.vector
        def _(v):
            for s in (shifts, summed):
                s.prime(v)

            def shift(t, p, b):
                v.wait_ge(row_kept.sem, row_kept.at(t))
                for j in range(JT):
                    v.wait_ge(logits.sem, logits.at(t, j + 1))
                    v.wait_ge(exps.sem, exps.at(t, j - 1))
                    v.tensor_tensor(shifted[:, j % 2, :], ps_l[j % 2][:, :], row[:, p, :], ALU.add).then_inc(shifts.sem, 1)

            def finish(t, p, b):
                v.wait_ge(stored.sems[p], stored.before(t, p))
                v.wait_ge(inv_kept.sem, inv_kept.at(t))
                for i in range(GT):
                    v.wait_ge(mixed.sem, mixed.at(t, i + 1))
                    hold(v, gate)
                    v.scalar_tensor_tensor(res[:, p, i, :], ps_o[i % 2][:, 0:D], inv[:, p, i:i + 1],
                                           flat(x_sb[:, bass.ds(t * GT + i, 1), :]), ALU.mult, ALU.add).then_inc(summed.sem, 1)
            per_sequence(v, shift, finish)


def two_layers(nc, t, out):
    scratch = {}
    for name, shape in (("slots_x", [G * (SLOTS + P), D]), ("slots_y", [G * (SLOTS + P), D]), ("proj", [T, PW]),
                        ("rec1", [NBK, B, H, REC1]), ("rec2", [NBK, VQ, B, H, REC2]), ("delta_out", [T, D])):
        scratch[name] = nc.dram_tensor(name, shape, F32, kind="Internal").ap()
    slots_x, slots_y, proj, rec1, rec2, delta_out = scratch.values()
    x = t["L0_attn_x"].rearrange("b s d -> (b s) d")
    soft = {name[7:]: ap for name, ap in t.items() if name.startswith("L1_ffn_")}

    def attn1(*names):
        return [t["L1_attn_" + n] for n in names]

    with ExitStack() as sems, ExitStack() as whole:
        def held(ctx, name, shape, dt=F32):
            return ctx.enter_context(nc.sbuf_tensor(name, shape, dt))

        set_up, zeroed = [sems.enter_context(nc.semaphore(n)) for n in ("set_up", "zeroed")]
        w_landed = [sems.enter_context(nc.semaphore(f"w_landed{g}")) for g in range(G)]
        ident = held(whole, "ident", [P, P])
        ident_bf = held(whole, "ident_bf", [P, P], BF16)
        layer = sems.enter_context(Semaphores(nc, sems))
        with Phase(nc, "id", layer) as ph:
            identity(nc, ph, ident)
        z_sb = held(whole, "z_sb", [P, NT, D])
        with ExitStack() as ctx:
            qk_sb = held(ctx, "qk_sb", [P, NT, 2 * D])
            v_sb = held(ctx, "v_sb", [P, NT, D])
            zeros = held(ctx, "zeros", [P, 2 * D])
            phase_qkv(nc, layer, x, t["L0_attn_qkv_w"], t["L0_attn_qkv_b"], t["rope"], qk_sb, v_sb, ident)
            with nc.Block() as block:
                @block.vector
                def _(v):
                    v.tensor_copy(ident_bf[:, :], ident[:, :]).then_inc(set_up, 1)
                    v.memset(zeros[:, :], 0.0).then_inc(set_up, 1)
                    v.wait_ge(set_up, 2)

                @block.sync
                def _(sp):
                    sp.wait_ge(set_up, 2)
                    zero_slots(nc, sp, zeros, slots_x, slots_y, zeroed)
            phase_attention(nc, layer, qk_sb, v_sb, z_sb, ident, ident_bf)
            with nc.Block() as block:
                @block.sync
                def _(sp):
                    sp.wait_ge(zeroed, 16 * ZEROINGS)
        x_sb = held(whole, "x_sb", [P, NT, D])
        weight = held(whole, "weight", [P, NT, G, TOPK])
        pos = held(whole, "pos", [P, NT, G, TOPK], U32)
        tile_expert = held(whole, "tile_expert", [1, G, SLOT_TILES + 1], U32)

        with ExitStack() as ctx:
            w_gu = held(ctx, "w_gu", [P, KD, E, 2, HID])
            experts = [[t[f"L0_ffn_{n}{g}"] for n in ("wg", "wu", "wd")] for g in range(G)]
            with nc.Block() as block:
                @block.sync
                def _(sp):
                    load_gate_up(sp, w_gu, *experts[0][:2], w_landed[0])
            with ExitStack() as routed:
                lg_sb = held(routed, "lg_sb", [P, NT, GE])
                top_val = held(routed, "top_val", [P, NT, G, TOPK])
                top_idx = held(routed, "top_idx", [P, NT, G, TOPK])
                phase_route(nc, layer, x, z_sb, t["L0_attn_out_w"], t["L0_attn_out_b"],
                            [t[f"L0_ffn_router_w{g}"] for g in range(G)], x_sb, z_sb, lg_sb, top_val, top_idx, ident)
                phase_slots(nc, layer, z_sb, lg_sb, top_val, top_idx, weight, pos, tile_expert, slots_x)
            w_d = held(ctx, "w_d", [P, E, D])
            for g in range(G):
                phase_experts(nc, layer, g, w_gu, w_d, experts[g], w_landed[g],
                              slots_x, slots_y, tile_expert, ident)
        phase_combine(nc, layer, x_sb, z_sb, weight, pos, slots_y, attn1("Wq", "Wk", "Wv"), attn1("Wb", "Wg"),
                      *attn1("ln1_g", "ln1_b"), proj, ident)

        layer.clear()
        phase_blocks(nc, layer, proj, rec1, rec2)
        phase_chain(nc, layer, rec1, rec2, delta_out, ident)
        phase_mlp(nc, layer, delta_out, x_sb, z_sb, *attn1("Wo", "bo", "ln2_g", "ln2_b", "w1", "b1", "w2", "b2"),
                  soft["norm_g"], soft["norm_b"], ident)

        xf_t = held(whole, "xf_t", [P, KD, T])
        se_t = held(whole, "se_t", [P, KD, NS])
        bias_cols = held(whole, "bias_cols", [P, 2, SE, FT])
        token_neg_max = held(whole, "token_neg_max", [P, NT])
        token_inv_sum = held(whole, "token_inv_sum", [P, NT])
        slots = held(whole, "slots", [P, KD, SE, B, SPE])
        phase_soft_turn(nc, layer, z_sb, xf_t, soft["slot_embeds"], soft["slot_g"], soft["slot_b"], soft["scale"],
                        soft["bg"], soft["bu"], se_t, bias_cols[:, :, :, :], ident)
        with ExitStack() as ctx:
            buffers = [held(ctx, "soft_wg", [P, RING, KD, F]), held(ctx, "soft_wu", [P, RING, KD, F]),
                       held(ctx, "soft_wd", [P, RING, FT, D])]
            weights = [soft["Wg"], soft["Wu"], soft["Wd"]]
            landed = Transfers([layer.take(f"soft_landed{p}") for p in range(RING)], 3, soft=True)
            with nc.Block() as block:
                @block.sync
                def _(sp):
                    for e in range(RING):
                        load_soft_expert(sp, e, e, buffers, weights, landed)
            with ExitStack() as dispatching:
                neg_max = held(dispatching, "neg_max", [P, B * NS])
                inv_sum = held(dispatching, "inv_sum", [P, B * NS])
                phase_slot_stats(nc, layer, xf_t, se_t, neg_max, inv_sum, ident)
                phase_dispatch(nc, layer, z_sb, xf_t, se_t, neg_max, inv_sum, slots, token_neg_max, token_inv_sum)
            slots_out = z_sb[:, 0:B * JT, :].rearrange("q (b j) d -> q b j d", b=B)
            phase_soft_experts(nc, layer, slots, bias_cols, buffers, weights, landed, soft["bd"], slots_out)
        phase_soft_combine(nc, layer, x_sb, xf_t, se_t, slots_out, token_neg_max, token_inv_sum, out, ident)


def kernel(**inputs):
    import concourse.bacc as _bacc
    from concourse.bass_utils import run_bass_kernel_spmd as _run

    nc = _bacc.Bacc("TRN2", target_bir_lowering=False, num_devices=1)
    inputs["rope"] = rope_tables()
    arrays, tensors = {}, {}
    for name, a in inputs.items():
        arrays[f"in_{name}"] = np.ascontiguousarray(a)
        tensors[name] = nc.dram_tensor(f"in_{name}", arrays[f"in_{name}"].shape,
                                       mybir.dt.from_np(arrays[f"in_{name}"].dtype), kind="ExternalInput").ap()
    out = nc.dram_tensor("out", [T, D], F32, kind="ExternalOutput").ap()
    two_layers(nc, tensors, out)
    r = _run(nc, [arrays], core_ids=[0])
    return r.results[0]["out"].reshape(B, S, D)
```
